# Optimizing a Trainium2 kernel written in Bass

```python
import numpy as np
import jax
import jax.numpy as jnp

def _softmax(x, axis=-1):
    return jax.nn.softmax(x, axis=axis)

def _gelu(x):
    return jax.nn.gelu(x, approximate=True)

def _silu(x):
    return jax.nn.silu(x)

def _sigmoid(x):
    return jax.nn.sigmoid(x)

def _layernorm(x, axis=-1, eps=1e-05):
    m = jnp.mean(x, axis=axis, keepdims=True)
    v = jnp.var(x, axis=axis, keepdims=True)
    return (x - m) / jnp.sqrt(v + eps)

def _scatter_add(tgt, idx, src, axis=0):
    return tgt.at[idx].add(src)

def _segment_sum(src, seg, n):
    return jax.ops.segment_sum(src, seg, n)
kernel_name = 'mk_gnn_ffn_d2_gnn_r8_e14cd6'

def setup_inputs(seed: int=0):
    np.random.seed(seed)
    _w = jnp.asarray

    def _rec_inputs():
        import jax
        import jax.numpy as jnp
        _gk = jax.random.key(seed)
        x = 1.508e-05 + 1 * jax.random.normal(jax.random.fold_in(_gk, 1), (1250, 512), jnp.float32)
        src = jax.random.randint(jax.random.fold_in(_gk, 2), (40000,), 0, 1250, jnp.int32)
        dst = jax.random.randint(jax.random.fold_in(_gk, 3), (40000,), 0, 1250, jnp.int32)
        _o = jnp.argsort(dst, stable=True)
        src = src[_o]
        dst = dst[_o]
        edge_attr_4 = 0.00171547 + 0.999346 * jax.random.normal(jax.random.fold_in(_gk, 11), (40000, 4), jnp.float32)
        edge_attr_8 = 0.000126197 + 0.999763 * jax.random.normal(jax.random.fold_in(_gk, 12), (40000, 8), jnp.float32)
        return (x, src, dst, edge_attr_4, edge_attr_8)
    x, src, dst, edge_attr_4, edge_attr_8 = _rec_inputs()

    def _L0_gnn_setup():
        import jax, jax.numpy as jnp
        import numpy as np
        N_FRAMES = 16384
        D_FEAT = 512
        N_SHOTS = 256
        SHOT_LEN = N_FRAMES // N_SHOTS
        key = jax.random.key(seed)
        x = jax.random.normal(key, (N_FRAMES, D_FEAT), dtype=jnp.float32)
        starts = jnp.arange(N_SHOTS, dtype=jnp.int64) * SHOT_LEN
        ends = starts + (SHOT_LEN - 1)
        graph = jnp.stack([starts, ends], axis=1)
        return {'input': x, 'graph': graph}
    _L0_gnn_all = _L0_gnn_setup()
    _L0_gnn_in = {k: v for k, v in _L0_gnn_all.items() if k in ()}
    del _L0_gnn_all

    def _L0_ffn_setup():
        import jax, jax.numpy as jnp
        import numpy as np
        NUM_EXPERTS = 8
        TOP_K = 2
        key = jax.random.key(seed)
        ks = jax.random.split(key, 5)
        B, T, D, H, E = (8, 512, 512, 1536, NUM_EXPERTS)
        scale = 0.02
        x = jax.random.normal(ks[0], (B, T, D), dtype=jnp.float32)
        gate_w = jax.random.normal(ks[1], (E, D), dtype=jnp.float32) * scale
        w1 = jax.random.normal(ks[2], (E, H, D), dtype=jnp.float32) * scale
        w3 = jax.random.normal(ks[3], (E, H, D), dtype=jnp.float32) * scale
        w2 = jax.random.normal(ks[4], (E, D, H), dtype=jnp.float32) * scale
        return {'x': x, 'gate_w': gate_w, 'w1': w1, 'w3': w3, 'w2': w2}
    _L0_ffn_all = _L0_ffn_setup()
    _L0_ffn_in = {k: v for k, v in _L0_ffn_all.items() if k in ('gate_w', 'w1', 'w3', 'w2')}
    del _L0_ffn_all

    def _L1_gnn_setup():
        import jax, jax.numpy as jnp
        import numpy as np
        MUL = 128
        N_NODES = 1250
        N_EDGES = 20000
        R_BASIS = 8
        HIDDEN = 64
        W_NUMEL = 4 * MUL
        SQRT3 = 3.0 ** 0.5
        SILU_2MOM = 1.679177
        AVG_NUM_NEIGHBORS = 10.0

        def _lin_irreps(x0, x1, W0, W1):
            y0 = x0 @ W0 / jnp.sqrt(jnp.float32(W0.shape[0]))
            y1 = jnp.einsum('num,uv->nvm', x1, W1) / jnp.sqrt(jnp.float32(W1.shape[0]))
            return (y0, y1)

        def _forward(node_feats, edge_attrs, edge_feats, edge_index, W_up0, W_up1, W_mlp1, W_mlp2, W_mlp3, W_mlp4, W_out0, W_out1):
            num_nodes = node_feats.shape[0]
            sender, receiver = (edge_index[0], edge_index[1])
            x0 = node_feats[:, :MUL]
            x1 = node_feats[:, MUL:].reshape(num_nodes, MUL, 3)
            x0, x1 = _lin_irreps(x0, x1, W_up0, W_up1)
            h = edge_feats
            for W in (W_mlp1, W_mlp2, W_mlp3):
                h = SILU_2MOM * jax.nn.silu(h @ W / jnp.sqrt(jnp.float32(W.shape[0])))
            tpw = h @ W_mlp4 / jnp.sqrt(jnp.float32(W_mlp4.shape[0]))
            w1, w2, w3, w4 = jnp.split(tpw, 4, axis=-1)
            s0 = x0[sender]
            s1 = x1[sender]
            y0 = edge_attrs[:, 0:1]
            y1 = edge_attrs[:, 1:4]
            p1 = w1 * s0 * y0
            p2 = (w2 * s0)[:, :, None] * y1[:, None, :]
            p3 = w3[:, :, None] * s1 * y0[:, None, :]
            p4 = w4 * jnp.einsum('eum,em->eu', s1, y1) / SQRT3
            m0 = jnp.concatenate([p1, p4], axis=-1)
            m1 = jnp.concatenate([p2, p3], axis=1)
            msg0 = jax.ops.segment_sum(m0, receiver, num_segments=num_nodes)
            msg1 = jax.ops.segment_sum(m1, receiver, num_segments=num_nodes)
            o0, o1 = _lin_irreps(msg0, msg1, W_out0, W_out1)
            out = jnp.concatenate([o0, o1.reshape(num_nodes, 3 * MUL)], axis=-1)
            return out / AVG_NUM_NEIGHBORS
        key = jax.random.key(seed)
        ks = jax.random.split(key, 12)
        rn = lambda k, s: jax.random.normal(k, s, dtype=jnp.float32)
        return {'node_feats': rn(ks[0], (N_NODES, 4 * MUL)), 'edge_attrs': rn(ks[1], (N_EDGES, 4)), 'edge_feats': rn(ks[2], (N_EDGES, R_BASIS)), 'edge_index': jax.random.randint(ks[3], (2, N_EDGES), 0, N_NODES), 'W_up0': rn(ks[4], (MUL, MUL)), 'W_up1': rn(ks[5], (MUL, MUL)), 'W_mlp1': rn(ks[6], (R_BASIS, HIDDEN)), 'W_mlp2': rn(ks[7], (HIDDEN, HIDDEN)), 'W_mlp3': rn(ks[8], (HIDDEN, HIDDEN)), 'W_mlp4': rn(ks[9], (HIDDEN, W_NUMEL)), 'W_out0': rn(ks[10], (2 * MUL, MUL)), 'W_out1': rn(ks[11], (2 * MUL, MUL))}
    _L1_gnn_all = _L1_gnn_setup()
    _L1_gnn_in = {k: v for k, v in _L1_gnn_all.items() if k in ('W_up0', 'W_up1', 'W_mlp1', 'W_mlp2', 'W_mlp3', 'W_mlp4', 'W_out0', 'W_out1')}
    del _L1_gnn_all

    def _L1_ffn_setup():
        import jax, jax.numpy as jnp
        import numpy as np
        NUM_EXPERTS = 8
        TOP_K = 2
        key = jax.random.key(seed)
        k0, k1, k2, k3, k4 = jax.random.split(key, 5)
        sl, bs, hs, ffn = (256, 2, 512, 256)
        T = sl * bs
        x = jax.random.normal(k0, (sl, bs, hs), jnp.float32)
        expert_weights = jax.random.uniform(k1, (T, TOP_K), jnp.float32)
        expert_indices = jax.random.randint(k2, (T, TOP_K), 0, NUM_EXPERTS)
        w1 = jax.random.normal(k3, (NUM_EXPERTS, hs, ffn), jnp.float32) * hs ** (-0.5)
        w2 = jax.random.normal(k4, (NUM_EXPERTS, ffn, hs), jnp.float32) * ffn ** (-0.5)
        return dict(x=x, expert_weights=expert_weights, expert_indices=expert_indices, w1=w1, w2=w2)
    _L1_ffn_all = _L1_ffn_setup()
    _L1_ffn_in = {k: v for k, v in _L1_ffn_all.items() if k in ('expert_weights', 'expert_indices', 'w1', 'w2')}
    del _L1_ffn_all
    return {'x': x, 'src': src, 'dst': dst, 'edge_attr_4': edge_attr_4, 'edge_attr_8': edge_attr_8, 'L0_ffn_gate_w': _L0_ffn_in['gate_w'], 'L0_ffn_w1': _L0_ffn_in['w1'], 'L0_ffn_w3': _L0_ffn_in['w3'], 'L0_ffn_w2': _L0_ffn_in['w2'], 'L1_gnn_W_up0': _L1_gnn_in['W_up0'], 'L1_gnn_W_up1': _L1_gnn_in['W_up1'], 'L1_gnn_W_mlp1': _L1_gnn_in['W_mlp1'], 'L1_gnn_W_mlp2': _L1_gnn_in['W_mlp2'], 'L1_gnn_W_mlp3': _L1_gnn_in['W_mlp3'], 'L1_gnn_W_mlp4': _L1_gnn_in['W_mlp4'], 'L1_gnn_W_out0': _L1_gnn_in['W_out0'], 'L1_gnn_W_out1': _L1_gnn_in['W_out1'], 'L1_ffn_expert_weights': _L1_ffn_in['expert_weights'], 'L1_ffn_expert_indices': _L1_ffn_in['expert_indices'], 'L1_ffn_w1': _L1_ffn_in['w1'], 'L1_ffn_w2': _L1_ffn_in['w2']}

def reference(x, src, dst, edge_attr_4, edge_attr_8, L0_ffn_gate_w, L0_ffn_w1, L0_ffn_w3, L0_ffn_w2, L1_gnn_W_up0, L1_gnn_W_up1, L1_gnn_W_mlp1, L1_gnn_W_mlp2, L1_gnn_W_mlp3, L1_gnn_W_mlp4, L1_gnn_W_out0, L1_gnn_W_out1, L1_ffn_expert_weights, L1_ffn_expert_indices, L1_ffn_w1, L1_ffn_w2):
    import jax
    import jax.numpy as jnp

    def _L0_gnn_ref(input, graph):
        import jax, jax.numpy as jnp
        import numpy as np
        N_FRAMES = 16384
        D_FEAT = 512
        N_SHOTS = 256
        SHOT_LEN = N_FRAMES // N_SHOTS
        n = input.shape[0]
        s = graph.shape[0]
        starts = graph[:, 0]
        counts = (graph[:, 1] - graph[:, 0] + 1).astype(input.dtype)
        seg_ids = jnp.searchsorted(starts, jnp.arange(n), side='right') - 1
        sums = jax.ops.segment_sum(input, seg_ids, num_segments=s)
        means = sums / counts[:, None]
        return means[seg_ids]

    def _L0_ffn_ref(x, gate_w, w1, w3, w2):
        import jax, jax.numpy as jnp
        import numpy as np
        NUM_EXPERTS = 8
        TOP_K = 2
        B, T, D = x.shape
        E = gate_w.shape[0]
        xf = x.reshape(-1, D)
        N = xf.shape[0]
        gate_logits = xf @ gate_w.T
        weights, indices = jax.lax.top_k(gate_logits, TOP_K)
        weights = jax.nn.softmax(weights, axis=-1)
        combine = jnp.zeros((N, E), dtype=xf.dtype).at[jnp.arange(N)[:, None], indices].add(weights)
        out = jnp.zeros_like(xf)
        for e in range(E):
            h = jax.nn.silu(xf @ w1[e].T) * (xf @ w3[e].T)
            y = h @ w2[e].T
            out = out + combine[:, e:e + 1] * y
        return out.reshape(B, T, D)

    def _L1_gnn_ref(node_feats, edge_attrs, edge_feats, edge_index, W_up0, W_up1, W_mlp1, W_mlp2, W_mlp3, W_mlp4, W_out0, W_out1):
        import jax, jax.numpy as jnp
        import numpy as np
        MUL = 128
        N_NODES = 1250
        N_EDGES = 20000
        R_BASIS = 8
        HIDDEN = 64
        W_NUMEL = 4 * MUL
        SQRT3 = 3.0 ** 0.5
        SILU_2MOM = 1.679177
        AVG_NUM_NEIGHBORS = 10.0

        def _lin_irreps(x0, x1, W0, W1):
            y0 = x0 @ W0 / jnp.sqrt(jnp.float32(W0.shape[0]))
            y1 = jnp.einsum('num,uv->nvm', x1, W1) / jnp.sqrt(jnp.float32(W1.shape[0]))
            return (y0, y1)

        def _forward(node_feats, edge_attrs, edge_feats, edge_index, W_up0, W_up1, W_mlp1, W_mlp2, W_mlp3, W_mlp4, W_out0, W_out1):
            num_nodes = node_feats.shape[0]
            sender, receiver = (edge_index[0], edge_index[1])
            x0 = node_feats[:, :MUL]
            x1 = node_feats[:, MUL:].reshape(num_nodes, MUL, 3)
            x0, x1 = _lin_irreps(x0, x1, W_up0, W_up1)
            h = edge_feats
            for W in (W_mlp1, W_mlp2, W_mlp3):
                h = SILU_2MOM * jax.nn.silu(h @ W / jnp.sqrt(jnp.float32(W.shape[0])))
            tpw = h @ W_mlp4 / jnp.sqrt(jnp.float32(W_mlp4.shape[0]))
            w1, w2, w3, w4 = jnp.split(tpw, 4, axis=-1)
            s0 = x0[sender]
            s1 = x1[sender]
            y0 = edge_attrs[:, 0:1]
            y1 = edge_attrs[:, 1:4]
            p1 = w1 * s0 * y0
            p2 = (w2 * s0)[:, :, None] * y1[:, None, :]
            p3 = w3[:, :, None] * s1 * y0[:, None, :]
            p4 = w4 * jnp.einsum('eum,em->eu', s1, y1) / SQRT3
            m0 = jnp.concatenate([p1, p4], axis=-1)
            m1 = jnp.concatenate([p2, p3], axis=1)
            msg0 = jax.ops.segment_sum(m0, receiver, num_segments=num_nodes)
            msg1 = jax.ops.segment_sum(m1, receiver, num_segments=num_nodes)
            o0, o1 = _lin_irreps(msg0, msg1, W_out0, W_out1)
            out = jnp.concatenate([o0, o1.reshape(num_nodes, 3 * MUL)], axis=-1)
            return out / AVG_NUM_NEIGHBORS
        return _forward(node_feats, edge_attrs, edge_feats, edge_index, W_up0, W_up1, W_mlp1, W_mlp2, W_mlp3, W_mlp4, W_out0, W_out1)

    def _L1_ffn_ref(x, expert_weights, expert_indices, w1, w2):
        import jax, jax.numpy as jnp
        import numpy as np
        NUM_EXPERTS = 8
        TOP_K = 2
        'Dropless MoE: sort assignments by expert, gather tokens, grouped MLP,\n            scatter-combine with top-k router weights (megablocks gather/scatter semantics).'
        in_shape = x.shape
        hs = in_shape[-1]
        x_flat = x.reshape(-1, hs)
        T = x_flat.shape[0]
        flat_ids = expert_indices.reshape(-1)
        order = jnp.argsort(flat_ids)
        bin_ids = flat_ids[order]
        token_ids = order // TOP_K
        xg = x_flat[token_ids]
        y = jnp.zeros_like(xg)
        for e in range(NUM_EXPERTS):
            h = jax.nn.gelu(xg @ w1[e], approximate=False)
            y = jnp.where((bin_ids == e)[:, None], h @ w2[e], y)
        w = expert_weights.reshape(-1)[order][:, None]
        out = jnp.zeros((T, hs), x.dtype).at[token_ids].add(w * y)
        return out.reshape(in_shape)
    edge_index = jnp.stack([src, dst])
    edge_index_t = jnp.stack([src, dst], axis=1)
    x = x + _L0_gnn_ref(_layernorm(x, axis=-1), edge_index_t)
    x = x + _L0_ffn_ref(_layernorm(x, axis=-1)[None], L0_ffn_gate_w, L0_ffn_w1, L0_ffn_w3, L0_ffn_w2)[0]
    x = x + _L1_gnn_ref(_layernorm(x, axis=-1), edge_attr_4, edge_attr_8, edge_index, L1_gnn_W_up0, L1_gnn_W_up1, L1_gnn_W_mlp1, L1_gnn_W_mlp2, L1_gnn_W_mlp3, L1_gnn_W_mlp4, L1_gnn_W_out0, L1_gnn_W_out1)
    x = x + _L1_ffn_ref(_layernorm(x, axis=-1)[None], L1_ffn_expert_weights, L1_ffn_expert_indices, L1_ffn_w1, L1_ffn_w2)[0]
    return x

_drawn_inputs = setup_inputs


def setup_inputs(seed=0):
    import zlib

    import numpy as np

    out = dict(_drawn_inputs(seed))
    spreads = {}
    factors = {}
    for name, (base, spread) in spreads.items():
        noise = np.random.default_rng([zlib.crc32(name.encode()), seed]).standard_normal(out[name].shape)
        drawn = base * np.exp(spread * noise) if base else spread * noise
        out[name] = jnp.asarray(drawn.astype(out[name].dtype))
    for name, factor in factors.items():
        out[name] = (out[name] * factor).astype(out[name].dtype)
    return out
```

```python
from contextlib import ExitStack

import numpy as np

import concourse.bass as bass
from concourse import mybir

F32 = mybir.dt.float32
I32 = mybir.dt.int32
ALU = mybir.AluOpType
ACT = mybir.ActivationFunctionType
AX = mybir.AxisListType

N, D = 1250, 512
NP, NT = 125, 10
NE, EP, EJ = 40000, 125, 320
SEARCH_LEVELS = 16
TOP = 7
LEAVES = 2 ** (SEARCH_LEVELS - TOP)
E0, H0 = 8, 1536
TILE = 128
FT = (2 * N - E0) // TILE + E0
HB = H0 // 512
GROUP = 4 * TILE
NG = NE // GROUP + NT
NG += NG % 2
NPAIR = NG // 2
SLOTS = NG * GROUP
REC = 16
MUL, HID = 128, 64
SILU_2MOM = 1.679177
T1, E1, H1 = 512, 8, 256
BIG = float(2 ** 20)
SKIP = 2 ** 20


def search_tree():
    lo, hi, levels = np.array([0]), np.array([NE]), []
    for _ in range(SEARCH_LEVELS):
        mid = (lo + hi) // 2
        levels.append(mid)
        lo, hi = np.stack([lo, mid], 1).ravel(), np.stack([mid, hi], 1).ravel()
    sub = np.arange(128)
    above = np.stack([levels[l][sub >> (TOP - l)] for l in range(TOP)], 1)
    below = np.concatenate([levels[l].reshape(128, -1) for l in range(TOP, SEARCH_LEVELS)], 1)
    return above, below, hi - 1


CONSTS = dict(ident=128, ones=128, before=128, node=N, node_col=NT, leaf1=LEAVES, right=TOP, left=TOP,
              part=1, sub512=1)


def constants():
    p = np.arange(128)[:, None]
    sub = (p >> (TOP - 1 - np.arange(TOP)[None])) & 1
    c = dict(ident=np.eye(128), ones=np.ones((128, 128)), before=p < p.T,
             node=np.broadcast_to(np.arange(N), (128, N)), node_col=p + NP * np.arange(NT)[None],
             leaf1=np.broadcast_to(np.arange(LEAVES) + 1, (128, LEAVES)), right=sub, left=1 - sub,
             part=p, sub512=p * LEAVES)
    return np.concatenate([np.asarray(c[k], np.float32) for k in CONSTS], 1)


class Lane:

    def __init__(self, sem):
        self.new_sem, self.steps, self.seen = sem, [], {}
        self.chained, self.last = False, None

    def stage(self, name, chained):
        self.sem, self.count, self.chained = self.new_sem(name), 0, chained

    def wait(self, after):
        need = {}
        for s, v in after:
            if v > self.seen.get(id(s), 0):
                need[id(s)] = (s, max(v, need.get(id(s), (s, 0))[1]))
        for k, (s, v) in need.items():
            self.seen[k] = v
            self.steps.append(lambda e, s=s, v=v: e.wait_ge(s, v))

    def __call__(self, op, /, *after, **kw):
        self.wait([*after, self.last] if self.chained and self.last else after)
        self.count += 1
        self.steps.append(lambda e, s=self.sem: method(e, op)(**kw).then_inc(s, 1))
        self.last = (self.sem, self.count)
        return self.last

    def quiet(self, op, /, *after, **kw):
        self.wait(after)
        self.steps.append(lambda e: method(e, op)(**kw))

    def dma(self, done, /, *after, **kw):
        self.wait(after)
        done.count += 16
        op = "indirect_dma_start" if "out_offset" in kw else "dma_start"
        self.steps.append(lambda e: method(e, op)(**kw).then_inc(done.sem, 16))
        return (done.sem, done.count)

    def run(self, e):
        for s in self.steps:
            s(e)


def method(e, op):
    return {
        "matmul": lambda: e.matmul, "transpose": lambda: e.transpose, "activation": lambda: e.activation,
        "tensor_scalar": lambda: e.tensor_scalar, "tensor_tensor": lambda: e.tensor_tensor,
        "scalar_tensor_tensor": lambda: e.scalar_tensor_tensor, "tensor_copy": lambda: e.tensor_copy,
        "tensor_reduce": lambda: e.tensor_reduce, "tensor_tensor_scan": lambda: e.tensor_tensor_scan,
        "bn_stats": lambda: e.bn_stats, "bn_aggr": lambda: e.bn_aggr, "reciprocal": lambda: e.reciprocal,
        "memset": lambda: e.memset, "dma_start": lambda: e.dma_start,
        "indirect_dma_start": lambda: e.indirect_dma_start,
    }[op]()


class Done:

    def __init__(self, sem):
        self.sem, self.count = sem, 0


def program(nc, consts, x, anc, sub, leaf_table, src, dst, ea4, ea8, gate, w13, w2, w_up, w_mlp1, w_mlp23,
            w_mlp4, w_out, ew, ei, v1, v2, out):
    ctx = ExitStack()
    with ctx:
        n_sem = [0]

        def sem(name):
            n_sem[0] += 1
            return ctx.enter_context(nc.semaphore(f"{name}_{n_sem[0]}"))

        def done(name):
            return Done(sem(name))

        def dram(name, shape, dt=F32):
            return nc.dram_tensor(name, shape, dt, kind="Internal").ap()

        PE, V, A, G, S = (Lane(lambda s, n=n: sem(f"{n}_{s}")) for n in ("pe", "dve", "act", "pool", "sp"))

        def stage(name, chained=True):
            for lane in (PE, V, A, G):
                lane.stage(name, chained and lane in (V, A))

        arena = ctx.enter_context(nc.sbuf_tensor("arena", [128, 52600], F32))
        top = [0]

        def carve(words, at=None):
            if at is None:
                at, top[0] = top[0], top[0] + words
                assert top[0] <= 52600, top[0]
            return arena[:, at:at + words]

        banks = [ctx.enter_context(nc.psum_tensor(f"bank{i}", [128, 512], F32)) for i in range(8)]

        cst = carve(sum(CONSTS.values()))
        K, at = {}, 0
        for name, w in CONSTS.items():
            K[name] = cst[:, at:at + w]
            at += w
        ident, ones, before = K["ident"], K["ones"], K["before"]
        xs = carve(NT * D).rearrange("p (t d) -> p t d", t=NT)
        ln_at = top[0]
        ln = carve(NT * D).rearrange("p (t d) -> p t d", t=NT)
        lnT_at = top[0]
        lnT = carve(4 * N).rearrange("p (k n) -> p k n", k=4)
        recs = carve(NG * 4 * REC).rearrange("p (s c) -> p s c", c=REC)
        edge_at = top[0]
        edges = carve(EJ * REC).rearrange("p (j c) -> p j c", c=REC)
        zone = top[0]
        carve(HB * (4096 + 2048))
        small_at = top[0]
        carve(3000)
        sm = [small_at]

        def small(words):
            sm[0] += words
            assert sm[0] <= small_at + 3000
            return carve(words, sm[0] - words)

        stage("load")
        d_const, d_x, d_tree, d_edge, d_wts = done("const"), done("x"), done("tree"), done("edge"), done("wts")
        ready_const = S.dma(d_const, out=cst, in_=consts)
        anc_i, sub_i = small(TOP), carve(LEAVES - 1, zone + 13000)
        S.dma(d_tree, out=anc_i.bitcast(I32), in_=anc)
        ready_tree = S.dma(d_tree, out=sub_i.bitcast(I32), in_=sub)
        ready_x = A.dma(d_x, out=xs[:NP], in_=x.rearrange("(t p) d -> p t d", p=NP))
        src_i = carve(EJ, zone + 13600)
        dst_i = carve(EJ, zone + 13920)
        at4, at8 = carve(EJ * 4, lnT_at), carve(EJ * 8, ln_at)
        A.dma(d_edge, out=src_i[:EP].bitcast(I32), in_=src.rearrange("(p j) -> p j", p=EP))
        A.dma(d_edge, out=dst_i[:EP].bitcast(I32), in_=dst.rearrange("(p j) -> p j", p=EP))
        A.dma(d_edge, out=at4[:EP], in_=ea4.rearrange("(p j) c -> p (j c)", p=EP))
        ready_edge = A.dma(d_edge, out=at8[:EP], in_=ea8.rearrange("(p j) c -> p (j c)", p=EP))
        gate_sb = small(4 * E0).rearrange("p (k e) -> p k e", k=4)
        wup_sb, m1_sb, m23_sb, m4_sb, wo_sb = small(2 * MUL), small(128), small(256), small(512), small(512)
        S.dma(d_wts, out=gate_sb, in_=gate)
        S.dma(d_wts, out=wup_sb, in_=w_up)
        S.dma(d_wts, out=m1_sb[:16], in_=w_mlp1)
        S.dma(d_wts, out=m23_sb, in_=w_mlp23)
        S.dma(d_wts, out=m4_sb, in_=w_mlp4)
        ready_wts = S.dma(d_wts, out=wo_sb, in_=w_out)
        ew_sb, ei_sb = small(10), small(10)
        d_ew = done("ew")
        n_full = T1 // NP
        rest = T1 - n_full * NP
        for sb, dr, ty in ((ew_sb, ew, F32), (ei_sb, ei, I32)):
            v = sb.bitcast(ty).rearrange("p (t k) -> p t k", k=2) if ty is I32 else sb.rearrange("p (t k) -> p t k", k=2)
            S.dma(d_ew, out=v[:NP, :n_full], in_=dr[:n_full * NP].rearrange("(t p) k -> p t k", p=NP))
            ready_ew = S.dma(d_ew, out=v[:rest, n_full], in_=dr[n_full * NP:])

        sorted_edges = dram("sorted_edges", [SLOTS, REC])
        m = G("memset", ap=recs, constant=0.0)
        m = G("memset", m, ap=recs[:, :, 1], constant=-1.0)
        d_fill = done("fill")
        filled = G.dma(d_fill, m, out=sorted_edges.rearrange("(p s) c -> p (s c)", p=128),
                       in_=recs.rearrange("p s c -> p (s c)"))
        ws, d_ws0 = dram("pair_rows", [FT * TILE, D]), done("zero_rows")
        zrow = carve(D, zone + 16000)
        m = G("memset", ap=zrow, constant=0.0)
        zeroed = G.dma(d_ws0, m, out=ws.rearrange("(t p) d -> p t d", p=128),
                       in_=zrow.unsqueeze(1).to_broadcast([128, FT, D]))

        er = edges[:EP]
        V("tensor_copy", ready_edge, out=er[:, :, 0].bitcast(I32), in_=src_i[:EP].bitcast(I32))
        dstf = carve(EJ, zone + 14240)[:EP]
        got_dst = V("tensor_copy", out=dstf, in_=dst_i[:EP].bitcast(I32))
        win = carve(EJ, zone + 14560)[:EP]
        c = V("tensor_scalar", got_dst, out=win, in0=dstf, scalar1=float(NP), scalar2=None, op0=ALU.is_ge)
        for w in range(2, NT):
            c = V("scalar_tensor_tensor", c, out=win, in0=dstf, scalar=float(NP * w), in1=win,
                  op0=ALU.is_ge, op1=ALU.add)
        in_win = carve(NT * EJ, zone + 8000)[:EP]
        in_win = in_win.rearrange("p (w j) -> p w j", w=NT)
        for w in range(NT):
            c2 = V("tensor_scalar", c, out=in_win[:, w], in0=win, scalar1=float(w), scalar2=None, op0=ALU.is_equal)
        row_tot = small(NT)
        c = V("tensor_reduce", c2, out=row_tot[:EP], in_=in_win, op=ALU.add, axis=AX.X)
        pe = PE("matmul", c, ready_const, out=banks[0][:EP, 0:NT], lhsT=before[:EP, :EP], rhs=row_tot[:EP],
                start=True, stop=True)
        pe = PE("matmul", out=banks[1][:, 0:NT], lhsT=ones[:EP, :], rhs=row_tot[:EP], start=True, stop=True)
        n_win, end_win, base_win, tmp_win = small(NT), small(NT), small(NT), small(NT)

        def whole(count, least, unit, shift, ends, base, pe, n, tmp):
            c = V("tensor_scalar", pe, out=tmp.bitcast(I32), in0=count, scalar1=float(unit - 1), scalar2=None,
                  op0=ALU.add)
            c = V("tensor_scalar", c, out=tmp.bitcast(I32), in0=tmp.bitcast(I32), scalar1=shift, scalar2=None,
                  op0=ALU.logical_shift_right)
            c = V("tensor_copy", c, out=n, in_=tmp.bitcast(I32))
            c = V("tensor_scalar", c, out=n, in0=n, scalar1=float(least), scalar2=None, op0=ALU.max)
            w = n.shape[-1]
            c = V("tensor_tensor_scan", c, ready_const, out=ends, data0=ones[:, 0:w], data1=n, initial=0.0,
                  op0=ALU.mult, op1=ALU.add)
            c = V("tensor_tensor", c, out=base, in0=ends, in1=n, op=ALU.subtract)
            return V("tensor_scalar", c, out=base, in0=base, scalar1=float(unit), scalar2=None, op0=ALU.mult)

        c = whole(banks[1][:, 0:NT], 1, GROUP, 9, end_win, base_win, pe, n_win, tmp_win)
        start = small(NT)[:EP]
        c = V("scalar_tensor_tensor", c, out=start, in0=banks[0][:EP, 0:NT], scalar=-1.0, in1=base_win[:EP],
              op0=ALU.add, op1=ALU.add)
        slot = carve(EJ, zone + 14880)[:EP]
        seq = [carve(EJ, zone + 11300 + EJ * i)[:EP] for i in range(2)]
        ones_row = carve(EJ, zone + 11940)[:EP]
        V("memset", ap=ones_row, constant=1.0)
        c = V("memset", c, ap=slot, constant=0.0)
        s_prev = c
        for w in range(NT):
            c = V("tensor_tensor_scan", s_prev, out=seq[w % 2], data0=ones_row, data1=in_win[:, w], initial=start[:, w:w + 1],
                  op0=ALU.mult, op1=ALU.add)
            c = V("tensor_tensor", c, out=seq[w % 2], in0=seq[w % 2], in1=in_win[:, w], op=ALU.mult)
            s_prev = V("tensor_tensor", c, out=slot, in0=slot, in1=seq[w % 2], op=ALU.add)
        slot_i = small(EJ)[:EP].bitcast(I32)
        c = V("tensor_copy", s_prev, out=slot_i, in_=slot)
        V("tensor_copy", out=er[:, :, 1], in_=dstf)
        V("tensor_copy", out=er[:, :, 2:6], in_=at4[:EP].rearrange("p (j c) -> p j c", c=4))
        V("memset", ap=er[:, :, 14:16], constant=0.0)
        recs_done = V("tensor_copy", out=er[:, :, 6:14], in_=at8[:EP].rearrange("p (j c) -> p j c", c=8))
        d_scatter = done("scatter")
        left = list(range(EJ))

        def scatter_edges(n):
            for _ in range(min(n, len(left))):
                j = left.pop(0)
                G.dma(d_scatter, recs_done, filled, out=sorted_edges,
                      out_offset=bass.IndirectOffsetOnAxis(ap=slot_i[:, j:j + 1], axis=0),
                      in_=er[:, j, :], in_offset=None)

        g_win, g_same, g_row = carve(NG, zone + 15600), small(NG), small(NG)
        g_first = small(NG)
        cmp = carve(NG * NT, zone + 17000).rearrange("p (g w) -> p g w", w=NT)
        c = V("tensor_tensor", out=cmp, in0=K["node"][:, 0:NG].unsqueeze(2).to_broadcast([128, NG, NT]),
              in1=end_win.unsqueeze(1).to_broadcast([128, NG, NT]), op=ALU.is_ge)
        c = V("tensor_reduce", c, out=g_win, in_=cmp, op=ALU.add, axis=AX.X)
        c = V("tensor_scalar", c, out=g_win, in0=g_win, scalar1=float(NT - 1), scalar2=None, op0=ALU.min)
        c = V("memset", c, ap=g_same[:, 0:1], constant=0.0)
        c = V("tensor_tensor", c, out=g_same[:, 1:], in0=g_win[:, 1:], in1=g_win[:, :NG - 1], op=ALU.is_equal)
        c = V("tensor_scalar", c, out=g_first, in0=g_win, scalar1=float(NP), scalar2=None, op0=ALU.mult)
        row_f = cmp.rearrange("p g w -> p (g w)")[:, 0:NG]
        c = V("tensor_scalar", c, out=row_f, in0=g_first, scalar1=K["part"], scalar2=None, op0=ALU.add)
        c = V("scalar_tensor_tensor", c, out=row_f[:, :NG - 1], in0=g_same[:, 1:], scalar=BIG,
              in1=row_f[:, :NG - 1], op0=ALU.mult, op1=ALU.add)
        groups_known = V("tensor_copy", c, out=g_row.bitcast(I32), in_=row_f)

        stats, mv, rstd, eps_v, nt_ = small(6 * 2), small(2 * NT), small(NT), small(NT), small(NT)

        def layer_norm(ready, tiles=NT):
            q = mv[:NP].rearrange("p (t c) -> p t c", c=2)
            c = None
            for t in range(tiles):
                st = stats[:NP, 6 * (t % 2):6 * (t % 2) + 6]
                s = V("bn_stats", *([ready] if t == 0 else []), *([V.last] if t else []), out=st, in_=xs[:NP, t])
                c = V("bn_aggr", s, out=q[:, t], in_=st)
            c = V("tensor_scalar", c, out=eps_v[:NP, :tiles], in0=q[:, :tiles, 1], scalar1=1e-5, scalar2=None,
                  op0=ALU.add)
            a = A("activation", c, out=nt_[:NP, :tiles], in_=eps_v[:NP, :tiles], func=ACT.Sqrt)
            c = V("reciprocal", a, out=rstd[:NP, :tiles], in_=nt_[:NP, :tiles])
            c = V("tensor_tensor", c, out=nt_[:NP, :tiles], in0=rstd[:NP, :tiles], in1=rstd[:NP, :tiles],
                  op=ALU.mult)
            c = V("tensor_tensor", c, out=nt_[:NP, :tiles], in0=nt_[:NP, :tiles], in1=eps_v[:NP, :tiles],
                  op=ALU.mult)
            c = V("tensor_scalar", c, out=nt_[:NP, :tiles], in0=nt_[:NP, :tiles], scalar1=-0.5, scalar2=1.5,
                  op0=ALU.mult, op1=ALU.add)
            c = V("tensor_tensor", c, out=rstd[:NP, :tiles], in0=nt_[:NP, :tiles], in1=rstd[:NP, :tiles],
                  op=ALU.mult)
            each = []
            for t in range(tiles):
                each.append(V("tensor_scalar", c, out=ln[:NP, t], in0=xs[:NP, t], scalar1=q[:, t, 0:1],
                              scalar2=rstd[:NP, t:t + 1], op0=ALU.subtract, op1=ALU.mult))
            return each

        def transpose_ln(each, tiles=NT, free=None):
            copied = [None, None]
            for t in range(tiles):
                bank = banks[t % 2]
                for k in range(4):
                    PE("transpose", each[t], ready_const, *[f for f in (copied[t % 2], free) if f],
                       out=bank[:, k * 128:k * 128 + NP], in_=ln[:NP, t, k * 128:(k + 1) * 128],
                       identity=ident[:NP, :NP])
                copied[t % 2] = A("activation", PE.last, out=lnT[:, :, t * NP:(t + 1) * NP],
                                  in_=bank[:, :].rearrange("p (k n) -> p k n", k=4)[:, :, 0:NP], func=ACT.Copy)
            return A.last

        stage("segment")
        ancf = small(TOP)
        lo_p, hi_p, t7 = small(1), small(1), small(TOP)
        c = V("tensor_copy", ready_tree, out=ancf, in_=anc_i.bitcast(I32))
        u = V("tensor_scalar", out=t7, in0=K["left"], scalar1=-BIG, scalar2=None, op0=ALU.mult)
        c = V("tensor_tensor", c, out=anc_i, in0=ancf, in1=K["right"], op=ALU.mult)
        c = V("tensor_tensor", c, u, out=t7, in0=t7, in1=anc_i, op=ALU.add)
        c = V("tensor_reduce", c, out=lo_p, in_=t7, op=ALU.max, axis=AX.X)
        c = V("tensor_tensor", c, out=anc_i, in0=ancf, in1=K["left"], op=ALU.mult)
        c = V("scalar_tensor_tensor", c, out=t7, in0=K["right"], scalar=BIG, in1=anc_i, op0=ALU.mult, op1=ALU.add)
        bounds = V("tensor_reduce", c, out=hi_p, in_=t7, op=ALU.min, axis=AX.X)
        in_sub = carve(N, zone + 5000)
        lowq = carve(N, zone + 6300)
        c = V("tensor_scalar", bounds, out=lowq, in0=K["node"], scalar1=lo_p, scalar2=None, op0=ALU.is_ge)
        in_sub_done = V("scalar_tensor_tensor", c, out=in_sub, in0=K["node"], scalar=hi_p, in1=lowq,
                        op0=ALU.is_lt, op1=ALU.mult)
        subf = carve(LEAVES - 1, zone + 4400)
        c = V("tensor_copy", out=subf, in_=sub_i.bitcast(I32))
        low = [carve(LEAVES, zone + 512 * i) for i in range(2)]
        high = [carve(LEAVES, zone + 1024 + 512 * i) for i in range(2)]
        V("tensor_copy", out=low[0][:, 0:1], in_=lo_p)
        c = V("tensor_copy", c, out=high[0][:, 0:1], in_=hi_p)
        for lv in range(SEARCH_LEVELS - TOP):
            n = 2 ** lv
            a, b = lv % 2, 1 - lv % 2
            v = subf[:, n - 1:2 * n - 1]
            nl, nh = (z[b][:, 0:2 * n].rearrange("p (n s) -> p n s", s=2) for z in (low, high))
            V("tensor_copy", c, out=nl[:, :, 0], in_=low[a][:, 0:n])
            V("tensor_tensor", out=nl[:, :, 1], in0=low[a][:, 0:n], in1=v, op=ALU.max)
            V("tensor_tensor", out=nh[:, :, 0], in0=high[a][:, 0:n], in1=v, op=ALU.min)
            c = V("tensor_copy", out=nh[:, :, 1], in_=high[a][:, 0:n])
        f = (SEARCH_LEVELS - TOP) % 2
        key = carve(LEAVES, zone + 2048)
        c = V("tensor_tensor", c, out=key, in0=low[f], in1=high[f], op=ALU.is_ge)
        key_done = V("scalar_tensor_tensor", c, out=key, in0=key, scalar=2 * BIG, in1=low[f], op0=ALU.mult,
                     op1=ALU.add)
        for t in range(NT):
            PE.quiet("matmul", in_sub_done, out=banks[2][:NP, t:t + 1], lhsT=in_sub[:, t * NP:(t + 1) * NP],
                     rhs=K["sub512"], start=True, stop=True)
        first_leaf = PE("matmul", out=banks[2][:NP, NT:NT + 1], lhsT=in_sub[:, 0:NP], rhs=K["sub512"],
                        start=True, stop=True)
        leaf = small(NT)[:NP]
        hit = [carve(LEAVES, zone + 2560 + 512 * i)[:NP] for i in range(2)]
        hit_done = [None, None]
        for t in range(NT):
            b = banks[3 + t % 3]
            k = PE("matmul", key_done, *([reads[t - 3]] if t >= 3 else []), out=b[:NP, :],
                   lhsT=in_sub[:, t * NP:(t + 1) * NP], rhs=key, start=True, stop=True)
            if t == 0:
                reads = []
            c = V("scalar_tensor_tensor", k, out=hit[t % 2], in0=b[:NP, :], scalar=K["node_col"][:NP, t:t + 1],
                  in1=K["leaf1"][:NP], op0=ALU.is_le, op1=ALU.mult)
            reads.append(c)
            c = V("tensor_reduce", c, out=leaf[:, t:t + 1], in_=hit[t % 2], op=ALU.max, axis=AX.X)
        leaf_i = small(NT)[:NP].bitcast(I32)
        c = V("scalar_tensor_tensor", c, first_leaf, out=leaf_i, in0=banks[2][:NP, 0:NT], scalar=-1.0, in1=leaf,
              op0=ALU.add, op1=ALU.add)
        d_leaf = done("leaf")
        found = carve(4 * NT, zone + 12600)[:NP].bitcast(I32).rearrange("p (t c) -> p t c", c=4)
        for t in range(NT):
            got = G.dma(d_leaf, c, out=found[:, t], out_offset=None, in_=leaf_table,
                        in_offset=bass.IndirectOffsetOnAxis(ap=leaf_i[:, t:t + 1], axis=0))
        scatter_edges(24)
        f4 = carve(4 * NT, zone + 12700)[:NP].rearrange("p (t c) -> p t c", c=4)
        c = V("tensor_copy", got, out=f4, in_=found)
        rcnt = small(NT)[:NP]
        c2 = V("tensor_tensor", c, out=rcnt, in0=f4[:, :, 3], in1=f4[:, :, 2], op=ALU.subtract)
        c2 = V("tensor_scalar", c2, out=rcnt, in0=rcnt, scalar1=1.0, scalar2=None, op0=ALU.add)
        c2 = V("reciprocal", c2, out=rcnt, in_=rcnt)
        diag = [carve(NP, zone + 2560 + 128 * i)[:NP] for i in range(NT)]
        for t in range(NT):
            dg = V("tensor_scalar", c, out=diag[t], in0=ident[:NP, :NP], scalar1=f4[:, t, 1:2], scalar2=None,
                   op0=ALU.mult)
            bank = banks[6] if t < 4 else banks[7] if t < 8 else banks[2]
            o = (t % 4) * 128
            sr = PE("matmul", dg, out=bank[:NP, o:o + NP], lhsT=ones[:NP, :NP], rhs=diag[t], start=True, stop=True)
        seg_row = carve(N, lnT_at)[:NP]
        for t in range(NT):
            bank = banks[6] if t < 4 else banks[7] if t < 8 else banks[2]
            o = (t % 4) * 128
            c2 = V("tensor_copy", sr, out=seg_row[:, t * NP:(t + 1) * NP], in_=bank[:NP, o:o + NP])
        row_done = c2
        normed = layer_norm(ready_x)
        member = carve(NT * N, zone)[:NP].rearrange("p (t q) -> p t q", t=NT)
        mem = [V("tensor_scalar", row_done, normed[-1], out=member[:, t], in0=seg_row, scalar1=f4[:, t, 0:1],
                 scalar2=None, op0=ALU.is_equal) for t in range(NT)]
        for t in range(NT):
            b = banks[3 + t % 3]
            for k in range(NT):
                c = PE("matmul", mem[k], normed[k], *([reads[-3]] if t >= 3 else [reads[-1]]), out=b[:NP, :],
                       lhsT=member[:, k, t * NP:(t + 1) * NP], rhs=ln[:NP, k], start=k == 0, stop=k == NT - 1)
            reads.append(V("scalar_tensor_tensor", c, out=xs[:NP, t], in0=b[:NP, :], scalar=rcnt[:, t:t + 1],
                           in1=xs[:NP, t], op0=ALU.mult, op1=ALU.add))
        segment_read = PE.last

        stage("route")
        normed = layer_norm(V.last)
        lnT_done = transpose_ln(normed, free=mem[-1])
        for t in range(NT):
            for k in range(4):
                c = PE("matmul", lnT_done, ready_wts, out=banks[2][:NP, t * E0:(t + 1) * E0],
                       lhsT=lnT[:, k, t * NP:(t + 1) * NP], rhs=gate_sb[:, k], start=k == 0, stop=k == 3)
        R0 = zone + 13000
        r_at = [R0]

        def r3():
            r_at[0] += NT * E0
            return carve(NT * E0, r_at[0] - NT * E0)[:NP].rearrange("p (t e) -> p t e", e=E0)

        logit, cand, pick1, pick2, both, rank = (r3() for _ in range(6))
        eid = K["node"][:NP, 0:E0].unsqueeze(1).to_broadcast([NP, NT, E0])
        top1, top2, first = small(NT)[:NP], small(NT)[:NP], small(NT)[:NP]

        def wide(v):
            return v.unsqueeze(2).to_broadcast([NP, NT, E0])

        c = V("tensor_copy", c, out=logit, in_=banks[2][:NP, 0:NT * E0].rearrange("p (t e) -> p t e", e=E0))
        for best, pick in ((top1, pick1), (top2, pick2)):
            c = V("tensor_reduce", c, out=best, in_=logit, op=ALU.max, axis=AX.X)
            c = V("tensor_tensor", c, out=cand, in0=logit, in1=wide(best), op=ALU.is_lt)
            c = V("scalar_tensor_tensor", c, out=cand, in0=cand, scalar=float(E0), in1=eid, op0=ALU.mult,
                  op1=ALU.add)
            c = V("tensor_reduce", c, out=first, in_=cand, op=ALU.min, axis=AX.X)
            c = V("tensor_tensor", c, out=pick, in0=eid, in1=wide(first), op=ALU.is_equal)
            c = V("scalar_tensor_tensor", c, out=logit, in0=pick, scalar=-1e30, in1=logit, op0=ALU.mult,
                  op1=ALU.add)
        c = V("tensor_tensor", c, out=both, in0=pick1, in1=pick2, op=ALU.add)
        picked = c
        for t in range(NT):
            for k in range(t + 1):
                PE.quiet("matmul", picked, out=banks[6][:NP, t * E0:(t + 1) * E0],
                         lhsT=before[:NP, :NP] if k == t else ones[:NP, :NP], rhs=both[:, k], start=k == 0,
                         stop=k == t)
        for k in range(NT):
            c = PE("matmul", out=banks[7][:, 0:E0], lhsT=ones[:NP, :], rhs=both[:, k], start=k == 0,
                   stop=k == NT - 1)
        n_t, end_t, base_t, tmp_t = small(E0), small(E0), small(E0), small(E0)
        c = whole(banks[7][:, 0:E0], 0, TILE, 7, end_t, base_t, c, n_t, tmp_t)
        c = V("tensor_tensor", c, out=rank, in0=banks[6][:NP, 0:NT * E0].rearrange("p (t e) -> p t e", e=E0),
              in1=base_t[:NP].unsqueeze(1).to_broadcast([NP, NT, E0]), op=ALU.add)
        pair_i = []
        for pick in (pick1, pick2):
            c = V("tensor_tensor", c, out=cand, in0=rank, in1=pick, op=ALU.mult)
            c = V("tensor_reduce", c, out=first, in_=cand, op=ALU.add, axis=AX.X)
            pair_i.append(small(NT)[:NP].bitcast(I32))
            c = V("tensor_copy", c, out=pair_i[-1], in_=first)
        pairs_known = c
        wt = [small(NT)[:NP], small(NT)[:NP]]
        c = V("tensor_tensor", out=first, in0=top2, in1=top1, op=ALU.subtract)
        a = A("activation", c, out=top2, in_=first, func=ACT.Exp)
        c = V("tensor_scalar", a, out=first, in0=top2, scalar1=1.0, scalar2=None, op0=ALU.add)
        c = V("reciprocal", c, out=wt[0], in_=first)
        weights_known = V("tensor_tensor", c, out=wt[1], in0=wt[0], in1=top2, op=ALU.mult)
        te = small(FT)
        cmp = carve(FT * E0, R0 + 600).rearrange("p (g e) -> p g e", e=E0)
        c = V("tensor_tensor", out=cmp, in0=K["node"][:, 0:FT].unsqueeze(2).to_broadcast([128, FT, E0]),
              in1=end_t.unsqueeze(1).to_broadcast([128, FT, E0]), op=ALU.is_ge)
        c = V("tensor_reduce", c, out=te, in_=cmp, op=ALU.add, axis=AX.X)
        c = V("tensor_scalar", c, out=te, in0=te, scalar1=float(E0 - 1), scalar2=None, op0=ALU.min)
        t_same = cmp.rearrange("p g e -> p (g e)")[:, 0:FT]
        c = V("memset", c, ap=t_same[:, 0:1], constant=0.0)
        c = V("tensor_tensor", c, out=t_same[:, 1:], in0=te[:, 1:], in1=te[:, :FT - 1], op=ALU.is_equal)
        c = V("tensor_scalar", c, out=te, in0=te, scalar1=128.0, scalar2=K["part"], op0=ALU.mult, op1=ALU.add)
        c = V("scalar_tensor_tensor", c, out=te, in0=t_same, scalar=float(SKIP), in1=te, op0=ALU.mult, op1=ALU.add)
        w_row = small(HB * FT).bitcast(I32).rearrange("p (b t) -> p b t", b=HB)
        for b in range(HB):
            tiles_known = V("tensor_scalar", c, out=w_row[:, b], in0=te, scalar1=float(b * E0 * 128), scalar2=None,
                            op0=ALU.add)
        d_pair = done("pair")
        rows_sent = None
        for t in range(NT):
            for kk in range(2):
                rows_sent = G.dma(d_pair, pairs_known, normed[t], zeroed, out=ws,
                                  out_offset=bass.IndirectOffsetOnAxis(ap=pair_i[kk][:, t:t + 1], axis=0),
                                  in_=ln[:NP, t], in_offset=None)

        stage("expert", chained=False)
        up = [carve(4096, zone + 4096 * b).rearrange("p (k c h) -> p k c h", k=4, c=2) for b in range(HB)]
        down = [carve(2048, zone + 4096 * HB + 2048 * b).rearrange("p (k d) -> p k d", k=4) for b in range(HB)]
        f_at = [ln_at]

        def buf(words, n=2):
            f_at[0] += words * n
            assert f_at[0] <= lnT_at + 4 * N
            return [carve(words, f_at[0] - words * (n - i)) for i in range(n)]

        xin, xT, sil, hid, hT, yo = buf(512), buf(512), buf(512), buf(1536, 1), buf(1536), buf(512)
        d_up = [done(f"up{b}") for b in range(HB)]
        d_dn = [done(f"down{b}") for b in range(HB)]
        d_in = [done(f"in{i}") for i in range(2)]
        d_out = [done(f"rows{i}") for i in range(2)]
        ys = dram("pair_out", [FT * TILE, D])
        up_read, dn_read = [segment_read] * HB, [zeroed] * HB
        xin_free, xT_free, h_free, hT_free, yo_free = [None] * 2, [None] * 2, None, [None] * 2, [None] * 2
        b01_free = [A.last, A.last]
        sil_free = [None, None]
        hb_free = [None, None]
        ty_free = None
        some = lambda *f: [v for v in f if v is not None]
        up_in, dn_in = [None] * HB, [None] * HB
        for i in range(FT):
            for b in range(HB):
                up_in[b] = G.dma(d_up[b], tiles_known, up_read[b], out=up[b].rearrange("p k c h -> p (k c h)"),
                                 out_offset=None, in_=w13,
                                 in_offset=bass.IndirectOffsetOnAxis(ap=w_row[:, b, i:i + 1], axis=0),
                                 bounds_check=HB * E0 * 128 - 1, oob_is_err=False)
            for b in range(HB):
                dn_in[b] = G.dma(d_dn[b], tiles_known, dn_read[b], out=down[b].rearrange("p k d -> p (k d)"),
                                 out_offset=None, in_=w2,
                                 in_offset=bass.IndirectOffsetOnAxis(ap=w_row[:, b, i:i + 1], axis=0),
                                 bounds_check=HB * E0 * 128 - 1, oob_is_err=False)
            scatter_edges(12)
            s = i % 2
            came = S.dma(d_in[s], rows_sent, lnT_done, picked, *some(xin_free[s]),
                         out=xin[s], in_=ws[i * TILE:(i + 1) * TILE])
            for k in range(4):
                tr = PE("transpose", came, *some(b01_free[0]), out=banks[0][:, k * 128:(k + 1) * 128],
                        in_=xin[s][:, k * 128:(k + 1) * 128], identity=ident)
            xin_free[s] = tr
            b01_free[0] = xt = A("activation", tr, *some(xT_free[s]), out=xT[s], in_=banks[0][:, :], func=ACT.Copy)
            for b in range(HB):
                q = b % 2
                for cc in range(2):
                    bank = banks[2 + 2 * q + cc]
                    for k in range(4):
                        mmt = PE("matmul", xt, up_in[b], *some(hb_free[q]), out=bank[:, :],
                                 lhsT=xT[s][:, k * 128:(k + 1) * 128], rhs=up[b][:, k, cc], start=k == 0,
                                 stop=k == 3)
                    if cc == 0:
                        sl = A("activation", mmt, *some(sil_free[q]), out=sil[q], in_=bank[:, :], func=ACT.Silu)
                up_read[b] = mmt
                if b == HB - 1:
                    xT_free[s] = mmt
                sil_free[q] = hb_free[q] = V("tensor_tensor", mmt, sl, *some(h_free),
                                             out=hid[0][:, b * 512:(b + 1) * 512], in0=bank[:, :], in1=sil[q],
                                             op=ALU.mult)
                hb = V.last
                tb = 1 if b % 2 else 6
                for k in range(4):
                    o = (b * 4 + k) * 128
                    tr = PE("transpose", hb, *some(b01_free[1] if tb == 1 else ty_free),
                            out=banks[tb][:, k * 128:(k + 1) * 128], in_=hid[0][:, o:o + 128], identity=ident)
                ht = A("activation", tr, *some(hT_free[s]), out=hT[s][:, b * 512:(b + 1) * 512],
                       in_=banks[tb][:, :], func=ACT.Copy)
                if tb == 1:
                    b01_free[1] = ht
                else:
                    ty_free = ht
                if b == 0:
                    h_parts = []
                h_parts.append(ht)
            h_free = tr
            for b in range(HB):
                for k in range(4):
                    mmt = PE("matmul", h_parts[b], dn_in[b], *some(yo_free[0] and y_read if i else None),
                             out=banks[7][:, :], lhsT=hT[s][:, (b * 4 + k) * 128:(b * 4 + k + 1) * 128],
                             rhs=down[b][:, k], start=b + k == 0, stop=b == HB - 1 and k == 3)
                dn_read[b] = mmt
            hT_free[s] = mmt
            y_read = V("tensor_copy", mmt, *some(yo_free[s]), out=yo[s], in_=banks[7][:, :])
            yo_free[s] = S.dma(d_out[s], y_read, out=ys[i * TILE:(i + 1) * TILE], in_=yo[s])
            if i == 0:
                yo_free[0] = yo_free[s]
        scatter_edges(EJ)
        scattered = (d_scatter.sem, d_scatter.count)
        yg = [carve(512, zone + 512 * i)[:NP] for i in range(20)]
        d_yg = [done(f"pick{i}") for i in range(4)]
        yg_in = []
        for t in range(NT):
            for kk in range(2):
                i = 2 * t + kk
                yg_in.append(G.dma(d_yg[i % 4], *yo_free, mmt, *([yg_in[i - 4]] if i >= 4 else []), out=yg[i],
                                   out_offset=None, in_=ys,
                                   in_offset=bass.IndirectOffsetOnAxis(ap=pair_i[kk][:, t:t + 1], axis=0)))
                V("scalar_tensor_tensor", yg_in[i], weights_known, *([V.last] if kk else []), out=xs[:NP, t],
                  in0=yg[i], scalar=wt[kk][:, t:t + 1], in1=xs[:NP, t], op0=ALU.mult, op1=ALU.add)

        stage("node")
        e_w = [carve(2048, edge_at + 2048 * i) for i in range(2)]
        d_ew_ = [done(f"w_second{i}") for i in range(2)]

        def load_second(e, *free):
            S.dma(d_ew_[e % 2], *free, out=e_w[e % 2][:, 0:1024], in_=v1[e])
            return S.dma(d_ew_[e % 2], *free, out=e_w[e % 2][:, 1024:2048], in_=v2[e])

        second_in = [load_second(e, scattered) for e in range(2)]
        d_rec = done("records")
        recs_in = S.dma(d_rec, scattered, out=recs, in_=sorted_edges.rearrange("(s p) c -> p s c", p=128))
        normed = layer_norm(V.last)
        copied = [None, None]
        table = dram("node_table", [N, 4 * MUL])
        d_tab = [done(f"table{i}") for i in range(2)]
        z = [zone + 10400 + 512 * i for i in range(6)]
        nT = [carve(512, z[i]) for i in range(2)]
        rows = [carve(512, z[2 + i])[:NP] for i in range(2)]
        sent = [None, None]
        nT_free, rows_ev = [None, None], [None, None]
        for t in range(NT):
            s = t % 2
            for k in range(4):
                piece = ln[:NP, t, 0:128] if k == 0 else ln[:NP, t, 128:512].rearrange("p (u m) -> p m u", m=3)[:, k - 1]
                tr = PE("transpose", normed[t], *some(copied[s]), out=banks[s][:, k * 128:k * 128 + NP], in_=piece,
                        identity=ident[:NP, :NP])
            copied[s] = A("activation", tr, *some(nT_free[s]),
                          out=nT[s].rearrange("p (k n) -> p k n", k=4)[:, :, 0:NP],
                          in_=banks[s][:, :].rearrange("p (k n) -> p k n", k=4)[:, :, 0:NP], func=ACT.Copy)
            for k in range(4):
                mmt = PE("matmul", copied[s], *some(rows_ev[s]), out=banks[2 + s][:NP, k * 128:(k + 1) * 128],
                         lhsT=nT[s][:, k * 128:k * 128 + NP], rhs=wup_sb[:, 0:128] if k == 0 else wup_sb[:, 128:256],
                         start=True, stop=True)
            nT_free[s] = mmt
            rows_ev[s] = V("tensor_scalar", mmt, *some(sent[s]), out=rows[s], in0=banks[2 + s][:NP, :],
                           scalar1=MUL ** -0.5, scalar2=None, op0=ALU.mult)
            sent[s] = S.dma(d_tab[s], rows_ev[s], out=table[t * NP:(t + 1) * NP], in_=rows[s])
        table_in = list(sent)

        stage("edge", chained=False)
        g_at = [zone]

        def ring(words, n):
            g_at[0] += words * n
            assert g_at[0] <= zone + 18432 + 0, g_at[0] - zone
            return [carve(words, g_at[0] - words * (n - i)) for i in range(n)]

        NGAT, NM = 6, 2
        gat = ring(512, NGAT)
        d_gat = [done(f"gather{i}") for i in range(NGAT)]
        pick_ = ring(5 * NP + 3, NM)
        msg0, msg1, vec = ring(512, NM), ring(256, NM), ring(128, NM)
        run_ = ring(1024, 2)
        act1, act2, act3 = ring(512, 1), ring(512, 1), ring(512, 2)
        fT = ring(512, 1)
        sums = dram("sums", [N, 8 * MUL])
        d_sum = [done(f"sum{i}") for i in range(2)]
        start_edges = [V.last, PE.last, A.last] + table_in
        rel_ready = []
        src_words = carve(NG * 4, lnT_at + NPAIR * 64).bitcast(I32)
        for g in range(NG):
            rel_ready.append(None)
        rv = recs.rearrange("p (g s) c -> p g s c", g=NG)
        rel = V("tensor_tensor", recs_in, groups_known, out=rv[:, :, :, 1], in0=rv[:, :, :, 1],
                in1=g_first.unsqueeze(2).to_broadcast([128, NG, 4]), op=ALU.subtract)
        rel = V("tensor_copy", recs_in, out=src_words, in_=recs[:, :, 0].bitcast(I32))
        feat = carve(NPAIR * 4 * 16, lnT_at).rearrange("p (r k g c) -> p r k g c", r=NPAIR, k=4, g=2)
        for h in range(2):
            packed = V("tensor_copy", recs_in, out=feat[:, :, :, h],
                       in_=recs.rearrange("p (r g k) c -> p r g k c", r=NPAIR, g=2)[:, :, h, :, 6:14])
        run_zero = V("memset", *start_edges, ap=run_[1], constant=0.0)
        gat_free = [None] * NGAT
        gat_in = {}
        NTILE = NG * 4

        def tile_of(i):
            return i

        def gather(i):
            s = i % NGAT
            gat_in[i] = G.dma(d_gat[s], rel, *start_edges, *some(gat_free[s]), out=gat[s], out_offset=None,
                              in_=table, in_offset=bass.IndirectOffsetOnAxis(ap=src_words[:, i:i + 1], axis=0))

        mlp_free = {"b7": None, "fT": None, "a1": None, "a2": None, "a3": [None, None]}
        mlp_out = {}

        def mlp_step(pr, stp):
            b7 = banks[7]
            if stp == 0:
                for k in range(4):
                    both_g = feat[:, pr, k].rearrange("p g c -> p (g c)")
                    tr = PE("transpose", packed, *start_edges, *some(mlp_free["b7"]),
                            out=b7[:16, k * 128:(k + 1) * 128], in_=both_g, identity=ident)
                mlp_free["b7"] = mlp_out["f"] = A("activation", tr, *some(mlp_free["fT"]), out=fT[0][:16],
                                                  in_=b7[:16, :], func=ACT.Copy)
            elif stp == 1:
                mlp_free["fT"] = mt = PE("matmul", mlp_out["f"], mlp_free["b7"], out=b7[:, :], lhsT=m1_sb[:16],
                                         rhs=fT[0][:16], start=True, stop=True)
                mlp_free["b7"] = mlp_out[1] = A("activation", mt, *some(mlp_free["a1"]), out=act1[0], in_=b7[:, :],
                                                func=ACT.Silu, scale=8 ** -0.5)
            elif stp == 2:
                mlp_free["a1"] = mt = PE("matmul", mlp_out[1], out=b7[:, :], lhsT=m23_sb[:, 0:128], rhs=act1[0],
                                         start=True, stop=True)
                mlp_free["b7"] = mlp_out[2] = A("activation", mt, *some(mlp_free["a2"]), out=act2[0], in_=b7[:, :],
                                                func=ACT.Silu, scale=SILU_2MOM / 8)
            else:
                mlp_free["a2"] = mt = PE("matmul", mlp_out[2], out=b7[:, :], lhsT=m23_sb[:, 128:256], rhs=act2[0],
                                         start=True, stop=True)
                mlp_free["b7"] = mlp_out[3, pr] = A("activation", mt, *some(mlp_free["a3"][pr % 2]),
                                                    out=act3[pr % 2], in_=b7[:, :], func=ACT.Silu,
                                                    scale=SILU_2MOM / 8)

        pick_free, msg_free, vec_free, tp_free = [None] * NM, [None] * NM, [None] * NM, [None] * 3
        agg_free = [None] * 2
        run_free = [None] * 2
        run_done = [None, run_zero]
        tp_in = {}

        def weights_of(i):
            pr, half, k = i // 8, (i // 4) % 2, i % 4
            b = banks[4 + i % 3]
            r = slice(64 * half, 64 * half + 64)
            tp_in[i] = PE("matmul", mlp_out[3, pr], *some(tp_free[i % 3]), out=b[:, :],
                          lhsT=act3[pr % 2][r, k * 128:(k + 1) * 128], rhs=m4_sb[r, :], start=True, stop=True)
            if i % 8 == 7:
                mlp_free["a3"][pr % 2] = tp_in[i]

        def y(i, c_):
            return recs[:, i, 2 + c_:3 + c_]

        for st in range(4):
            mlp_step(0, st)
        for i in range(NGAT):
            gather(i)
        weights_of(0)
        for i in range(NTILE):
            g, k, s, gs = i // 4, i % 4, i % NM, i % NGAT
            nodes = K["node"][:, 0:NP]
            pk = [pick_[s][:, j * NP:(j + 1) * NP] for j in range(5)]
            relc = recs[:, i, 1:2]
            for j in range(5):
                lane = G if j in (1, 2, 3) else V
                kw = dict(scalar2=None) if j == 4 else dict(scalar2=y(i, j), op1=ALU.mult)
                pk_t = lane("tensor_scalar", rel, *start_edges, *some(pick_free[s]), out=pk[j], in0=nodes, scalar1=relc,
                            op0=ALU.is_equal, **kw)
                if j == 3:
                    picks_g = pk_t
            picks_v = pk_t
            if i + 1 < NTILE:
                weights_of(i + 1)
            tp = banks[4 + i % 3][:, :].rearrange("p (w u) -> p w u", w=4)
            s0 = gat[gs][:, 0:128]
            s1 = gat[gs][:, 128:512].rearrange("p (m u) -> p m u", m=3)
            a = A("activation", gat_in[i], *some(vec_free[s]), out=vec[s], in_=s1[:, 0], func=ACT.Copy, scale=y(i, 1))
            c = V("scalar_tensor_tensor", a, out=vec[s], in0=s1[:, 1], scalar=y(i, 2), in1=vec[s], op0=ALU.mult,
                  op1=ALU.add)
            c = V("scalar_tensor_tensor", c, out=vec[s], in0=s1[:, 2], scalar=y(i, 3), in1=vec[s], op0=ALU.mult,
                  op1=ALU.add)
            V("tensor_tensor", tp_in[i], gat_in[i], *some(msg_free[s]), out=msg0[s][:, 0:128], in0=tp[:, 0], in1=s0, op=ALU.mult)
            V("tensor_tensor", out=msg1[s][:, 128:256], in0=tp[:, 1], in1=s0, op=ALU.mult)
            V("tensor_tensor", out=msg0[s][:, 128:512].rearrange("p (m u) -> p m u", m=3),
              in0=tp[:, 2:3].to_broadcast([128, 3, 128]), in1=s1, op=ALU.mult)
            made = V("tensor_tensor", c, out=msg1[s][:, 0:128], in0=tp[:, 3], in1=vec[s], op=ALU.mult)
            tp_free[i % 3] = vec_free[s] = gat_free[gs] = made
            if i + NGAT < NTILE:
                gather(i + NGAT)
            ga, gb = banks[2 * (g % 2)], banks[2 * (g % 2) + 1]
            af = some(agg_free[g % 2]) if k == 0 else []
            PE.quiet("matmul", made, picks_g, picks_v, *af, out=ga[:NP, :], lhsT=pk[0], rhs=msg0[s], start=k == 0,
                     stop=k == 3)
            PE.quiet("matmul", out=gb[:NP, 0:128], lhsT=pk[4], rhs=msg1[s][:, 0:128], start=k == 0, stop=k == 3,
                     skip_group_check=True)
            for j in range(3):
                mmt = PE("matmul", out=gb[:NP, 128 * (j + 1):128 * (j + 2)], lhsT=pk[1 + j],
                         rhs=msg1[s][:, 128:256], start=False, stop=k == 3, skip_group_check=True)
            pick_free[s] = msg_free[s] = mmt
            if i % 2 == 0 and i // 8 + 1 < NPAIR:
                mlp_step(i // 8 + 1, (i % 8) // 2)
            if k == 3:
                for hf, bank in ((0, ga), (1, gb)):
                    c = V("scalar_tensor_tensor", mmt, run_done[(g + 1) % 2], *some(run_free[g % 2]),
                          out=run_[g % 2][:NP, 512 * hf:512 * hf + 512],
                          in0=run_[(g + 1) % 2][:NP, 512 * hf:512 * hf + 512], scalar=g_same[:NP, g:g + 1],
                          in1=bank[:NP, :], op0=ALU.mult, op1=ALU.add)
                run_done[g % 2] = agg_free[g % 2] = c
                run_free[g % 2] = G.dma(d_sum[g % 2], c, out=sums,
                                        out_offset=bass.IndirectOffsetOnAxis(ap=g_row[:NP, g:g + 1].bitcast(I32), axis=0),
                                        in_=run_[g % 2][:NP], in_offset=None, bounds_check=N - 1, oob_is_err=False)

        stage("out")
        p4 = A("activation", ready_wts, out=wo_sb[:, 128:256], in_=wo_sb[:, 128:256], func=ACT.Copy, scale=3 ** -0.5)
        sin = ring_at(carve, ln_at, 1024, 3)
        sT = ring_at(carve, ln_at + 3072, 1024, 2)
        d_sin = [done(f"sums_in{i}") for i in range(3)]
        sin_free, sT_free, tb_free, o_free = [None] * 3, [None] * 2, [None] * 4, [None] * 2
        after_edges = [PE.last, V.last, A.last, *run_free]
        edge_read = V.last
        after_edges = [mmt, edge_read, *run_free]
        out_scale = (SILU_2MOM / 8) / 16 / 10
        for w in range(NT):
            s = w % 2
            inn = S.dma(d_sin[w % 3], *after_edges, *some(sin_free[w % 3]), out=sin[w % 3][:NP],
                        in_=sums[w * NP:(w + 1) * NP])
            for h in range(2):
                bank = banks[2 * s + h]
                for k in range(4):
                    o = (4 * h + k) * 128
                    tr = PE("transpose", inn, *some(tb_free[2 * s + h]), out=bank[:, k * 128:k * 128 + NP],
                            in_=sin[w % 3][:NP, o:o + 128], identity=ident[:NP, :NP])
                tb_free[2 * s + h] = A("activation", tr, *some(sT_free[s]),
                                       out=sT[s][:, 512 * h:512 * h + 512].rearrange("p (k n) -> p k n", k=4)[:, :, 0:NP],
                                       in_=bank[:, :].rearrange("p (k n) -> p k n", k=4)[:, :, 0:NP], func=ACT.Copy)
            sin_free[w % 3] = tr
            bank = banks[4 + s]
            for k in range(4):
                lo_, hi_ = (0, 4) if k == 0 else (4 + k, k)
                wo = wo_sb[:, 0:256] if k == 0 else wo_sb[:, 256:512]
                for n_, blk in enumerate((lo_, hi_)):
                    mmt = PE("matmul", A.last, p4, *some(o_free[s]), out=bank[:NP, k * 128:(k + 1) * 128],
                             lhsT=sT[s][:, blk * 128:blk * 128 + NP], rhs=wo[:, n_ * 128:(n_ + 1) * 128],
                             start=n_ == 0, stop=n_ == 1)
            sT_free[s] = mmt
            V("scalar_tensor_tensor", mmt, out=xs[:NP, w, 0:128], in0=bank[:NP, 0:128], scalar=out_scale,
              in1=xs[:NP, w, 0:128], op0=ALU.mult, op1=ALU.add)
            xv = xs[:NP, w, 128:512].rearrange("p (u m) -> p m u", m=3)
            o_free[s] = V("scalar_tensor_tensor", out=xv, in0=bank[:NP, 128:512].rearrange("p (m u) -> p m u", m=3),
                          scalar=out_scale, in1=xv, op0=ALU.mult, op1=ALU.add)

        stage("second")
        d_store = done("store")
        T5 = n_full + 1
        S.dma(d_store, V.last, out=out[T5 * NP:].rearrange("(t p) d -> p t d", p=NP), in_=xs[:NP, T5:])
        normed = layer_norm(V.last, T5)
        lnT_done = transpose_ln(normed, T5, free=o_free[1])
        hidT = [carve(1024, zone + 1024 * i).rearrange("p (h n) -> p h n", h=2) for i in range(2)]
        c = V("tensor_copy", ready_ew, out=ei_sb[:NP, 0:2 * n_full], in_=ei_sb[:NP, 0:2 * n_full].bitcast(I32))
        c = V("tensor_copy", c, out=ei_sb[:rest, 2 * n_full:], in_=ei_sb[:rest, 2 * n_full:].bitcast(I32))
        co = carve(E1 * 5, zone + 2100).rearrange("p (e t) -> p e t", e=E1)
        cw = carve(10, zone + 2200).rearrange("p (t k) -> p t k", k=2)
        for rws, tl in ((NP, slice(0, n_full)), (rest, slice(n_full, T5))):
            iv = ei_sb.rearrange("p (t k) -> p t k", k=2)[:rws, tl]
            wv = ew_sb.rearrange("p (t k) -> p t k", k=2)[:rws, tl]
            for e in range(E1):
                c = V("scalar_tensor_tensor", c, out=cw[:rws, tl], in0=iv, scalar=float(e), in1=wv, op0=ALU.is_equal,
                      op1=ALU.mult)
                c = V("tensor_reduce", c, out=co[:rws, e, tl], in_=cw[:rws, tl], op=ALU.add, axis=AX.X)
        coef = c
        hid_free, yb_free, hb_free = [None] * 2, [None] * 2, [None] * 2
        n_y = 0
        for e in range(E1):
            s = e % 2
            a1 = e_w[s][:, 0:1024].rearrange("p (k h) -> p k h", k=4)
            a2 = e_w[s][:, 1024:2048].rearrange("p (k d) -> p k d", k=2)
            for h in range(2):
                bank = banks[2 + h]
                for k in range(4):
                    mmt = PE("matmul", lnT_done, second_in[e], *some(hb_free[h]), out=bank[:, :],
                             lhsT=a1[:, k, h * 128:(h + 1) * 128], rhs=lnT[:, k, 0:T1], start=k == 0, stop=k == 3)
                hb_free[h] = A("activation", mmt, *some(hid_free[s]), out=hidT[s][:, h], in_=bank[:, :],
                               func=ACT.Gelu)
            for t in range(T5):
                r = NP if t < n_full else rest
                bank = banks[4 + n_y % 2]
                for k in range(2):
                    mmt = PE("matmul", hb_free[0], hb_free[1], *some(yb_free[n_y % 2]), out=bank[:r, :],
                             lhsT=hidT[s][:, k, t * NP:t * NP + r], rhs=a2[:, k], start=k == 0, stop=k == 1)
                yb_free[n_y % 2] = V("scalar_tensor_tensor", mmt, coef, *( [V.last] if t == 0 else []), out=xs[:r, t],
                                     in0=bank[:r, :], scalar=co[:r, e, t:t + 1], in1=xs[:r, t], op0=ALU.mult,
                                     op1=ALU.add)
                n_y += 1
            hid_free[s] = mmt
            if e + 2 < E1:
                second_in.append(load_second(e + 2, mmt))
        stored = S.dma(d_store, V.last, out=out[0:T5 * NP].rearrange("(t p) d -> p t d", p=NP), in_=xs[:NP, 0:T5])
        S.wait([stored, (d_pair.sem, d_pair.count), *run_free, *sent, *yo_free, filled, zeroed, scattered])

        block = ctx.enter_context(nc.Block())
        for lane, where in ((PE, block.tensor), (V, block.vector), (A, block.scalar), (G, block.gpsimd),
                            (S, block.sync)):
            where(lane.run)


def ring_at(carve, at, words, n):
    return [carve(words, at + words * i) for i in range(n)]


def kernel(**inputs):
    import concourse.bacc as bacc
    from concourse.bass_utils import run_bass_kernel_spmd

    a = {k: np.asarray(v) for k, v in inputs.items()}
    above, below, leaf = search_tree()
    src, dst = a["src"], a["dst"]
    leaf32 = leaf.astype(np.int32)
    table = np.stack([leaf32, np.where(leaf32 < 0, np.int32(NE - 1), leaf32), src[leaf], dst[leaf]], 1)

    def feature_rows(w, k):
        return w.reshape(w.shape[0], k, 128, w.shape[-1]).transpose(0, 2, 1, 3)

    w1, w3, w2 = (a[f"L0_ffn_{n}"].transpose(0, 2, 1) for n in ("w1", "w3", "w2"))
    w13 = np.stack([feature_rows(w, 4).reshape(E0, 128, 4, HB, 512) for w in (w1, w3)], 4)
    w13 = w13.transpose(3, 0, 1, 2, 4, 5).reshape(HB * E0 * 128, 4096)
    w2 = w2.reshape(E0, HB, 4, 128, D).transpose(1, 0, 3, 2, 4).reshape(HB * E0 * 128, 2048)

    def twice(w):
        z = np.zeros_like(w)
        return np.block([[w, z], [z, w]])

    g = {k[7:]: v for k, v in a.items() if k.startswith("L1_gnn_")}
    arrays = dict(
        consts=constants(), x=a["x"], anc=src[above], sub=src[below], leaf_table=table, src=src, dst=dst,
        ea4=a["edge_attr_4"], ea8=a["edge_attr_8"],
        gate=a["L0_ffn_gate_w"].T.reshape(4, 128, E0).transpose(1, 0, 2), w13=w13, w2=w2,
        w_up=np.concatenate([g["W_up0"], g["W_up1"]], 1), w_mlp1=twice(g["W_mlp1"]),
        w_mlp23=np.concatenate([twice(g["W_mlp2"]), twice(g["W_mlp3"])], 1),
        w_mlp4=np.concatenate([g["W_mlp4"], g["W_mlp4"]], 0),
        w_out=np.concatenate([g["W_out0"][:128], g["W_out0"][128:], g["W_out1"][:128], g["W_out1"][128:]], 1),
        ew=a["L1_ffn_expert_weights"], ei=a["L1_ffn_expert_indices"],
        v1=feature_rows(a["L1_ffn_w1"], 4).reshape(E1, 128, 1024),
        v2=feature_rows(a["L1_ffn_w2"], 2).reshape(E1, 128, 1024))
    nc = bacc.Bacc("TRN2", target_bir_lowering=False, num_devices=1)
    given, args = {}, []
    for name, v in arrays.items():
        v = np.ascontiguousarray(v)
        given[f"in_{name}"] = v
        args.append(nc.dram_tensor(f"in_{name}", v.shape, mybir.dt.from_np(v.dtype), kind="ExternalInput").ap())
    out = nc.dram_tensor("out", (N, D), F32, kind="ExternalOutput").ap()
    program(nc, *args, out)
    return run_bass_kernel_spmd(nc, [given], core_ids=[0]).results[0]["out"]
```

```python
from contextlib import ExitStack

import numpy as np

import concourse.bass as bass
from concourse import mybir

F32 = mybir.dt.float32
I32 = mybir.dt.int32
BF16 = mybir.dt.bfloat16
ALU = mybir.AluOpType
ACT = mybir.ActivationFunctionType
AX = mybir.AxisListType

N, D = 1250, 512
NP, NT = 128, 10
NPAD = NP * NT
NE, EP, EJ = 40000, 125, 320
SEARCH_LEVELS = 16
TOP = 7
LEAVES = 2 ** (SEARCH_LEVELS - TOP)
E0, H0 = 8, 1536
TILE = 128
FT = (2 * N - E0) // TILE + E0
HB = H0 // 512
WN, NW = 64, NPAD // 64
GT = 2
GROUP = GT * TILE
NG = (NE - NW) // GROUP + NW
BT = 8
NB = -(-NG * GT // BT)
NG = NB * BT // GT
NTILE = NG * GT
SLOTS = NG * GROUP
REC = 16
MUL, HID = 128, 64
SILU_2MOM = 1.679177
T1, E1, H1 = 512, 8, 256
BIG = float(2 ** 20)
ARENA = 52600
ZONE = HB * (4096 + 2048)
SKIP = 2 ** 20


def rows(t):
    return min(NP, N - t * NP)


def search_tree():
    lo, hi, levels = np.array([0]), np.array([NE]), []
    for _ in range(SEARCH_LEVELS):
        mid = (lo + hi) // 2
        levels.append(mid)
        lo, hi = np.stack([lo, mid], 1).ravel(), np.stack([mid, hi], 1).ravel()
    sub = np.arange(128)
    above = np.stack([levels[l][sub >> (TOP - l)] for l in range(TOP)], 1)
    below = np.concatenate([levels[l].reshape(128, -1) for l in range(TOP, SEARCH_LEVELS)], 1)
    return above, below, hi - 1


CONSTS = dict(ident=128, ones=128, before=128, node=NPAD, node_col=NT, valid=NT, leaf1=LEAVES, right=TOP, left=TOP,
              part=1, sub512=1)


def constants():
    p = np.arange(128)[:, None]
    sub = (p >> (TOP - 1 - np.arange(TOP)[None])) & 1
    c = dict(ident=np.eye(128), ones=np.ones((128, 128)), before=p < p.T,
             node=np.broadcast_to(np.arange(NPAD), (128, NPAD)), node_col=p + NP * np.arange(NT)[None],
             valid=p + NP * np.arange(NT)[None] < N,
             leaf1=np.broadcast_to(np.arange(LEAVES) + 1, (128, LEAVES)), right=sub, left=1 - sub,
             part=p, sub512=p * LEAVES)
    return np.concatenate([np.asarray(c[k], np.float32) for k in CONSTS], 1)


class Lane:

    def __init__(self, sem):
        self.new_sem, self.steps, self.seen = sem, [], {}
        self.chained, self.last = False, None

    def stage(self, name, chained):
        self.sem, self.count, self.chained = self.new_sem(name), 0, chained

    def wait(self, after):
        need = {}
        for s, v in after:
            if v > self.seen.get(id(s), 0):
                need[id(s)] = (s, max(v, need.get(id(s), (s, 0))[1]))
        for k, (s, v) in need.items():
            self.seen[k] = v
            self.steps.append(lambda e, s=s, v=v: e.wait_ge(s, v))

    def __call__(self, op, /, *after, **kw):
        self.wait([*after, self.last] if self.chained and self.last else after)
        self.count += 1
        self.steps.append(lambda e, s=self.sem: method(e, op)(**kw).then_inc(s, 1))
        self.last = (self.sem, self.count)
        return self.last

    def quiet(self, op, /, *after, **kw):
        self.wait(after)
        self.steps.append(lambda e: method(e, op)(**kw))

    def dma(self, done, /, *after, **kw):
        self.wait(after)
        done.count += 16
        op = "indirect_dma_start" if "out_offset" in kw else "dma_start"
        self.steps.append(lambda e: method(e, op)(**kw).then_inc(done.sem, 16))
        return (done.sem, done.count)

    def run(self, e):
        for s in self.steps:
            s(e)


def method(e, op):
    return {
        "matmul": lambda: e.matmul, "transpose": lambda: e.transpose, "activation": lambda: e.activation,
        "tensor_scalar": lambda: e.tensor_scalar, "tensor_tensor": lambda: e.tensor_tensor,
        "scalar_tensor_tensor": lambda: e.scalar_tensor_tensor, "tensor_copy": lambda: e.tensor_copy,
        "tensor_reduce": lambda: e.tensor_reduce, "tensor_tensor_scan": lambda: e.tensor_tensor_scan,
        "bn_stats": lambda: e.bn_stats, "bn_aggr": lambda: e.bn_aggr, "reciprocal": lambda: e.reciprocal,
        "memset": lambda: e.memset, "dma_start": lambda: e.dma_start,
        "indirect_dma_start": lambda: e.indirect_dma_start,
    }[op]()


class Done:

    def __init__(self, sem):
        self.sem, self.count = sem, 0


def program(nc, consts, x, anc, sub, leaf_table, src, dst, ea4, ea8, gate, w13, w2, w_up, w_mlp1, w_mlp23,
            w_mlp4, w_out, ew, ei, v1, v2, out):
    ctx = ExitStack()
    with ctx:
        n_sem = [0]

        def sem(name):
            n_sem[0] += 1
            return ctx.enter_context(nc.semaphore(f"{name}_{n_sem[0]}"))

        def done(name):
            return Done(sem(name))

        def dram(name, shape, dt=F32):
            return nc.dram_tensor(name, shape, dt, kind="Internal").ap()

        def some(*tokens):
            return [v for v in tokens if v is not None]

        PE, V, A, G, S = (Lane(lambda s, n=n: sem(f"{n}_{s}")) for n in ("pe", "dve", "act", "pool", "sp"))

        def stage(name, chained=True):
            for lane in (PE, V, A, G):
                lane.stage(name, chained and lane in (V, A))

        arena = ctx.enter_context(nc.sbuf_tensor("arena", [128, ARENA], F32))
        top = [0]

        def carve(words, at=None):
            if at is None:
                at, top[0] = top[0], top[0] + words
                assert top[0] <= ARENA, top[0]
            return arena[:, at:at + words]

        def zone_of(at, size):
            used = [0]

            def take(words):
                used[0] += words
                assert used[0] <= size, used[0]
                return carve(words, at + used[0] - words)

            return take

        banks = [ctx.enter_context(nc.psum_tensor(f"bank{i}", [128, 512], F32)) for i in range(8)]

        cst = carve(sum(CONSTS.values()))
        K, at = {}, 0
        for name, w in CONSTS.items():
            K[name] = cst[:, at:at + w]
            at += w
        ident, ones, before = K["ident"], K["ones"], K["before"]
        xs = carve(NT * D).rearrange("p (t d) -> p t d", t=NT)
        ln_at = top[0]
        ln = carve(NT * D).rearrange("p (t d) -> p t d", t=NT)
        lnT_at = top[0]
        lnT = carve(4 * NPAD).rearrange("p (k n) -> p k n", k=4)
        rec_at = top[0]
        recs = carve(NTILE * REC).rearrange("p (s c) -> p s c", c=REC)
        edge_at = top[0]
        edges = carve(EJ * REC).rearrange("p (j c) -> p j c", c=REC)
        zone = top[0]
        carve(ZONE)
        small_at = top[0]
        small = zone_of(small_at, ARENA - small_at)

        stage("load")
        d_const, d_x, d_tree, d_edge, d_wts = done("const"), done("x"), done("tree"), done("edge"), done("wts")
        early = zone_of(zone + NT * NPAD, ZONE - NT * NPAD)
        anc_i, sub_i = small(TOP), early(LEAVES - 1)
        S.dma(d_tree, out=anc_i.bitcast(I32), in_=anc)
        ready_tree = S.dma(d_tree, out=sub_i.bitcast(I32), in_=sub)
        ready_const = S.dma(d_const, out=cst, in_=consts)
        last = rows(NT - 1)
        blank = V("memset", ap=xs[:, NT - 1], constant=0.0)
        A.dma(d_x, out=xs[:, :NT - 1], in_=x[:NP * (NT - 1)].rearrange("(t p) d -> p t d", p=NP))
        ready_x = A.dma(d_x, blank, out=xs[:last, NT - 1], in_=x[NP * (NT - 1):])
        src_i, dst_i = early(EJ), early(EJ)
        A.dma(d_edge, out=src_i[:EP].bitcast(I32), in_=src.rearrange("(p j) -> p j", p=EP))
        A.dma(d_edge, out=dst_i[:EP].bitcast(I32), in_=dst.rearrange("(p j) -> p j", p=EP))
        gate_sb = small(4 * E0).rearrange("p (k e) -> p k e", k=4)
        wup_sb, m1_sb, m23_sb, m4_sb, wo_sb = small(2 * MUL), small(128), small(256), small(512), small(512)
        S.dma(d_wts, out=gate_sb, in_=gate)
        S.dma(d_wts, out=wup_sb, in_=w_up)
        S.dma(d_wts, out=m1_sb[:16], in_=w_mlp1)
        S.dma(d_wts, out=m23_sb, in_=w_mlp23)
        S.dma(d_wts, out=m4_sb, in_=w_mlp4)
        ready_wts = S.dma(d_wts, out=wo_sb, in_=w_out)
        T5 = T1 // NP
        ew_sb, ei_sb = small(2 * T5), small(2 * T5)
        d_ew = done("ew")
        S.dma(d_ew, out=ew_sb.rearrange("p (t k) -> p t k", k=2), in_=ew.rearrange("(t p) k -> p t k", p=NP))
        ready_ew = S.dma(d_ew, out=ei_sb.bitcast(I32).rearrange("p (t k) -> p t k", k=2),
                         in_=ei.rearrange("(t p) k -> p t k", p=NP))

        sorted_edges = dram("sorted_edges", [SLOTS, REC])
        m = G("memset", ap=recs, constant=0.0)
        m = G("memset", m, ap=recs[:, :, 1], constant=-1.0)
        d_fill = done("fill")
        filled = G.dma(d_fill, m, out=sorted_edges.rearrange("(p s) c -> p (s c)", p=128),
                       in_=recs.rearrange("p s c -> p (s c)"))
        ws, d_ws0 = dram("pair_rows", [FT * TILE, D]), done("zero_rows")
        zrow = early(D)
        m = G("memset", ap=zrow, constant=0.0)
        zeroed = G.dma(d_ws0, m, out=ws.rearrange("(t p) d -> p t d", p=128),
                       in_=zrow.unsqueeze(1).to_broadcast([128, FT, D]))
        at48 = zone_of(rec_at, NTILE * REC)
        at4, at8 = at48(EJ * 4), at48(EJ * 8)
        A.dma(d_edge, filled, out=at4[:EP], in_=ea4.rearrange("(p j) c -> p (j c)", p=EP))
        ready_edge = A.dma(d_edge, out=at8[:EP], in_=ea8.rearrange("(p j) c -> p (j c)", p=EP))

        def whole(count, least, unit, shift, ends, base, pe, n, tmp):
            c = V("tensor_scalar", pe, out=tmp.bitcast(I32), in0=count, scalar1=float(unit - 1), scalar2=None,
                  op0=ALU.add)
            c = V("tensor_scalar", c, out=tmp.bitcast(I32), in0=tmp.bitcast(I32), scalar1=shift, scalar2=None,
                  op0=ALU.logical_shift_right)
            c = V("tensor_copy", c, out=n, in_=tmp.bitcast(I32))
            c = V("tensor_scalar", c, out=n, in0=n, scalar1=float(least), scalar2=None, op0=ALU.max)
            c = V("tensor_tensor_scan", c, ready_const, out=ends, data0=ones[:, 0:n.shape[-1]], data1=n,
                  initial=0.0, op0=ALU.mult, op1=ALU.add)
            c = V("tensor_tensor", c, out=base, in0=ends, in1=n, op=ALU.subtract)
            return V("tensor_scalar", c, out=base, in0=base, scalar1=float(unit), scalar2=None, op0=ALU.mult)

        er = edges[:EP]
        slot_i = small(EJ)[:EP].bitcast(I32)
        g_same, g_row, g_first = small(NG), small(NG), small(NG)
        known = {}

        def sort_edges():
            dstf, win, slot, ones_row = (early(EJ)[:EP] for _ in range(4))
            seq = [early(EJ)[:EP] for _ in range(2)]
            in_win = carve(NW * EJ // 2, lnT_at + NPAD)[:EP].bitcast(BF16).rearrange("p (w j) -> p w j", w=NW)
            row_tot, n_win, end_win, base_win, tmp_win, start = (small(NW) for _ in range(6))
            start = start[:EP]
            V("memset", ap=ones_row, constant=1.0)
            V("memset", ap=slot, constant=0.0)
            V("tensor_copy", ready_edge, out=er[:, :, 0].bitcast(I32), in_=src_i[:EP].bitcast(I32))
            c = V("tensor_copy", out=dstf, in_=dst_i[:EP].bitcast(I32))
            yield
            c = V("tensor_scalar", c, out=win, in0=dstf, scalar1=float(WN), scalar2=None, op0=ALU.is_ge)
            for w in range(2, NW):
                c = V("scalar_tensor_tensor", c, out=win, in0=dstf, scalar=float(WN * w), in1=win,
                      op0=ALU.is_ge, op1=ALU.add)
                yield
            for w in range(NW):
                c = V("tensor_scalar", c, out=in_win[:, w], in0=win, scalar1=float(w), scalar2=None,
                      op0=ALU.is_equal)
                yield
            c = V("tensor_reduce", c, out=row_tot[:EP], in_=in_win, op=ALU.add, axis=AX.X)
            PE("matmul", c, ready_const, out=banks[0][:EP, 0:NW], lhsT=before[:EP, :EP], rhs=row_tot[:EP],
               start=True, stop=True)
            pe = PE("matmul", out=banks[1][:, 0:NW], lhsT=ones[:EP, :], rhs=row_tot[:EP], start=True, stop=True)
            yield
            whole(banks[1][:, 0:NW], 1, GROUP, GROUP.bit_length() - 1, end_win, base_win, pe, n_win, tmp_win)
            c = V("scalar_tensor_tensor", out=start, in0=banks[0][:EP, 0:NW], scalar=-1.0, in1=base_win[:EP],
                  op0=ALU.add, op1=ALU.add)
            yield
            for w in range(NW):
                V("tensor_tensor_scan", out=seq[w % 2], data0=ones_row, data1=in_win[:, w],
                  initial=start[:, w:w + 1], op0=ALU.mult, op1=ALU.add)
                V("tensor_tensor", out=seq[w % 2], in0=seq[w % 2], in1=in_win[:, w], op=ALU.mult)
                V("tensor_tensor", out=slot, in0=slot, in1=seq[w % 2], op=ALU.add)
                yield
            V("tensor_copy", out=slot_i, in_=slot)
            V("tensor_copy", out=er[:, :, 1], in_=dstf)
            V("memset", ap=er[:, :, 14:16], constant=0.0)
            V("tensor_copy", out=er[:, :, 2:6], in_=at4[:EP].rearrange("p (j c) -> p j c", c=4))
            yield
            known["records"] = V("tensor_copy", out=er[:, :, 6:14], in_=at8[:EP].rearrange("p (j c) -> p j c", c=8))
            yield
            g_win = early(NG)
            cmp = carve(NG * NW, lnT_at + NPAD).rearrange("p (g w) -> p g w", w=NW)
            V("tensor_tensor", out=cmp, in0=K["node"][:, 0:NG].unsqueeze(2).to_broadcast([128, NG, NW]),
              in1=end_win.unsqueeze(1).to_broadcast([128, NG, NW]), op=ALU.is_ge)
            yield
            V("tensor_reduce", out=g_win, in_=cmp, op=ALU.add, axis=AX.X)
            yield
            V("tensor_scalar", out=g_win, in0=g_win, scalar1=float(NW - 1), scalar2=None, op0=ALU.min)
            V("memset", ap=g_same[:, 0:1], constant=0.0)
            V("tensor_tensor", out=g_same[:, 1:], in0=g_win[:, 1:], in1=g_win[:, :NG - 1], op=ALU.is_equal)
            V("tensor_scalar", out=g_first, in0=g_win, scalar1=float(WN), scalar2=None, op0=ALU.mult)
            row_f = cmp.rearrange("p g w -> p (g w)")[:, 0:NG]
            V("tensor_scalar", out=row_f, in0=g_win, scalar1=128.0, scalar2=K["part"], op0=ALU.mult, op1=ALU.add)
            V("scalar_tensor_tensor", out=row_f[:, :NG - 1], in0=g_same[:, 1:], scalar=BIG,
              in1=row_f[:, :NG - 1], op0=ALU.mult, op1=ALU.add)
            known["groups"] = V("tensor_copy", out=g_row.bitcast(I32), in_=row_f)
            yield

        edge_sort = sort_edges()

        def advance(n):
            for _ in range(n):
                next(edge_sort, None)

        d_scatter = done("scatter")
        left = list(range(EJ))

        def scatter_edges(n):
            for _ in range(min(n, len(left))):
                j = left.pop(0)
                G.dma(d_scatter, known["records"], filled, out=sorted_edges,
                      out_offset=bass.IndirectOffsetOnAxis(ap=slot_i[:, j:j + 1], axis=0),
                      in_=er[:, j, :], in_offset=None)

        stats, mv, rstd, eps_v, nt_ = small(6 * 2), small(2 * NT), small(NT), small(NT), small(NT)

        def layer_norm(ready, tiles=NT):
            q = mv.rearrange("p (t c) -> p t c", c=2)
            for t in range(tiles):
                st = stats[:, 6 * (t % 2):6 * (t % 2) + 6]
                V("bn_stats", ready, out=st, in_=xs[:, t])
                V("bn_aggr", out=q[:, t], in_=st)
            c = V("tensor_scalar", out=eps_v[:, :tiles], in0=q[:, :tiles, 1], scalar1=1e-5, scalar2=None,
                  op0=ALU.add)
            a = A("activation", c, out=nt_[:, :tiles], in_=eps_v[:, :tiles], func=ACT.Sqrt)
            V("reciprocal", a, out=rstd[:, :tiles], in_=nt_[:, :tiles])
            V("tensor_tensor", out=nt_[:, :tiles], in0=rstd[:, :tiles], in1=rstd[:, :tiles], op=ALU.mult)
            V("tensor_tensor", out=nt_[:, :tiles], in0=nt_[:, :tiles], in1=eps_v[:, :tiles], op=ALU.mult)
            V("tensor_scalar", out=nt_[:, :tiles], in0=nt_[:, :tiles], scalar1=-0.5, scalar2=1.5, op0=ALU.mult,
              op1=ALU.add)
            V("tensor_tensor", out=rstd[:, :tiles], in0=nt_[:, :tiles], in1=rstd[:, :tiles], op=ALU.mult)
            return [V("tensor_scalar", out=ln[:, t], in0=xs[:, t], scalar1=q[:, t, 0:1],
                      scalar2=rstd[:, t:t + 1], op0=ALU.subtract, op1=ALU.mult) for t in range(tiles)]

        def transpose_ln(each, tiles=NT):
            copied = [None, None]
            for t in range(tiles):
                bank = banks[t % 2]
                for k in range(4):
                    tr = PE("transpose", each[t], *some(copied[t % 2]), out=bank[:, k * 128:(k + 1) * 128],
                            in_=ln[:, t, k * 128:(k + 1) * 128], identity=ident)
                copied[t % 2] = A("activation", tr, out=lnT[:, :, t * NP:(t + 1) * NP],
                                  in_=bank[:, :].rearrange("p (k n) -> p k n", k=4), func=ACT.Copy)
            return A.last

        stage("segment")
        ancf = small(TOP)
        lo_p, hi_p, t7 = small(1), small(1), small(TOP)
        V("tensor_copy", ready_tree, ready_const, out=ancf, in_=anc_i.bitcast(I32))
        V("tensor_scalar", out=t7, in0=K["left"], scalar1=-BIG, scalar2=None, op0=ALU.mult)
        V("tensor_tensor", out=anc_i, in0=ancf, in1=K["right"], op=ALU.mult)
        V("tensor_tensor", out=t7, in0=t7, in1=anc_i, op=ALU.add)
        V("tensor_reduce", out=lo_p, in_=t7, op=ALU.max, axis=AX.X)
        V("tensor_tensor", out=anc_i, in0=ancf, in1=K["left"], op=ALU.mult)
        V("scalar_tensor_tensor", out=t7, in0=K["right"], scalar=BIG, in1=anc_i, op0=ALU.mult, op1=ALU.add)
        V("tensor_reduce", out=hi_p, in_=t7, op=ALU.min, axis=AX.X)
        find = zone_of(zone, NT * NPAD)
        in_sub, lowq = find(NPAD), find(NPAD)
        V("tensor_scalar", out=lowq, in0=K["node"], scalar1=lo_p, scalar2=None, op0=ALU.is_ge)
        in_sub_done = V("scalar_tensor_tensor", out=in_sub, in0=K["node"], scalar=hi_p, in1=lowq,
                        op0=ALU.is_lt, op1=ALU.mult)
        subf = find(LEAVES - 1)
        V("tensor_copy", out=subf, in_=sub_i.bitcast(I32))
        low, high = [find(LEAVES) for _ in range(2)], [find(LEAVES) for _ in range(2)]
        V("tensor_copy", out=low[0][:, 0:1], in_=lo_p)
        V("tensor_copy", out=high[0][:, 0:1], in_=hi_p)
        for lv in range(SEARCH_LEVELS - TOP):
            n = 2 ** lv
            a, b = lv % 2, 1 - lv % 2
            v = subf[:, n - 1:2 * n - 1]
            nl, nh = (z[b][:, 0:2 * n].rearrange("p (n s) -> p n s", s=2) for z in (low, high))
            V("tensor_copy", out=nl[:, :, 0], in_=low[a][:, 0:n])
            V("tensor_tensor", out=nl[:, :, 1], in0=low[a][:, 0:n], in1=v, op=ALU.max)
            V("tensor_tensor", out=nh[:, :, 0], in0=high[a][:, 0:n], in1=v, op=ALU.min)
            V("tensor_copy", out=nh[:, :, 1], in_=high[a][:, 0:n])
        f = (SEARCH_LEVELS - TOP) % 2
        key = find(LEAVES)
        V("tensor_tensor", out=key, in0=low[f], in1=high[f], op=ALU.is_ge)
        key_done = V("scalar_tensor_tensor", out=key, in0=key, scalar=2 * BIG, in1=low[f], op0=ALU.mult,
                     op1=ALU.add)
        for t in range(NT):
            first_leaf = PE("matmul", in_sub_done, out=banks[2][:, t:t + 1], lhsT=in_sub[:, t * NP:(t + 1) * NP],
                            rhs=K["sub512"], start=True, stop=True)
        leaf = small(NT)
        hit = [find(LEAVES) for _ in range(2)]
        reads = []
        for t in range(NT):
            b = banks[3 + t % 3]
            k = PE("matmul", key_done, *(reads[-3:-2] if t >= 3 else []), out=b[:, :],
                   lhsT=in_sub[:, t * NP:(t + 1) * NP], rhs=key, start=True, stop=True)
            reads.append(V("scalar_tensor_tensor", k, out=hit[t % 2], in0=b[:, :],
                           scalar=K["node_col"][:, t:t + 1], in1=K["leaf1"], op0=ALU.is_le, op1=ALU.mult))
            V("tensor_reduce", out=leaf[:, t:t + 1], in_=hit[t % 2], op=ALU.max, axis=AX.X)
        leaf_i = small(NT).bitcast(I32)
        c = V("scalar_tensor_tensor", first_leaf, out=leaf_i, in0=banks[2][:, 0:NT], scalar=-1.0, in1=leaf,
              op0=ALU.add, op1=ALU.add)
        leaf_known = c
        d_leaf = done("leaf")
        found = small(4 * NT).bitcast(I32).rearrange("p (t c) -> p t c", c=4)
        for t in range(NT):
            got = G.dma(d_leaf, leaf_known, out=found[:, t], out_offset=None, in_=leaf_table,
                        in_offset=bass.IndirectOffsetOnAxis(ap=leaf_i[:, t:t + 1], axis=0))
        normed = layer_norm(ready_x)
        f4 = small(4 * NT).rearrange("p (t c) -> p t c", c=4)
        c = V("tensor_copy", got, out=f4, in_=found)
        diag = [find(NP) for _ in range(NT)]
        place = [(banks[(6, 7, 2)[t // 4]], (t % 4) * 128) for t in range(NT)]
        for t in range(NT):
            dg = V("tensor_scalar", out=diag[t], in0=ident, scalar1=f4[:, t, 1:2], scalar2=None, op0=ALU.mult)
            sr = PE("matmul", dg, leaf_known, out=place[t][0][:, place[t][1]:place[t][1] + NP], lhsT=ones,
                    rhs=diag[t], start=True, stop=True)
        rcnt = small(NT)
        V("tensor_tensor", out=rcnt, in0=f4[:, :, 3], in1=f4[:, :, 2], op=ALU.subtract)
        V("tensor_scalar", out=rcnt, in0=rcnt, scalar1=1.0, scalar2=None, op0=ALU.add)
        V("reciprocal", out=rcnt, in_=rcnt)
        seg_row = carve(NPAD, lnT_at)
        for t in range(0, NT, 4):
            n = min(4, NT - t) * NP
            V("tensor_copy", sr, out=seg_row[:, t * NP:t * NP + n], in_=place[t][0][:, 0:n])
        member = carve(NT * NPAD, zone).rearrange("p (t q) -> p t q", t=NT)
        mem = [V("tensor_scalar", out=member[:, t], in0=seg_row, scalar1=f4[:, t, 0:1], scalar2=None,
                 op0=ALU.is_equal) for t in range(NT)]
        advance(4)
        for t in range(NT):
            b, r = banks[3 + t % 3], rows(t)
            for k in range(NT):
                c = PE("matmul", mem[k], normed[k], *some(reads[-3] if t >= 3 else reads[-1]), out=b[:r, :],
                       lhsT=member[:rows(k), k, t * NP:t * NP + r], rhs=ln[:rows(k), k], start=k == 0,
                       stop=k == NT - 1)
            reads.append(V("scalar_tensor_tensor", c, out=xs[:r, t], in0=b[:r, :], scalar=rcnt[:r, t:t + 1],
                           in1=xs[:r, t], op0=ALU.mult, op1=ALU.add))
            if t < NT - 1:
                advance(9)
        segment_read = PE.last
        advance(1000)

        stage("route")
        normed = layer_norm(V.last)
        lnT_done = transpose_ln(normed)
        for t in range(NT):
            for k in range(4):
                c = PE("matmul", lnT_done, ready_wts, out=banks[2][:, t * E0:(t + 1) * E0],
                       lhsT=lnT[:, k, t * NP:(t + 1) * NP], rhs=gate_sb[:, k], start=k == 0, stop=k == 3)
        pair_tmp = zone_of(zone + NT * NPAD, 1000)
        logit, cand, pick1, pick2, both, rank = (pair_tmp(NT * E0).rearrange("p (t e) -> p t e", e=E0)
                                                 for _ in range(6))
        eid = K["node"][:, 0:E0].unsqueeze(1).to_broadcast([128, NT, E0])
        top1, top2, first = small(NT), small(NT), small(NT)

        def wide(v):
            return v.unsqueeze(2).to_broadcast([128, NT, E0])

        V("tensor_copy", c, out=logit, in_=banks[2][:, 0:NT * E0].rearrange("p (t e) -> p t e", e=E0))
        for best, pick in ((top1, pick1), (top2, pick2)):
            V("tensor_reduce", out=best, in_=logit, op=ALU.max, axis=AX.X)
            V("tensor_tensor", out=cand, in0=logit, in1=wide(best), op=ALU.is_lt)
            V("scalar_tensor_tensor", out=cand, in0=cand, scalar=float(E0), in1=eid, op0=ALU.mult, op1=ALU.add)
            V("tensor_reduce", out=first, in_=cand, op=ALU.min, axis=AX.X)
            V("tensor_tensor", out=pick, in0=eid, in1=wide(first), op=ALU.is_equal)
            V("scalar_tensor_tensor", out=logit, in0=pick, scalar=-1e30, in1=logit, op0=ALU.mult, op1=ALU.add)
        V("tensor_tensor", out=both, in0=pick1, in1=pick2, op=ALU.add)
        picked = V("tensor_tensor", out=both, in0=both, in1=wide(K["valid"]), op=ALU.mult)
        for t in range(NT):
            for k in range(t + 1):
                PE.quiet("matmul", picked, out=banks[6][:, t * E0:(t + 1) * E0],
                         lhsT=before if k == t else ones, rhs=both[:, k], start=k == 0, stop=k == t)
        for k in range(NT):
            c = PE("matmul", out=banks[7][:, 0:E0], lhsT=ones, rhs=both[:, k], start=k == 0, stop=k == NT - 1)
        n_t, end_t, base_t, tmp_t = small(E0), small(E0), small(E0), small(E0)
        whole(banks[7][:, 0:E0], 0, TILE, TILE.bit_length() - 1, end_t, base_t, c, n_t, tmp_t)
        V("tensor_tensor", out=rank, in0=banks[6][:, 0:NT * E0].rearrange("p (t e) -> p t e", e=E0),
          in1=base_t.unsqueeze(1).to_broadcast([128, NT, E0]), op=ALU.add)
        pair_i = [small(NT).bitcast(I32) for _ in range(2)]
        for pick, place_i in ((pick1, pair_i[0]), (pick2, pair_i[1])):
            V("tensor_tensor", out=cand, in0=rank, in1=pick, op=ALU.mult)
            V("tensor_reduce", out=first, in_=cand, op=ALU.add, axis=AX.X)
            pairs_known = V("tensor_copy", out=place_i, in_=first)
        te = small(FT)
        cmp = pair_tmp(FT * E0).rearrange("p (g e) -> p g e", e=E0)
        V("tensor_tensor", out=cmp, in0=K["node"][:, 0:FT].unsqueeze(2).to_broadcast([128, FT, E0]),
          in1=end_t.unsqueeze(1).to_broadcast([128, FT, E0]), op=ALU.is_ge)
        V("tensor_reduce", out=te, in_=cmp, op=ALU.add, axis=AX.X)
        V("tensor_scalar", out=te, in0=te, scalar1=float(E0 - 1), scalar2=None, op0=ALU.min)
        t_same = cmp.rearrange("p g e -> p (g e)")[:, 0:FT]
        V("memset", ap=t_same[:, 0:1], constant=0.0)
        V("tensor_tensor", out=t_same[:, 1:], in0=te[:, 1:], in1=te[:, :FT - 1], op=ALU.is_equal)
        V("tensor_scalar", out=te, in0=te, scalar1=128.0, scalar2=K["part"], op0=ALU.mult, op1=ALU.add)
        V("scalar_tensor_tensor", out=te, in0=t_same, scalar=float(SKIP), in1=te, op0=ALU.mult, op1=ALU.add)
        w_row = small(HB * FT).bitcast(I32).rearrange("p (b t) -> p b t", b=HB)
        for b in range(HB):
            tiles_known = V("tensor_scalar", out=w_row[:, b], in0=te, scalar1=float(b * E0 * 128), scalar2=None,
                            op0=ALU.add)
        wt = [small(NT), small(NT)]
        c = V("tensor_tensor", out=first, in0=top2, in1=top1, op=ALU.subtract)
        a = A("activation", c, out=top2, in_=first, func=ACT.Exp)
        V("tensor_scalar", a, out=first, in0=top2, scalar1=1.0, scalar2=None, op0=ALU.add)
        V("reciprocal", out=wt[0], in_=first)
        route_done = weights_known = V("tensor_tensor", out=wt[1], in0=wt[0], in1=top2, op=ALU.mult)

        stage("expert", chained=False)
        d_pair = done("pair")
        wz = zone_of(zone, ZONE)
        up = [wz(4096).rearrange("p (k c h) -> p k c h", k=4, c=2) for b in range(HB)]
        down = [wz(2048).rearrange("p (k d) -> p k d", k=4) for b in range(HB)]
        d_up = [done(f"up{b}") for b in range(HB)]
        d_dn = [done(f"down{b}") for b in range(HB)]
        up_read, dn_read = [segment_read] * HB, [route_done] * HB
        up_in, dn_in = [None] * HB, [None] * HB

        def load_weights(i):
            for b in range(HB):
                up_in[b] = G.dma(d_up[b], tiles_known, up_read[b], out=up[b].rearrange("p k c h -> p (k c h)"),
                                 out_offset=None, in_=w13,
                                 in_offset=bass.IndirectOffsetOnAxis(ap=w_row[:, b, i:i + 1], axis=0),
                                 bounds_check=HB * E0 * 128 - 1, oob_is_err=False)
            for b in range(HB):
                dn_in[b] = G.dma(d_dn[b], dn_read[b], zeroed, out=down[b].rearrange("p k d -> p (k d)"),
                                 out_offset=None, in_=w2,
                                 in_offset=bass.IndirectOffsetOnAxis(ap=w_row[:, b, i:i + 1], axis=0),
                                 bounds_check=HB * E0 * 128 - 1, oob_is_err=False)

        for t in range(NT):
            for kk in range(2):
                r = rows(t)
                rows_sent = G.dma(d_pair, pairs_known, normed[t], zeroed, out=ws,
                                  out_offset=bass.IndirectOffsetOnAxis(ap=pair_i[kk][:r, t:t + 1], axis=0),
                                  in_=ln[:r, t], in_offset=None)
        load_weights(0)
        buf = zone_of(ln_at, NT * D + 4 * NPAD)
        xin, xT, sil = ([buf(512) for _ in range(2)] for _ in range(3))
        hid, hT, yo = buf(1536), [buf(1536) for _ in range(2)], [buf(512) for _ in range(2)]
        d_in = [done(f"in{i}") for i in range(2)]
        d_out = [done(f"rows{i}") for i in range(2)]
        ys = dram("pair_out", [FT * TILE, D])
        xin_free, xT_free, sil_free, up_free = [None] * 2, [None] * 2, [None] * 2, [None] * 2
        hT_free, yo_free = [None] * 2, [None] * 2
        tr_free = {0: None, 1: None, 6: None}
        hid_free, y_read = [None] * HB, None
        came, xt = {}, {}

        def load_rows(i):
            came[i] = S.dma(d_in[i % 2], rows_sent, picked, lnT_done, *some(xin_free[i % 2]), out=xin[i % 2],
                            in_=ws[i * TILE:(i + 1) * TILE])

        def turn_rows(i):
            s = i % 2
            for k in range(4):
                tr = PE("transpose", came[i], *some(tr_free[0]), out=banks[0][:, k * 128:(k + 1) * 128],
                        in_=xin[s][:, k * 128:(k + 1) * 128], identity=ident)
            xin_free[s] = tr
            tr_free[0] = xt[i] = A("activation", tr, *some(xT_free[s]), out=xT[s], in_=banks[0][:, :],
                                   func=ACT.Copy)

        def turn_hidden(i, b):
            bank = (6, 1)[b % 2]
            for k in range(4):
                o = (b * 4 + k) * 128
                tr = PE("transpose", h_made[b], *some(tr_free[bank]), out=banks[bank][:, k * 128:(k + 1) * 128],
                        in_=hid[:, o:o + 128], identity=ident)
            hid_free[b] = tr
            tr_free[bank] = h_turned[b] = A("activation", tr, *some(hT_free[i % 2]),
                                            out=hT[i % 2][:, b * 512:(b + 1) * 512], in_=banks[bank][:, :],
                                            func=ACT.Copy)

        def project_up(i, b):
            q = b % 2
            for cc in range(2):
                bank = banks[2 + 2 * q + cc]
                for k in range(4):
                    mm = PE("matmul", xt[i], up_in[b], *some(up_free[q]), out=bank[:, :],
                            lhsT=xT[i % 2][:, k * 128:(k + 1) * 128], rhs=up[b][:, k, cc], start=k == 0,
                            stop=k == 3)
                if cc == 0:
                    sl = A("activation", mm, *some(sil_free[q]), out=sil[q], in_=bank[:, :], func=ACT.Silu)
            up_read[b] = xT_free[i % 2] = mm
            sil_free[q] = up_free[q] = h_made[b] = V(
                "tensor_tensor", mm, sl, *some(hid_free[b]), out=hid[:, b * 512:(b + 1) * 512], in0=bank[:, :],
                in1=sil[q], op=ALU.mult)

        def project_down(i, b):
            for k in range(4):
                mm = PE("matmul", h_turned[b], dn_in[b], *some(y_read), out=banks[7][:, :],
                        lhsT=hT[i % 2][:, (b * 4 + k) * 128:(b * 4 + k + 1) * 128], rhs=down[b][:, k],
                        start=b + k == 0, stop=b == HB - 1 and k == 3)
            dn_read[b] = hT_free[i % 2] = mm
            return mm

        load_rows(0)
        load_rows(1)
        turn_rows(0)
        for i in range(FT):
            h_made, h_turned = [None] * HB, [None] * HB
            project_up(i, 0)
            project_up(i, 1)
            turn_hidden(i, 0)
            project_up(i, 2)
            turn_hidden(i, 1)
            if i + 1 < FT:
                turn_rows(i + 1)
            project_down(i, 0)
            turn_hidden(i, 2)
            project_down(i, 1)
            mm = project_down(i, 2)
            y_read = V("tensor_copy", mm, *some(yo_free[i % 2]), out=yo[i % 2], in_=banks[7][:, :])
            yo_free[i % 2] = S.dma(d_out[i % 2], y_read, out=ys[i * TILE:(i + 1) * TILE], in_=yo[i % 2])
            if i + 2 < FT:
                load_rows(i + 2)
            if i + 1 < FT:
                load_weights(i + 1)
            scatter_edges(13)
        scatter_edges(EJ)
        scattered = (d_scatter.sem, d_scatter.count)
        experts_read = mm
        yz = zone_of(zone, ZONE)
        yg = [yz(512) for i in range(2 * NT)]
        d_yg = [done(f"pick{i}") for i in range(4)]
        yg_in = []
        for t in range(NT):
            for kk in range(2):
                i, r = 2 * t + kk, rows(t)
                yg_in.append(G.dma(d_yg[i % 4], *yo_free, experts_read, *(yg_in[i - 4:i - 3] if i >= 4 else []),
                                   out=yg[i][:r], out_offset=None, in_=ys,
                                   in_offset=bass.IndirectOffsetOnAxis(ap=pair_i[kk][:r, t:t + 1], axis=0)))
                V("scalar_tensor_tensor", yg_in[i], weights_known, V.last, out=xs[:r, t], in0=yg[i][:r],
                  scalar=wt[kk][:r, t:t + 1], in1=xs[:r, t], op0=ALU.mult, op1=ALU.add)

        stage("node")
        e_w = [carve(2048, edge_at + 2048 * i) for i in range(2)]
        d_second = [done(f"w_second{i}") for i in range(2)]

        def load_second(e, *free):
            S.dma(d_second[e % 2], *free, out=e_w[e % 2][:, 0:1024], in_=v1[e])
            return S.dma(d_second[e % 2], *free, out=e_w[e % 2][:, 1024:2048], in_=v2[e])

        second_in = [load_second(e, scattered) for e in range(2)]
        d_rec = done("records")
        recs_in = S.dma(d_rec, scattered, out=recs, in_=sorted_edges.rearrange("(s p) c -> p s c", p=128))
        normed = layer_norm(V.last)
        table = dram("node_table", [N, 4 * MUL])
        d_tab = [done(f"table{i}") for i in range(2)]
        nz = zone_of(zone + 12000, ZONE - 12000)
        nT = [nz(512) for _ in range(2)]
        table_rows = [nz(512) for _ in range(2)]
        copied, sent, nT_free, rows_made = [None] * 2, [None] * 2, [None] * 2, [None] * 2
        for t in range(NT):
            s, r = t % 2, rows(t)
            for k in range(4):
                piece = (ln[:, t, 0:MUL] if k == 0 else
                         ln[:, t, MUL:].rearrange("p (u m) -> p m u", m=3)[:, k - 1])
                tr = PE("transpose", normed[t], *some(copied[s]), out=banks[s][:, k * 128:(k + 1) * 128], in_=piece,
                        identity=ident)
            copied[s] = A("activation", tr, *some(nT_free[s]), out=nT[s], in_=banks[s][:, :], func=ACT.Copy)
            for k in range(4):
                mm = PE("matmul", copied[s], *some(rows_made[s]), out=banks[2 + s][:, k * 128:(k + 1) * 128],
                        lhsT=nT[s][:, k * 128:(k + 1) * 128],
                        rhs=wup_sb[:, 0:MUL] if k == 0 else wup_sb[:, MUL:2 * MUL], start=True, stop=True)
            nT_free[s] = mm
            rows_made[s] = V("tensor_scalar", mm, *some(sent[s]), out=table_rows[s], in0=banks[2 + s][:, :],
                             scalar1=MUL ** -0.5, scalar2=None, op0=ALU.mult)
            sent[s] = S.dma(d_tab[s], rows_made[s], out=table[t * NP:t * NP + r], in_=table_rows[s][:r])
        table_in = list(sent)

        senders = carve(NTILE, lnT_at + NB * 64).bitcast(I32)
        V("tensor_copy", recs_in, out=senders, in_=recs[:, :, 0].bitcast(I32))
        rv = recs.rearrange("p (g s) c -> p g s c", g=NG)
        rel = V("tensor_tensor", known["groups"], out=rv[:, :, :, 1], in0=rv[:, :, :, 1],
                in1=g_first.unsqueeze(2).to_broadcast([128, NG, GT]), op=ALU.subtract)
        feat = carve(NB * 64, lnT_at).rearrange("p (r k h c) -> p r k h c", r=NB, k=4, h=2)
        for h in range(2):
            packed = V("tensor_copy", out=feat[:, :, :, h],
                       in_=recs.rearrange("p (r h k) c -> p r h k c", r=NB, h=2)[:, :, h, :, 6:14])
        node_done = [V.last, PE.last, A.last] + table_in

        stage("edge", chained=False)
        NGAT, NM = 8, 3
        ring = zone_of(zone, ZONE)
        gat = [ring(512) for _ in range(NGAT)]
        d_gat = [done(f"gather{i}") for i in range(NGAT)]
        picks = [ring(4 * WN).rearrange("p (c n) -> p c n", c=4) for _ in range(NM)]
        msg_a = [ring(2 * MUL) for _ in range(NM)]
        msg_b = [ring(6 * MUL) for _ in range(NM)]
        run_sum = [ring(8 * WN) for _ in range(2)]
        act1, act2, act3, fT = ring(512), ring(512), [ring(512) for _ in range(2)], ring(512)
        sums = dram("sums", [NW * 128, 8 * WN])
        d_sum = [done(f"sum{i}") for i in range(2)]
        sum_zero = V("memset", *node_done, ap=run_sum[1], constant=0.0)
        gat_free, gat_in = [None] * NGAT, {}

        def gather(i):
            s = i % NGAT
            gat_in[i] = G.dma(d_gat[s], *node_done, *some(gat_free[s]), out=gat[s], out_offset=None,
                              in_=table, in_offset=bass.IndirectOffsetOnAxis(ap=senders[:, i:i + 1], axis=0))

        free = dict(bank=None, fT=None, act1=None, act2=None)
        act3_free, mlp_out = [None] * 2, {}

        def mlp_step(r, step):
            b7 = banks[7]
            if step == 0:
                for k in range(4):
                    tr = PE("transpose", packed, *node_done, *some(free["bank"]),
                            out=b7[:16, k * 128:(k + 1) * 128], in_=feat[:, r, k].rearrange("p h c -> p (h c)"),
                            identity=ident)
                free["bank"] = mlp_out[0] = A("activation", tr, *some(free["fT"]), out=fT[:16], in_=b7[:16, :],
                                              func=ACT.Copy)
            elif step == 1:
                mm = free["fT"] = PE("matmul", mlp_out[0], out=b7[:, :], lhsT=m1_sb[:16], rhs=fT[:16], start=True,
                                     stop=True)
                free["bank"] = mlp_out[1] = A("activation", mm, *some(free["act1"]), out=act1, in_=b7[:, :],
                                              func=ACT.Silu, scale=8 ** -0.5)
            elif step == 2:
                mm = free["act1"] = PE("matmul", mlp_out[1], out=b7[:, :], lhsT=m23_sb[:, 0:128], rhs=act1,
                                       start=True, stop=True)
                free["bank"] = mlp_out[2] = A("activation", mm, *some(free["act2"]), out=act2, in_=b7[:, :],
                                              func=ACT.Silu, scale=SILU_2MOM / 8)
            else:
                mm = free["act2"] = PE("matmul", mlp_out[2], out=b7[:, :], lhsT=m23_sb[:, 128:256], rhs=act2,
                                       start=True, stop=True)
                free["bank"] = mlp_out[3, r] = A("activation", mm, *some(act3_free[r % 2]), out=act3[r % 2],
                                                 in_=b7[:, :], func=ACT.Silu, scale=SILU_2MOM / 8)

        tp_free, tp_in = [None] * 3, {}

        def weights_of(i):
            batch, half, k = i // BT, (i // 4) % 2, i % 4
            p = slice(64 * half, 64 * half + 64)
            tp_in[i] = PE("matmul", mlp_out[3, batch], *some(tp_free[i % 3]), out=banks[4 + i % 3][:, :],
                          lhsT=act3[batch % 2][p, k * 128:(k + 1) * 128], rhs=m4_sb[p, :], start=True, stop=True)
            if i % BT == BT - 1:
                act3_free[batch % 2] = tp_in[i]

        tile_free = [None] * NM
        bank_free, sum_free, sum_made = [None] * 2, [None] * 2, [None, sum_zero]
        group_end = {}

        def close_group(g):
            b = g % 2
            sum_made[b] = bank_free[b] = V(
                "scalar_tensor_tensor", group_end[g], sum_made[1 - b], *some(sum_free[b]), out=run_sum[b],
                in0=run_sum[1 - b], scalar=g_same[:, g:g + 1], in1=banks[b][:, :], op0=ALU.mult, op1=ALU.add)
            sum_free[b] = G.dma(d_sum[b], sum_made[b], out=sums,
                                out_offset=bass.IndirectOffsetOnAxis(ap=g_row[:, g:g + 1].bitcast(I32), axis=0),
                                in_=run_sum[b], in_offset=None, bounds_check=NW * 128 - 1, oob_is_err=False)

        for step in range(4):
            mlp_step(0, step)
        for i in range(NGAT):
            gather(i)
        weights_of(0)
        weights_of(1)
        for i in range(NTILE):
            g, k, s, gs = i // GT, i % GT, i % NM, i % NGAT
            for c in range(4):
                V("tensor_scalar", *node_done, *some(tile_free[s]), out=picks[s][:, c], in0=K["node"][:, 0:WN],
                  scalar1=recs[:, i, 1:2], scalar2=recs[:, i, 2 + c:3 + c], op0=ALU.is_equal, op1=ALU.mult)
            tp = banks[4 + i % 3][:, :].rearrange("p (w u) -> p w u", w=4)
            s0 = gat[gs][:, 0:MUL].unsqueeze(1).to_broadcast([128, 2, MUL])
            s1 = gat[gs][:, MUL:].rearrange("p (m u) -> p m u", m=3)
            V("tensor_tensor", tp_in[i], gat_in[i], out=msg_a[s].rearrange("p (w u) -> p w u", w=2),
              in0=tp[:, 0:2], in1=s0, op=ALU.mult)
            made = V("tensor_tensor", out=msg_b[s].rearrange("p (w m u) -> p w m u", w=2, m=3),
                     in0=tp[:, 2:4].unsqueeze(2).to_broadcast([128, 2, 3, MUL]),
                     in1=s1.unsqueeze(1).to_broadcast([128, 2, 3, MUL]), op=ALU.mult)
            tp_free[i % 3] = gat_free[gs] = made
            if k == 0 and g > 0:
                close_group(g - 1)
            if i + NGAT < NTILE:
                gather(i + NGAT)
            if i + 2 < NTILE:
                weights_of(i + 2)
            if i % BT < 4 and i // BT + 1 < NB:
                mlp_step(i // BT + 1, i % BT)
            bank, wait = banks[g % 2], some(bank_free[g % 2]) if k == 0 else []

            def add(cols, msg, pick, first=False, last=False):
                return PE("matmul", made, *wait, out=bank[:, cols * WN:(cols + pick.shape[-1] // WN) * WN], lhsT=msg,
                          rhs=pick, start=first, stop=last, skip_group_check=True)

            y0 = picks[s][:, 0]
            add(0, msg_a[s][:, 0:MUL], y0, first=k == 0, last=k == GT - 1)
            for m in range(3):
                add(1 + m, msg_b[s][:, m * MUL:(m + 1) * MUL], y0, last=k == GT - 1)
            for m in range(3):
                add(4, msg_b[s][:, (3 + m) * MUL:(4 + m) * MUL], picks[s][:, 1 + m], last=k == GT - 1 and m == 2)
            tile_free[s] = group_end[g] = add(5, msg_a[s][:, MUL:], picks[s][:, 1:4].rearrange("p c n -> p (c n)"),
                                              last=k == GT - 1)
        close_group(NG - 1)

        stage("out")
        p4 = A("activation", ready_wts, out=wo_sb[:, MUL:2 * MUL], in_=wo_sb[:, MUL:2 * MUL], func=ACT.Copy,
               scale=3 ** -0.5)
        sums_in = [carve(8 * WN, ln_at + 8 * WN * i) for i in range(6)]
        d_sin = [done(f"sums_in{i}") for i in range(6)]
        sin_free, o_free = [None] * 6, [None] * 2
        after_edges = [PE.last, V.last] + some(group_end[NG - 1], made, *sum_free)
        after_edges = [group_end[NG - 1], made, *sum_free]
        out_scale = (SILU_2MOM / 8) / 16 / 10
        for t in range(NT):
            s = t % 2
            bank = banks[4 + s]
            for h in range(2):
                w = 2 * t + h
                q = w % 6
                inn = S.dma(d_sin[q], *after_edges, *some(sin_free[q]), out=sums_in[q],
                            in_=sums[w * 128:(w + 1) * 128])
                for k in range(4):
                    for n, blk in enumerate((0, 4) if k == 0 else (4 + k, k)):
                        o = (256 if k else 0) + n * MUL
                        mm = PE("matmul", inn, p4, *some(o_free[s]),
                                out=bank[64 * h:64 * h + WN, k * 128:(k + 1) * 128],
                                lhsT=sums_in[q][:, blk * WN:(blk + 1) * WN], rhs=wo_sb[:, o:o + MUL],
                                start=n == 0, stop=n == 1)
                sin_free[q] = mm
            r = rows(t)
            V("scalar_tensor_tensor", mm, out=xs[:r, t, 0:MUL], in0=bank[:r, 0:MUL], scalar=out_scale,
              in1=xs[:r, t, 0:MUL], op0=ALU.mult, op1=ALU.add)
            xv = xs[:r, t, MUL:].rearrange("p (u m) -> p m u", m=3)
            o_free[s] = V("scalar_tensor_tensor", out=xv, in0=bank[:r, MUL:].rearrange("p (m u) -> p m u", m=3),
                          scalar=out_scale, in1=xv, op0=ALU.mult, op1=ALU.add)

        stage("second")
        d_store = done("store")
        S.dma(d_store, o_free[1], out=out[T5 * NP:NP * (NT - 1)].rearrange("(t p) d -> p t d", p=NP),
              in_=xs[:, T5:NT - 1])
        S.dma(d_store, o_free[1], out=out[NP * (NT - 1):], in_=xs[:last, NT - 1])
        normed = layer_norm(V.last, T5)
        lnT_done = transpose_ln(normed, T5)
        sz = zone_of(zone, ZONE)
        hidT = [sz(1024).rearrange("p (h n) -> p h n", h=2) for i in range(2)]
        V("tensor_copy", ready_ew, out=ei_sb, in_=ei_sb.bitcast(I32))
        co = sz(E1 * T5).rearrange("p (e t) -> p e t", e=E1)
        cw = sz(2 * T5).rearrange("p (t k) -> p t k", k=2)
        for e in range(E1):
            V("scalar_tensor_tensor", out=cw, in0=ei_sb.rearrange("p (t k) -> p t k", k=2), scalar=float(e),
              in1=ew_sb.rearrange("p (t k) -> p t k", k=2), op0=ALU.is_equal, op1=ALU.mult)
            coef = V("tensor_reduce", out=co[:, e], in_=cw, op=ALU.add, axis=AX.X)
        hid_free, yb_free, hb_free = [None] * 2, [None] * 2, [None] * 2
        n_y = 0
        for e in range(E1):
            s = e % 2
            a1 = e_w[s][:, 0:1024].rearrange("p (k h) -> p k h", k=4)
            a2 = e_w[s][:, 1024:2048].rearrange("p (k d) -> p k d", k=2)
            for h in range(2):
                bank = banks[2 + h]
                for k in range(4):
                    mm = PE("matmul", lnT_done, second_in[e], *some(hb_free[h]), out=bank[:, :],
                            lhsT=a1[:, k, h * 128:(h + 1) * 128], rhs=lnT[:, k, 0:T1], start=k == 0, stop=k == 3)
                hb_free[h] = A("activation", mm, *some(hid_free[s]), out=hidT[s][:, h], in_=bank[:, :],
                               func=ACT.Gelu)
            for t in range(T5):
                bank = banks[4 + n_y % 2]
                for k in range(2):
                    mm = PE("matmul", hb_free[0], hb_free[1], *some(yb_free[n_y % 2]), out=bank[:, :],
                            lhsT=hidT[s][:, k, t * NP:(t + 1) * NP], rhs=a2[:, k], start=k == 0, stop=k == 1)
                yb_free[n_y % 2] = V("scalar_tensor_tensor", mm, coef, out=xs[:, t], in0=bank[:, :],
                                     scalar=co[:, e, t:t + 1], in1=xs[:, t], op0=ALU.mult, op1=ALU.add)
                n_y += 1
            hid_free[s] = mm
            if e + 2 < E1:
                second_in.append(load_second(e + 2, mm))
        stored = S.dma(d_store, V.last, out=out[0:T5 * NP].rearrange("(t p) d -> p t d", p=NP), in_=xs[:, 0:T5])
        S.wait([stored, (d_pair.sem, d_pair.count), *sum_free, *sent, *yo_free, filled, zeroed, scattered])

        block = ctx.enter_context(nc.Block())
        for lane, where in ((PE, block.tensor), (V, block.vector), (A, block.scalar), (G, block.gpsimd),
                            (S, block.sync)):
            where(lane.run)


def kernel(**inputs):
    import concourse.bacc as bacc
    from concourse.bass_utils import run_bass_kernel_spmd

    a = {k: np.asarray(v) for k, v in inputs.items()}
    above, below, leaf = search_tree()
    src, dst = a["src"], a["dst"]
    leaf32 = leaf.astype(np.int32)
    table = np.stack([leaf32, np.where(leaf32 < 0, np.int32(NE - 1), leaf32), src[leaf], dst[leaf]], 1)

    def feature_rows(w, k):
        return w.reshape(w.shape[0], k, 128, w.shape[-1]).transpose(0, 2, 1, 3)

    w1, w3, w2 = (a[f"L0_ffn_{n}"].transpose(0, 2, 1) for n in ("w1", "w3", "w2"))
    w13 = np.stack([feature_rows(w, 4).reshape(E0, 128, 4, HB, 512) for w in (w1, w3)], 4)
    w13 = w13.transpose(3, 0, 1, 2, 4, 5).reshape(HB * E0 * 128, 4096)
    w2 = w2.reshape(E0, HB, 4, 128, D).transpose(1, 0, 3, 2, 4).reshape(HB * E0 * 128, 2048)

    def twice(w):
        z = np.zeros_like(w)
        return np.block([[w, z], [z, w]])

    g = {k[7:]: v for k, v in a.items() if k.startswith("L1_gnn_")}
    arrays = dict(
        consts=constants(), x=a["x"], anc=src[above], sub=src[below], leaf_table=table, src=src, dst=dst,
        ea4=a["edge_attr_4"], ea8=a["edge_attr_8"],
        gate=a["L0_ffn_gate_w"].T.reshape(4, 128, E0).transpose(1, 0, 2), w13=w13, w2=w2,
        w_up=np.concatenate([g["W_up0"], g["W_up1"]], 1), w_mlp1=twice(g["W_mlp1"]),
        w_mlp23=np.concatenate([twice(g["W_mlp2"]), twice(g["W_mlp3"])], 1),
        w_mlp4=np.concatenate([g["W_mlp4"], g["W_mlp4"]], 0),
        w_out=np.concatenate([g["W_out0"][:128], g["W_out0"][128:], g["W_out1"][:128], g["W_out1"][128:]], 1),
        ew=a["L1_ffn_expert_weights"], ei=a["L1_ffn_expert_indices"],
        v1=feature_rows(a["L1_ffn_w1"], 4).reshape(E1, 128, 1024),
        v2=feature_rows(a["L1_ffn_w2"], 2).reshape(E1, 128, 1024))
    nc = bacc.Bacc("TRN2", target_bir_lowering=False, num_devices=1)
    given, args = {}, []
    for name, v in arrays.items():
        v = np.ascontiguousarray(v)
        given[f"in_{name}"] = v
        args.append(nc.dram_tensor(f"in_{name}", v.shape, mybir.dt.from_np(v.dtype), kind="ExternalInput").ap())
    out = nc.dram_tensor("out", (N, D), F32, kind="ExternalOutput").ap()
    program(nc, *args, out)
    return run_bass_kernel_spmd(nc, [given], core_ids=[0]).results[0]["out"]
```

```python
from contextlib import ExitStack

import numpy as np

import concourse.bass as bass
from concourse import mybir

F32 = mybir.dt.float32
I32 = mybir.dt.int32
F32R = mybir.dt.float32r
BF16 = mybir.dt.bfloat16
ALU = mybir.AluOpType
ACT = mybir.ActivationFunctionType
AX = mybir.AxisListType

N, D = 1250, 512
NP, NT = 128, 10
NPAD = NP * NT
NE, EP, EJ = 40000, 125, 320
SEARCH_LEVELS = 16
TOP = 7
LEAVES = 2 ** (SEARCH_LEVELS - TOP)
E0, H0 = 8, 1536
TILE = 128
FT = (2 * N - E0) // TILE + E0
HB = H0 // 512
WN, NW = 64, NPAD // 64
GT = 1
GROUP = GT * TILE
NG = (NE - NW) // GROUP + NW
BT = 8
NTILE = NG * GT
NB = -(-NTILE // BT)
NREC = NB * BT
SLOTS = NREC * TILE
assert SLOTS * NREC < 2 ** 24
REC = 16
MUL, HID = 128, 64
SILU_2MOM = 1.679177
T1, E1, H1 = 512, 8, 256
BIG = float(2 ** 20)
ARENA = 42700
ZONE = HB * (4096 + 2048)
SKIP = 2 ** 20


def rows(t):
    return min(NP, N - t * NP)


def search_tree():
    lo, hi, levels = np.array([0]), np.array([NE]), []
    for _ in range(SEARCH_LEVELS):
        mid = (lo + hi) // 2
        levels.append(mid)
        lo, hi = np.stack([lo, mid], 1).ravel(), np.stack([mid, hi], 1).ravel()
    sub = np.arange(128)
    above = np.stack([levels[l][sub >> (TOP - l)] for l in range(TOP)], 1)
    below = np.concatenate([levels[l].reshape(128, -1) for l in range(TOP, SEARCH_LEVELS)], 1)
    return above, below, hi - 1


CONSTS = dict(ident=128, ones=128, before=128, node=NPAD, node_col=NT, valid=NT, right=TOP, left=TOP,
              part=1, sub512=1)


def constants():
    p = np.arange(128)[:, None]
    sub = (p >> (TOP - 1 - np.arange(TOP)[None])) & 1
    c = dict(ident=np.eye(128), ones=np.ones((128, 128)), before=p < p.T,
             node=np.broadcast_to(np.arange(NPAD), (128, NPAD)), node_col=p + NP * np.arange(NT)[None],
             valid=p + NP * np.arange(NT)[None] < N,
             right=sub, left=1 - sub,
             part=p, sub512=p * LEAVES)
    return np.concatenate([np.asarray(c[k], np.float32) for k in CONSTS], 1)


class Lane:

    def __init__(self, sem):
        self.new_sem, self.steps, self.seen = sem, [], {}
        self.chained, self.last = False, None

    def stage(self, name, chained):
        self.sem, self.count, self.chained = self.new_sem(name), 0, chained

    def wait(self, after):
        need = {}
        for s, v in after:
            if v > self.seen.get(id(s), 0):
                need[id(s)] = (s, max(v, need.get(id(s), (s, 0))[1]))
        for k, (s, v) in need.items():
            self.seen[k] = v
            self.steps.append(lambda e, s=s, v=v: e.wait_ge(s, v))

    def __call__(self, op, /, *after, **kw):
        self.wait([*after, self.last] if self.chained and self.last else after)
        self.count += 1
        self.steps.append(lambda e, s=self.sem: method(e, op)(**kw).then_inc(s, 1))
        self.last = (self.sem, self.count)
        return self.last

    def quiet(self, op, /, *after, **kw):
        self.wait(after)
        self.steps.append(lambda e: method(e, op)(**kw))

    def dma(self, done, /, *after, **kw):
        self.wait(after)
        done.count += 16
        op = "indirect_dma_start" if "out_offset" in kw else "dma_start"
        self.steps.append(lambda e: method(e, op)(**kw).then_inc(done.sem, 16))
        return (done.sem, done.count)

    def run(self, e):
        for s in self.steps:
            s(e)


def method(e, op):
    return {
        "matmul": lambda: e.matmul, "transpose": lambda: e.transpose, "activation": lambda: e.activation,
        "tensor_scalar": lambda: e.tensor_scalar, "tensor_tensor": lambda: e.tensor_tensor,
        "scalar_tensor_tensor": lambda: e.scalar_tensor_tensor, "tensor_copy": lambda: e.tensor_copy,
        "tensor_reduce": lambda: e.tensor_reduce, "tensor_tensor_scan": lambda: e.tensor_tensor_scan,
        "bn_stats": lambda: e.bn_stats, "bn_aggr": lambda: e.bn_aggr, "reciprocal": lambda: e.reciprocal,
        "memset": lambda: e.memset, "dma_start": lambda: e.dma_start,
        "indirect_dma_start": lambda: e.indirect_dma_start,
    }[op]()


class Done:

    def __init__(self, sem):
        self.sem, self.count = sem, 0


def program(nc, consts, x, anc, sub, leaf_table, src, dst, ea4, ea8, gate, w13, w2, w_up, w_mlp1, w_mlp23,
            w_mlp4, w_out, ew, ei, v1, v2, out):
    ctx = ExitStack()
    with ctx:
        n_sem = [0]

        def sem(name):
            n_sem[0] += 1
            return ctx.enter_context(nc.semaphore(f"{name}_{n_sem[0]}"))

        def done(name):
            return Done(sem(name))

        def dram(name, shape, dt=F32):
            return nc.dram_tensor(name, shape, dt, kind="Internal").ap()

        def some(*tokens):
            return [v for v in tokens if v is not None]

        PE, V, A, G, S = (Lane(lambda s, n=n: sem(f"{n}_{s}")) for n in ("pe", "dve", "act", "pool", "sp"))

        def stage(name, chained=True):
            for lane in (PE, V, A, G):
                lane.stage(name, chained and lane in (V, A))

        arena = ctx.enter_context(nc.sbuf_tensor("arena", [128, ARENA], F32))
        phase = [ExitStack()]
        ctx.callback(lambda: phase[0].close())

        def phase_tensor(name, words, dt=F32):
            return phase[0].enter_context(nc.sbuf_tensor(name, [128, words], dt))[:, :]

        def next_phase():
            phase[0].close()
            phase[0] = ExitStack()

        top = [0]

        def carve(words, at=None):
            if at is None:
                at, top[0] = top[0], top[0] + words
                assert top[0] <= ARENA, top[0]
            return arena[:, at:at + words]

        def zone_of(at, size):
            used = [0]

            def take(words):
                used[0] += words
                assert used[0] <= size, (used[0], size)
                return carve(words, at + used[0] - words)

            return take

        banks = [ctx.enter_context(nc.psum_tensor(f"bank{i}", [128, 512], F32)) for i in range(8)]

        cst = carve(sum(CONSTS.values()))
        K, at = {}, 0
        for name, w in CONSTS.items():
            K[name] = cst[:, at:at + w]
            at += w
        ident, ones, before = K["ident"], K["ones"], K["before"]
        xs = carve(NT * D).rearrange("p (t d) -> p t d", t=NT)
        ln_at = top[0]
        ln = carve(NT * D).rearrange("p (t d) -> p t d", t=NT)
        lnT_at = top[0]
        lnT = carve(4 * NPAD).rearrange("p (k n) -> p k n", k=4)
        edge_at = top[0]
        edges = carve(EJ * REC).rearrange("p (j c) -> p j c", c=REC)
        zone = top[0]
        carve(ZONE)
        small_at = top[0]
        small = zone_of(small_at, ARENA - small_at)

        stage("load")
        d_const, d_x, d_tree, d_edge, d_wts = done("const"), done("x"), done("tree"), done("edge"), done("wts")
        early = zone_of(zone + NT * NPAD, ZONE - NT * NPAD)
        anc_i, sub_i = small(TOP), early(LEAVES - 1)
        S.dma(d_tree, out=anc_i.bitcast(I32), in_=anc)
        ready_tree = S.dma(d_tree, out=sub_i.bitcast(I32), in_=sub)
        ready_const = S.dma(d_const, out=cst, in_=consts)
        last = rows(NT - 1)
        blank = V("memset", ap=xs[:, NT - 1], constant=0.0)
        A.dma(d_x, out=xs[:, :NT - 1], in_=x[:NP * (NT - 1)].rearrange("(t p) d -> p t d", p=NP))
        ready_x = A.dma(d_x, blank, out=xs[:last, NT - 1], in_=x[NP * (NT - 1):])
        src_i, dst_i = early(EJ), early(EJ)
        A.dma(d_edge, out=src_i[:EP].bitcast(I32), in_=src.rearrange("(p j) -> p j", p=EP))
        A.dma(d_edge, out=dst_i[:EP].bitcast(I32), in_=dst.rearrange("(p j) -> p j", p=EP))
        gate_sb = small(4 * E0).rearrange("p (k e) -> p k e", k=4)
        m1_sb = small(128)
        S.dma(d_wts, out=gate_sb, in_=gate)
        ready_wts = S.dma(d_wts, out=m1_sb[:16], in_=w_mlp1)
        T5 = T1 // NP
        ew_sb, ei_sb = small(2 * T5), small(2 * T5)
        d_ew = done("ew")
        S.dma(d_ew, out=ew_sb.rearrange("p (t k) -> p t k", k=2), in_=ew.rearrange("(t p) k -> p t k", p=NP))
        ready_ew = S.dma(d_ew, out=ei_sb.bitcast(I32).rearrange("p (t k) -> p t k", k=2),
                         in_=ei.rearrange("(t p) k -> p t k", p=NP))

        sorted_edges = dram("sorted_edges", [SLOTS, REC])
        blank_recs = phase_tensor("blank_records", NREC * REC)
        in_win_space = phase_tensor("in_window", NW * EJ // 2)
        blank_rec = blank_recs.rearrange("p (s c) -> p s c", c=REC)
        m = G("memset", ap=blank_recs, constant=0.0)
        m = G("memset", m, ap=blank_rec[:, :, 1], constant=-1.0)
        d_fill = done("fill")
        filled = G.dma(d_fill, m, out=sorted_edges.rearrange("(p s) c -> p (s c)", p=128),
                       in_=blank_recs)
        ws, d_ws0 = dram("pair_rows", [FT * TILE, D]), done("zero_rows")
        zrow = early(D)
        m = G("memset", ap=zrow, constant=0.0)
        zeroed = G.dma(d_ws0, m, out=ws.rearrange("(t p) d -> p t d", p=128),
                       in_=zrow.unsqueeze(1).to_broadcast([128, FT, D]))
        at4, at8 = blank_recs[:, :EJ * 4], blank_recs[:, EJ * 4:EJ * 12]
        A.dma(d_edge, filled, out=at4[:EP], in_=ea4.rearrange("(p j) c -> p (j c)", p=EP))
        ready_edge = A.dma(d_edge, out=at8[:EP], in_=ea8.rearrange("(p j) c -> p (j c)", p=EP))

        def whole(count, least, unit, shift, ends, base, pe, n, tmp):
            c = V("tensor_scalar", pe, out=tmp.bitcast(I32), in0=count, scalar1=float(unit - 1), scalar2=None,
                  op0=ALU.add)
            c = V("tensor_scalar", c, out=tmp.bitcast(I32), in0=tmp.bitcast(I32), scalar1=shift, scalar2=None,
                  op0=ALU.logical_shift_right)
            c = V("tensor_copy", c, out=n, in_=tmp.bitcast(I32))
            c = V("tensor_scalar", c, out=n, in0=n, scalar1=float(least), scalar2=None, op0=ALU.max)
            c = V("tensor_tensor_scan", c, ready_const, out=ends, data0=ones[:, 0:n.shape[-1]], data1=n,
                  initial=0.0, op0=ALU.mult, op1=ALU.add)
            c = V("tensor_tensor", c, out=base, in0=ends, in1=n, op=ALU.subtract)
            return V("tensor_scalar", c, out=base, in0=base, scalar1=float(unit), scalar2=None, op0=ALU.mult)

        er = edges[:EP]
        slot_i = small(EJ)[:EP].bitcast(I32)
        g_same, g_row, g_first = small(NG), small(NG), small(NG)
        known = {}

        PAUSE = 8

        def sort_edges():
            dstf, win, slot, ones_row = (early(EJ)[:EP] for _ in range(4))
            seq = [early(EJ)[:EP] for _ in range(2)]
            in_win = in_win_space[:EP].bitcast(BF16).rearrange("p (w j) -> p w j", w=NW)
            row_tot, n_win, end_win, base_win, tmp_win, start = (small(NW) for _ in range(6))
            start = start[:EP]
            V("memset", ap=ones_row, constant=1.0)
            V("memset", ap=slot, constant=0.0)
            V("tensor_copy", ready_edge, out=er[:, :, 0].bitcast(I32), in_=src_i[:EP].bitcast(I32))
            c = V("tensor_copy", out=dstf, in_=dst_i[:EP].bitcast(I32))
            yield
            c = V("tensor_scalar", c, out=win, in0=dstf, scalar1=float(WN), scalar2=None, op0=ALU.is_ge)
            for w in range(2, NW):
                c = V("scalar_tensor_tensor", c, out=win, in0=dstf, scalar=float(WN * w), in1=win,
                      op0=ALU.is_ge, op1=ALU.add)
                yield
            for w in range(NW):
                c = V("tensor_scalar", c, out=in_win[:, w], in0=win, scalar1=float(w), scalar2=None,
                      op0=ALU.is_equal)
                yield
            c = V("tensor_reduce", c, out=row_tot[:EP], in_=in_win, op=ALU.add, axis=AX.X)
            for _ in range(PAUSE):
                yield
            PE("matmul", c, ready_const, out=banks[6][:EP, 0:NW], lhsT=before[:EP, :EP], rhs=row_tot[:EP],
               start=True, stop=True)
            pe = PE("matmul", out=banks[7][:, 0:NW], lhsT=ones[:EP, :], rhs=row_tot[:EP], start=True, stop=True)
            for _ in range(PAUSE):
                yield
            whole(banks[7][:, 0:NW], 1, GROUP, GROUP.bit_length() - 1, end_win, base_win, pe, n_win, tmp_win)
            c = V("scalar_tensor_tensor", out=start, in0=banks[6][:EP, 0:NW], scalar=-1.0, in1=base_win[:EP],
                  op0=ALU.add, op1=ALU.add)
            yield
            for w in range(NW):
                V("tensor_tensor_scan", out=seq[w % 2], data0=ones_row, data1=in_win[:, w],
                  initial=start[:, w:w + 1], op0=ALU.mult, op1=ALU.add)
                V("tensor_tensor", out=seq[w % 2], in0=seq[w % 2], in1=in_win[:, w], op=ALU.mult)
                V("tensor_tensor", out=slot, in0=slot, in1=seq[w % 2], op=ALU.add)
                yield
            tile_i, tile_f = seq[0].bitcast(I32), seq[1]
            V("tensor_copy", out=slot_i, in_=slot)
            V("tensor_scalar", out=tile_i, in0=slot_i, scalar1=TILE.bit_length() - 1, scalar2=None,
              op0=ALU.logical_shift_right)
            V("tensor_copy", out=tile_f, in_=tile_i)
            V("tensor_scalar", out=slot, in0=slot, scalar1=float(NREC), scalar2=None, op0=ALU.mult)
            V("scalar_tensor_tensor", out=slot_i, in0=tile_f, scalar=float(1 - TILE * NREC), in1=slot,
              op0=ALU.mult, op1=ALU.add)
            yield
            V("tensor_copy", out=er[:, :, 1], in_=dstf)
            V("memset", ap=er[:, :, 14:16], constant=0.0)
            V("tensor_copy", out=er[:, :, 2:6], in_=at4[:EP].rearrange("p (j c) -> p j c", c=4))
            yield
            known["records"] = V("tensor_copy", out=er[:, :, 6:14], in_=at8[:EP].rearrange("p (j c) -> p j c", c=8))
            yield
            g_win = early(NG)
            V("memset", ap=g_win, constant=0.0)
            for w in range(NW - 1):
                V("scalar_tensor_tensor", out=g_win, in0=K["node"][:, 0:NG], scalar=end_win[:, w:w + 1], in1=g_win,
                  op0=ALU.is_ge, op1=ALU.add)
                yield
            V("memset", ap=g_same[:, 0:1], constant=0.0)
            V("tensor_tensor", out=g_same[:, 1:], in0=g_win[:, 1:], in1=g_win[:, :NG - 1], op=ALU.is_equal)
            V("tensor_scalar", out=g_first, in0=g_win, scalar1=float(WN), scalar2=None, op0=ALU.mult)
            row_f = early(NG)
            V("tensor_scalar", out=row_f, in0=g_win, scalar1=128.0, scalar2=K["part"], op0=ALU.mult, op1=ALU.add)
            V("scalar_tensor_tensor", out=row_f[:, :NG - 1], in0=g_same[:, 1:], scalar=BIG,
              in1=row_f[:, :NG - 1], op0=ALU.mult, op1=ALU.add)
            known["groups"] = V("tensor_copy", out=g_row.bitcast(I32), in_=row_f)
            yield

        edge_sort = sort_edges()

        def advance(n):
            for _ in range(n):
                next(edge_sort, None)

        d_scatter = done("scatter")
        left = list(range(EJ))

        def scatter_edges(n):
            for _ in range(min(n, len(left))):
                j = left.pop(0)
                G.dma(d_scatter, known["records"], filled, out=sorted_edges,
                      out_offset=bass.IndirectOffsetOnAxis(ap=slot_i[:, j:j + 1], axis=0),
                      in_=er[:, j, :], in_offset=None)

        stats, mv, rstd, eps_v, nt_ = small(6 * 2), small(2 * NT), small(NT), small(NT), small(NT)

        def block_stats(t, ready):
            st = stats[:, 6 * (t % 2):6 * (t % 2) + 6]
            V("bn_stats", ready, out=st, in_=xs[:, t])
            return V("bn_aggr", out=mv[:, 2 * t:2 * t + 2], in_=st)

        def layer_norm(blocks=range(NT)):
            q = mv.rearrange("p (t c) -> p t c", c=2)
            b = slice(blocks[0], blocks[-1] + 1)
            c = V("tensor_scalar", out=eps_v[:, b], in0=q[:, b, 1], scalar1=1e-5, scalar2=None, op0=ALU.add)
            a = A("activation", c, out=nt_[:, b], in_=eps_v[:, b], func=ACT.Sqrt)
            V("reciprocal", a, out=rstd[:, b], in_=nt_[:, b])
            V("tensor_tensor", out=nt_[:, b], in0=rstd[:, b], in1=rstd[:, b], op=ALU.mult)
            V("tensor_tensor", out=nt_[:, b], in0=nt_[:, b], in1=eps_v[:, b], op=ALU.mult)
            V("tensor_scalar", out=nt_[:, b], in0=nt_[:, b], scalar1=-0.5, scalar2=1.5, op0=ALU.mult, op1=ALU.add)
            V("tensor_tensor", out=rstd[:, b], in0=nt_[:, b], in1=rstd[:, b], op=ALU.mult)
            return [V("tensor_scalar", out=ln[:, t], in0=xs[:, t], scalar1=q[:, t, 0:1],
                      scalar2=rstd[:, t:t + 1], op0=ALU.subtract, op1=ALU.mult) for t in blocks]

        def turn_ln(t, ready):
            for k in range(4):
                tr = PE("transpose", ready, *some(turned[t % 2]), out=banks[t % 2][:, k * 128:(k + 1) * 128],
                        in_=ln[:, t, k * 128:(k + 1) * 128], identity=ident)
            return tr, banks[t % 2][:, :].rearrange("p (k n) -> p k n", k=4)

        stage("segment")
        ancf = small(TOP)
        lo_p, hi_p, t7 = small(1), small(1), small(TOP)
        V("tensor_copy", ready_tree, ready_const, out=ancf, in_=anc_i.bitcast(I32))
        V("tensor_scalar", out=t7, in0=K["left"], scalar1=-BIG, scalar2=None, op0=ALU.mult)
        V("tensor_tensor", out=anc_i, in0=ancf, in1=K["right"], op=ALU.mult)
        V("tensor_tensor", out=t7, in0=t7, in1=anc_i, op=ALU.add)
        V("tensor_reduce", out=lo_p, in_=t7, op=ALU.max, axis=AX.X)
        V("tensor_tensor", out=anc_i, in0=ancf, in1=K["left"], op=ALU.mult)
        V("scalar_tensor_tensor", out=t7, in0=K["right"], scalar=BIG, in1=anc_i, op0=ALU.mult, op1=ALU.add)
        V("tensor_reduce", out=hi_p, in_=t7, op=ALU.min, axis=AX.X)
        find = zone_of(zone, NT * NPAD)
        in_sub, lowq = find(NPAD), find(NPAD)
        V("tensor_scalar", out=lowq, in0=K["node"], scalar1=lo_p, scalar2=None, op0=ALU.is_ge)
        in_sub_done = V("scalar_tensor_tensor", out=in_sub, in0=K["node"], scalar=hi_p, in1=lowq,
                        op0=ALU.is_lt, op1=ALU.mult)
        subf = find(LEAVES - 1)
        V("tensor_copy", out=subf, in_=sub_i.bitcast(I32))
        low, high = [find(LEAVES) for _ in range(2)], [find(LEAVES) for _ in range(2)]
        V("tensor_copy", out=low[0][:, 0:1], in_=lo_p)
        V("tensor_copy", out=high[0][:, 0:1], in_=hi_p)
        for lv in range(SEARCH_LEVELS - TOP):
            n = 2 ** lv
            a, b = lv % 2, 1 - lv % 2
            v = subf[:, n - 1:2 * n - 1]
            nl, nh = (z[b][:, 0:2 * n].rearrange("p (n s) -> p n s", s=2) for z in (low, high))
            V("tensor_copy", out=nl[:, :, 0], in_=low[a][:, 0:n])
            V("tensor_tensor", out=nl[:, :, 1], in0=low[a][:, 0:n], in1=v, op=ALU.max)
            V("tensor_tensor", out=nh[:, :, 0], in0=high[a][:, 0:n], in1=v, op=ALU.min)
            V("tensor_copy", out=nh[:, :, 1], in_=high[a][:, 0:n])
        f = (SEARCH_LEVELS - TOP) % 2
        key = find(LEAVES)
        V("tensor_tensor", out=key, in0=low[f], in1=high[f], op=ALU.is_ge)
        key_done = V("scalar_tensor_tensor", out=key, in0=key, scalar=2 * BIG, in1=low[f], op0=ALU.mult,
                     op1=ALU.add)
        for t in range(NT):
            first_leaf = PE("matmul", in_sub_done, out=banks[2][:, t:t + 1], lhsT=in_sub[:, t * NP:(t + 1) * NP],
                            rhs=K["sub512"], start=True, stop=True)
        leaf = small(NT)
        hit = [find(LEAVES) for _ in range(2)]
        reads = []
        for t in range(NT):
            b = banks[3 + t % 3]
            k = PE("matmul", key_done, *(reads[-3:-2] if t >= 3 else []), out=b[:, :],
                   lhsT=in_sub[:, t * NP:(t + 1) * NP], rhs=key, start=True, stop=True)
            reads.append(V("scalar_tensor_tensor", k, out=hit[t % 2], in0=b[:, :],
                           scalar=K["node_col"][:, t:t + 1], in1=K["node"][:, 1:LEAVES + 1], op0=ALU.is_le, op1=ALU.mult))
            V("tensor_reduce", out=leaf[:, t:t + 1], in_=hit[t % 2], op=ALU.max, axis=AX.X)
        leaf_i = small(NT).bitcast(I32)
        c = V("scalar_tensor_tensor", first_leaf, out=leaf_i, in0=banks[2][:, 0:NT], scalar=-1.0, in1=leaf,
              op0=ALU.add, op1=ALU.add)
        leaf_known = c
        d_leaf = done("leaf")
        found = small(4 * NT).bitcast(I32).rearrange("p (t c) -> p t c", c=4)
        for t in range(NT):
            got = G.dma(d_leaf, leaf_known, out=found[:, t], out_offset=None, in_=leaf_table,
                        in_offset=bass.IndirectOffsetOnAxis(ap=leaf_i[:, t:t + 1], axis=0))
        for t in range(NT):
            block_stats(t, ready_x)
        normed = layer_norm()
        f4 = small(4 * NT).rearrange("p (t c) -> p t c", c=4)
        c = V("tensor_copy", got, out=f4, in_=found)
        diag = [find(NP) for _ in range(NT)]
        place = [(banks[(6, 7, 2)[t // 4]], (t % 4) * 128) for t in range(NT)]
        for t in range(NT):
            dg = V("tensor_scalar", out=diag[t], in0=ident, scalar1=f4[:, t, 1:2], scalar2=None, op0=ALU.mult)
            sr = PE("matmul", dg, leaf_known, out=place[t][0][:, place[t][1]:place[t][1] + NP], lhsT=ones,
                    rhs=diag[t], start=True, stop=True)
        rcnt = small(NT)
        V("tensor_tensor", out=rcnt, in0=f4[:, :, 3], in1=f4[:, :, 2], op=ALU.subtract)
        V("tensor_scalar", out=rcnt, in0=rcnt, scalar1=1.0, scalar2=None, op0=ALU.add)
        V("reciprocal", out=rcnt, in_=rcnt)
        seg_row = carve(NPAD, lnT_at)
        for t in range(0, NT, 4):
            n = min(4, NT - t) * NP
            V("tensor_copy", sr, out=seg_row[:, t * NP:t * NP + n], in_=place[t][0][:, 0:n])
        member = carve(NT * NPAD, zone).rearrange("p (t q) -> p t q", t=NT)
        mem = [V("tensor_scalar", out=member[:, t], in0=seg_row, scalar1=f4[:, t, 0:1], scalar2=None,
                 op0=ALU.is_equal) for t in range(NT)]
        advance(4)
        for t in range(NT):
            b, r = banks[3 + t % 3], rows(t)
            for k in range(NT):
                c = PE("matmul", mem[k], normed[k], *some(reads[-3] if t >= 3 else reads[-1]), out=b[:r, :],
                       lhsT=member[:rows(k), k, t * NP:t * NP + r], rhs=ln[:rows(k), k], start=k == 0,
                       stop=k == NT - 1)
            reads.append(V("scalar_tensor_tensor", c, out=xs[:r, t], in0=b[:r, :], scalar=rcnt[:r, t:t + 1],
                           in1=xs[:r, t], op0=ALU.mult, op1=ALU.add))
            block_stats(t, reads[-1])
            if t < NT - 1:
                advance(8)
        segment_read = PE.last

        stage("route")
        normed = layer_norm()
        turned = [None, None]

        def turn(t):
            tr, block = turn_ln(t, normed[t])
            turned[t % 2] = A("activation", tr, out=lnT[:, :, t * NP:(t + 1) * NP], in_=block, func=ACT.Copy)

        turn(0)
        for t in range(NT):
            lnT_done = turned[t % 2]
            if t + 1 < NT:
                turn(t + 1)
            for k in range(4):
                c = PE("matmul", lnT_done, ready_wts, out=banks[2][:, t * E0:(t + 1) * E0],
                       lhsT=lnT[:, k, t * NP:(t + 1) * NP], rhs=gate_sb[:, k], start=k == 0, stop=k == 3)
        lnT_read = c
        pair_tmp = zone_of(zone, 1600)
        logit, cand, pick1, pick2, both, rank = (pair_tmp(NT * E0).rearrange("p (t e) -> p t e", e=E0)
                                                 for _ in range(6))
        eid = K["node"][:, 0:E0].unsqueeze(1).to_broadcast([128, NT, E0])
        top1, top2, first = small(NT), small(NT), small(NT)

        def wide(v):
            return v.unsqueeze(2).to_broadcast([128, NT, E0])

        advance(30)
        V("tensor_copy", c, out=logit, in_=banks[2][:, 0:NT * E0].rearrange("p (t e) -> p t e", e=E0))
        for best, pick in ((top1, pick1), (top2, pick2)):
            V("tensor_reduce", out=best, in_=logit, op=ALU.max, axis=AX.X)
            V("tensor_tensor", out=cand, in0=logit, in1=wide(best), op=ALU.is_lt)
            V("scalar_tensor_tensor", out=cand, in0=cand, scalar=float(E0), in1=eid, op0=ALU.mult, op1=ALU.add)
            V("tensor_reduce", out=first, in_=cand, op=ALU.min, axis=AX.X)
            V("tensor_tensor", out=pick, in0=eid, in1=wide(first), op=ALU.is_equal)
            V("scalar_tensor_tensor", out=logit, in0=pick, scalar=-1e30, in1=logit, op0=ALU.mult, op1=ALU.add)
        V("tensor_tensor", out=both, in0=pick1, in1=pick2, op=ALU.add)
        V("tensor_tensor", out=both, in0=both, in1=wide(K["valid"]), op=ALU.mult)
        so_far = pair_tmp((NT + 1) * E0).rearrange("p (t e) -> p t e", e=E0)
        V("memset", ap=so_far[:, 0], constant=0.0)
        for t in range(NT):
            picked = V("tensor_tensor", out=so_far[:, t + 1], in0=so_far[:, t], in1=both[:, t], op=ALU.add)
        PE.quiet("matmul", picked, out=banks[6][:, 0:NT * E0], lhsT=before, rhs=both.rearrange("p t e -> p (t e)"),
                 start=True, stop=False)
        PE.quiet("matmul", out=banks[6][:, 0:NT * E0], lhsT=ones,
                 rhs=so_far[:, 0:NT].rearrange("p t e -> p (t e)"), start=False, stop=True)
        c = PE("matmul", out=banks[7][:, 0:E0], lhsT=ones, rhs=so_far[:, NT], start=True, stop=True)
        n_t, end_t, base_t, tmp_t = small(E0), small(E0), small(E0), small(E0)
        whole(banks[7][:, 0:E0], 0, TILE, TILE.bit_length() - 1, end_t, base_t, c, n_t, tmp_t)
        V("tensor_tensor", out=rank, in0=banks[6][:, 0:NT * E0].rearrange("p (t e) -> p t e", e=E0),
          in1=base_t.unsqueeze(1).to_broadcast([128, NT, E0]), op=ALU.add)
        pair_i = [small(NT).bitcast(I32) for _ in range(2)]
        for pick, place_i in ((pick1, pair_i[0]), (pick2, pair_i[1])):
            V("tensor_tensor", out=cand, in0=rank, in1=pick, op=ALU.mult)
            V("tensor_reduce", out=first, in_=cand, op=ALU.add, axis=AX.X)
            pairs_known = V("tensor_copy", out=place_i, in_=first)
        te = small(FT)
        cmp = pair_tmp(FT * E0).rearrange("p (g e) -> p g e", e=E0)
        V("tensor_tensor", out=cmp, in0=K["node"][:, 0:FT].unsqueeze(2).to_broadcast([128, FT, E0]),
          in1=end_t.unsqueeze(1).to_broadcast([128, FT, E0]), op=ALU.is_ge)
        V("tensor_reduce", out=te, in_=cmp, op=ALU.add, axis=AX.X)
        V("tensor_scalar", out=te, in0=te, scalar1=float(E0 - 1), scalar2=None, op0=ALU.min)
        t_same = cmp.rearrange("p g e -> p (g e)")[:, 0:FT]
        V("memset", ap=t_same[:, 0:1], constant=0.0)
        V("tensor_tensor", out=t_same[:, 1:], in0=te[:, 1:], in1=te[:, :FT - 1], op=ALU.is_equal)
        V("tensor_scalar", out=te, in0=te, scalar1=128.0, scalar2=K["part"], op0=ALU.mult, op1=ALU.add)
        V("scalar_tensor_tensor", out=te, in0=t_same, scalar=float(SKIP), in1=te, op0=ALU.mult, op1=ALU.add)
        w_row = small(HB * FT).bitcast(I32).rearrange("p (b t) -> p b t", b=HB)
        for b in range(HB):
            tiles_known = V("tensor_scalar", out=w_row[:, b], in0=te, scalar1=float(b * E0 * 128), scalar2=None,
                            op0=ALU.add)
        wt = [small(NT), small(NT)]
        c = V("tensor_tensor", out=first, in0=top2, in1=top1, op=ALU.subtract)
        a = A("activation", c, out=top2, in_=first, func=ACT.Exp)
        V("tensor_scalar", a, out=first, in0=top2, scalar1=1.0, scalar2=None, op0=ALU.add)
        V("reciprocal", out=wt[0], in_=first)
        weights_known = V("tensor_tensor", out=wt[1], in0=wt[0], in1=top2, op=ALU.mult)
        advance(1000)
        route_done = V.last

        stage("expert", chained=False)
        d_pair = done("pair")
        wz = zone_of(zone, ZONE)
        up = [wz(4096).rearrange("p (k c h) -> p k c h", k=4, c=2) for b in range(HB)]
        down = [wz(2048).rearrange("p (k d) -> p k d", k=4) for b in range(HB)]
        d_up = [done(f"up{b}") for b in range(HB)]
        d_dn = [done(f"down{b}") for b in range(HB)]
        up_read, dn_read = [route_done] * HB, [route_done] * HB
        up_in, dn_in = [None] * HB, [None] * HB

        def load_up(i, b):
            up_in[b] = G.dma(d_up[b], tiles_known, up_read[b], out=up[b].rearrange("p k c h -> p (k c h)"),
                             out_offset=None, in_=w13,
                             in_offset=bass.IndirectOffsetOnAxis(ap=w_row[:, b, i:i + 1], axis=0),
                             bounds_check=HB * E0 * 128 - 1, oob_is_err=False)

        def load_down(i, b):
            dn_in[b] = G.dma(d_dn[b], dn_read[b], zeroed, out=down[b].rearrange("p k d -> p (k d)"),
                             out_offset=None, in_=w2,
                             in_offset=bass.IndirectOffsetOnAxis(ap=w_row[:, b, i:i + 1], axis=0),
                             bounds_check=HB * E0 * 128 - 1, oob_is_err=False)

        load_up(0, 0)
        for t in range(NT):
            for kk in range(2):
                r = rows(t)
                rows_sent = G.dma(d_pair, pairs_known, normed[t], zeroed, out=ws,
                                  out_offset=bass.IndirectOffsetOnAxis(ap=pair_i[kk][:r, t:t + 1], axis=0),
                                  in_=ln[:r, t], in_offset=None)
        for b in range(1, HB):
            load_up(0, b)
        for b in range(HB):
            load_down(0, b)
        LATE = 2 * MUL + 256 + 512 + 512
        assert NB * 64 + NTILE <= 4 * NPAD - LATE
        buf = zone_of(ln_at, NT * D)
        xin, sil = ([buf(512) for _ in range(2)] for _ in range(2))
        hid, yo = buf(1536), [buf(512) for _ in range(2)]
        next_phase()
        xT, hT = ([phase_tensor(f"{n}{i}", 1024, F32R).rearrange("p (s c) -> p s c", s=2) for i in range(2)]
                  for n in ("rows_hl", "hidden_hl"))
        NW3 = 3
        part = [phase_tensor(f"weights_hl{i}", 2048, F32R).rearrange("p (s c) -> p s c", s=2) for i in range(NW3)]
        part_free, part_high, part_low = [None] * NW3, {}, {}
        d_in = [done(f"in{i}") for i in range(2)]
        d_out = [done(f"rows{i}") for i in range(2)]
        ys = dram("pair_out", [FT * TILE, D])
        xin_free, xT_free, sil_free, up_free = [None] * 2, [None] * 2, [None] * 2, [None] * 2
        hT_free, yo_free = [None] * 2, [None] * 2
        tr_free = {0: None, 1: None, 6: None}
        hid_free, y_read = [None] * HB, None
        came, xt = {}, {}

        def load_rows(i):
            came[i] = S.dma(d_in[i % 2], rows_sent, picked, lnT_done, *some(xin_free[i % 2]), out=xin[i % 2],
                            in_=ws[i * TILE:(i + 1) * TILE])

        def split_turned(tr, free, bank, out):
            high = A("activation", tr, *some(free), out=out[:, 0], in_=bank, func=ACT.Copy)
            return V("tensor_tensor", high, out=out[:, 1], in0=bank, in1=out[:, 0].bitcast(F32), op=ALU.subtract)

        def turn_rows(i):
            s = i % 2
            for k in range(4):
                tr = PE("transpose", came[i], *some(tr_free[0]), out=banks[0][:, k * 128:(k + 1) * 128],
                        in_=xin[s][:, k * 128:(k + 1) * 128], identity=ident)
            xin_free[s] = tr
            tr_free[0] = xt[i] = split_turned(tr, xT_free[s], banks[0][:, :], xT[s])

        def turn_hidden(b):
            bank = (6, 1)[b % 2]
            for k in range(4):
                o = (b * 4 + k) * 128
                tr = PE("transpose", h_made[b], *some(tr_free[bank]), out=banks[bank][:, k * 128:(k + 1) * 128],
                        in_=hid[:, o:o + 128], identity=ident)
            hid_free[b] = tr
            tr_free[bank] = h_turned[b] = split_turned(tr, hT_free[b % 2], banks[bank][:, :], hT[b % 2])

        CHUNKS = [("up", b, k) for b in range(HB) for k in range(4)] + [("down", b, k) for b in range(HB)
                                                                         for k in (0, 2)]

        def split_weights(n):
            if n >= FT * len(CHUNKS):
                return
            i, (kind, b, k) = n // len(CHUNKS), CHUNKS[n % len(CHUNKS)]
            src = (up[b][:, k].rearrange("p c h -> p (c h)") if kind == "up" else
                   down[b][:, k:k + 2].rearrange("p k d -> p (k d)"))
            s = n % NW3
            part_high[n] = A("activation", up_in[b] if kind == "up" else dn_in[b], *some(part_free[s]),
                             out=part[s][:, 0], in_=src, func=ACT.Copy)
            part_low[n] = V("tensor_tensor", part_high[n], out=part[s][:, 1], in0=src,
                            in1=part[s][:, 0].bitcast(F32), op=ALU.subtract)
            if (kind, k) == ("up", 3):
                up_read[b] = part_low[n]
                if i + 1 < FT:
                    load_up(i + 1, b)
            if (kind, k) == ("down", 2):
                dn_read[b] = part_low[n]
                if i + 1 < FT:
                    load_down(i + 1, b)

        def in_parts(n, products, *after):
            s = n % NW3
            for ready, a, w in ((part_high[n], 0, 0), (part_low[n], 0, 1), (part_low[n], 1, 0)):
                for bank, st, half, first, final in products:
                    mm = PE("matmul", ready, *after, out=bank[:, :], lhsT=st[:, a],
                            rhs=part[s][:, w, half * 512:(half + 1) * 512], start=first and (a, w) == (0, 0),
                            stop=final and a == 1)
            part_free[s] = mm
            return mm

        def project_up(i, b):
            q = b % 2
            pair = [banks[2 + 2 * q + c] for c in range(2)]
            for k in range(4):
                n = i * len(CHUNKS) + b * 4 + k
                split_weights(n + 2)
                st = xT[i % 2][:, :, k * 128:(k + 1) * 128]
                mm = in_parts(n, [(pair[c], st, c, k == 0, k == 3) for c in range(2)], xt[i], *some(up_free[q]))
            sl = A("activation", mm, *some(sil_free[q]), out=sil[q], in_=pair[0][:, :], func=ACT.Silu)
            xT_free[i % 2] = mm
            return lambda: make_hidden(b, q, pair, mm, sl)

        def make_hidden(b, q, pair, mm, sl):
            sil_free[q] = up_free[q] = h_made[b] = V(
                "tensor_tensor", mm, sl, *some(hid_free[b]), out=hid[:, b * 512:(b + 1) * 512], in0=pair[1][:, :],
                in1=sil[q], op=ALU.mult)

        def project_down(i, b):
            for kk in range(2):
                n = i * len(CHUNKS) + 4 * HB + 2 * b + kk
                split_weights(n + 2)
                mm = in_parts(n, [(banks[7], hT[b % 2][:, :, (2 * kk + h) * 128:(2 * kk + h + 1) * 128], h,
                                   b + kk + h == 0, b == HB - 1 and kk + h == 2) for h in range(2)],
                              h_turned[b], *some(y_read))
            hT_free[b % 2] = mm
            return mm

        e_w = [carve(2048, edge_at + 2048 * i) for i in range(2)]
        d_second = [done(f"w_second{i}") for i in range(2)]

        def load_second(e, *free):
            S.dma(d_second[e % 2], *free, out=e_w[e % 2][:, 0:1024], in_=v1[e])
            return S.dma(d_second[e % 2], *free, out=e_w[e % 2][:, 1024:2048], in_=v2[e])

        d_rec = done("records")
        SCATTERS = 14
        assert FT * SCATTERS >= EJ
        load_rows(0)
        load_rows(1)
        d_late = done("late_weights")
        late = zone_of(lnT_at + 4 * NPAD - LATE, LATE)
        wup_sb, m23_sb, m4_sb, wo_sb = late(2 * MUL), late(256), late(512), late(512)
        for sb, w in ((wup_sb, w_up), (m23_sb, w_mlp23), (m4_sb, w_mlp4), (wo_sb, w_out)):
            ready_late = S.dma(d_late, lnT_read, out=sb, in_=w)
        turn_rows(0)
        split_weights(0)
        split_weights(1)
        for i in range(FT):
            h_made, h_turned = [None] * HB, [None] * HB
            if i > 0 and i + 1 < FT:
                load_rows(i + 1)
            project_up(i, 0)()
            project_up(i, 1)()
            turn_hidden(0)
            project_up(i, 2)()
            turn_hidden(1)
            if i + 1 < FT:
                turn_rows(i + 1)
            project_down(i, 0)
            turn_hidden(2)
            project_down(i, 1)
            mm = project_down(i, 2)
            y_read = A("activation", mm, *some(yo_free[i % 2]), out=yo[i % 2], in_=banks[7][:, :], func=ACT.Copy)
            yo_free[i % 2] = S.dma(d_out[i % 2], y_read, out=ys[i * TILE:(i + 1) * TILE], in_=yo[i % 2])
            scatter_edges(SCATTERS)
        experts_read = [mm, V.last, A.last]
        scattered = (d_scatter.sem, d_scatter.count)
        next_phase()
        recs = phase_tensor("records", NREC * REC).rearrange("p (s c) -> p s c", c=REC)
        act3 = [[phase_tensor(f"hidden{r}{h}", 512, F32R) for h in range(2)] for r in range(2)]
        m4_high, m4_low = phase_tensor("w_mlp4_high", 512, F32R), phase_tensor("w_mlp4_low", 512, F32R)
        yz = zone_of(zone, ZONE)
        yg = [yz(512) for i in range(2 * NT)]
        d_yg = [done(f"pick{i}") for i in range(2 * NT)]
        yg_in = []
        for t in range(NT):
            for kk in range(2):
                i, r = 2 * t + kk, rows(t)
                yg_in.append(G.dma(d_yg[i], *yo_free, *experts_read, out=yg[i][:r], out_offset=None, in_=ys,
                                   in_offset=bass.IndirectOffsetOnAxis(ap=pair_i[kk][:r, t:t + 1], axis=0)))
        recs_in = S.dma(d_rec, scattered, *experts_read, yg_in[-1], out=recs,
                        in_=sorted_edges.rearrange("(p s) c -> p s c", p=128))
        second_in = [load_second(e, scattered) for e in range(2)]

        def combine(t):
            for kk in range(2):
                i, r = 2 * t + kk, rows(t)
                c = V("scalar_tensor_tensor", yg_in[i], weights_known, V.last, out=xs[:r, t], in0=yg[i][:r],
                      scalar=wt[kk][:r, t:t + 1], in1=xs[:r, t], op0=ALU.mult, op1=ALU.add)
            return c

        stage("node")
        normed = []
        for half in (range(0, NT // 2), range(NT // 2, NT)):
            for t in half:
                block_stats(t, combine(t))
            normed += layer_norm(half)
        table = dram("node_table", [N, 4 * MUL])
        d_tab = [done(f"table{i}") for i in range(4)]
        nz = zone_of(zone + ZONE - 3072, 3072)
        nT = [nz(512) for _ in range(2)]
        table_rows = [nz(512) for _ in range(4)]
        copied, sent, nT_free, rows_made = [None] * 2, [None] * 4, [None] * 2, [None] * 2
        def turn_node(t):
            s = t % 2
            for k in range(4):
                piece = (ln[:, t, 0:MUL] if k == 0 else
                         ln[:, t, MUL:].rearrange("p (u m) -> p m u", m=3)[:, k - 1])
                tr = PE("transpose", normed[t], *some(copied[s]), out=banks[s][:, k * 128:(k + 1) * 128], in_=piece,
                        identity=ident)
            copied[s] = A("activation", tr, *some(nT_free[s]), out=nT[s], in_=banks[s][:, :], func=ACT.Copy)

        senders = carve(NTILE, lnT_at + NB * 64).bitcast(I32)
        V("tensor_copy", recs_in, out=senders, in_=recs[:, :NTILE, 0].bitcast(I32))
        rv = recs[:, :NTILE].rearrange("p (g s) c -> p g s c", g=NG)
        rel = V("tensor_tensor", known["groups"], out=rv[:, :, :, 1], in0=rv[:, :, :, 1],
                in1=g_first.unsqueeze(2).to_broadcast([128, NG, GT]), op=ALU.subtract)
        feat = carve(NB * 64, lnT_at).rearrange("p (r k h c) -> p r k h c", r=NB, k=4, h=2)
        for h in range(2):
            packed = V("tensor_copy", out=feat[:, :, :, h],
                       in_=recs.rearrange("p (r k h) c -> p r k h c", r=NB, h=2)[:, :, :, h, 6:14])
        turn_node(0)
        for t in range(NT):
            s, r = t % 2, rows(t)
            if t + 1 < NT:
                turn_node(t + 1)
            for k in range(4):
                mm = PE("matmul", copied[s], ready_late, *some(rows_made[s]), out=banks[2 + s][:, k * 128:(k + 1) * 128],
                        lhsT=nT[s][:, k * 128:(k + 1) * 128],
                        rhs=wup_sb[:, 0:MUL] if k == 0 else wup_sb[:, MUL:2 * MUL], start=True, stop=True)
            nT_free[s] = mm
            q = t % 4
            rows_made[s] = V("tensor_scalar", mm, *some(sent[q]), out=table_rows[q], in0=banks[2 + s][:, :],
                             scalar1=MUL ** -0.5, scalar2=None, op0=ALU.mult)
            sent[q] = S.dma(d_tab[q], rows_made[s], out=table[t * NP:t * NP + r], in_=table_rows[q][:r])
        table_in = list(sent)

        node_done = [V.last, PE.last, A.last]

        stage("edge", chained=False)
        NGAT, NM, NSUM, NTP, NBANK, NHOT = 8, 6, 3, 3, 3, 4
        ring = zone_of(zone, ZONE)
        gat = [ring(512) for _ in range(NGAT)]
        d_gat = [done(f"gather{i}") for i in range(NGAT)]
        hot = [ring(2 * WN).rearrange("p (i n) -> p i n", i=2) for _ in range(NHOT)]
        picks = [ring(4 * WN).rearrange("p (c n) -> p c n", c=4) for _ in range(NM)]
        msg_a = [ring(2 * MUL) for _ in range(NM)]
        msg_b = [carve(4 * MUL, ln_at + 4 * MUL * i) for i in range(NM)]
        dot = [ring(3 * MUL) for _ in range(NM)]
        run_sum = [ring(8 * WN) for _ in range(NSUM)]
        act1, act2, fT, silu3 = ring(512), ring(512), ring(512), [ring(512) for _ in range(2)]
        sums = dram("sums", [NW * 128, 8 * WN])
        d_sum = [done(f"sum{i}") for i in range(NSUM)]
        sum_zero = V("memset", *node_done, ap=run_sum[NSUM - 1], constant=0.0)
        gat_free, gat_in = [None] * NGAT, {}

        def gather(i):
            s = i % NGAT
            gat_in[i] = G.dma(d_gat[s], *node_done, *table_in, *some(gat_free[s]), out=gat[s], out_offset=None,
                              in_=table, in_offset=bass.IndirectOffsetOnAxis(ap=senders[:, i:i + 1], axis=0))

        mlp_bank, mlp_n = (banks[6], banks[7]), [0]
        free = dict(bank6=None, bank7=None, fT=None, act1=None, act2=None)
        free |= {3: None, 4: None}
        act3_free, mlp_out = [None] * 2, {}

        def mlp_products(r, step):
            b = mlp_bank[mlp_n[0] % 2]
            mlp_n[0] += 1
            wait = some(free[b.name])
            if step == 0:
                for k in range(4):
                    mm = PE("transpose", packed, *wait, out=b[:16, k * 128:(k + 1) * 128],
                            in_=feat[:, r, k].rearrange("p h c -> p (h c)"), identity=ident)
            elif step == 1:
                mm = free["fT"] = PE("matmul", mlp_out[0], *wait, out=b[:, :], lhsT=m1_sb[:16], rhs=fT[:16],
                                     start=True, stop=True)
            elif step == 2:
                mm = free["act1"] = PE("matmul", mlp_out[1], *wait, out=b[:, :], lhsT=m23_sb[:, 0:128], rhs=act1,
                                       start=True, stop=True)
            else:
                p = slice(64 * (step - 3), 64 * (step - 2))
                mm = free["act2"] = PE("matmul", mlp_out[2], *wait, out=b[:, :], lhsT=m23_sb[p, 128:256],
                                       rhs=act2[p], start=True, stop=True)
            return r, step, b, mm

        def mlp_function(r, step, b, mm):
            if step == 0:
                c = mlp_out[0] = A("activation", mm, *some(free["fT"]), out=fT[:16], in_=b[:16, :], func=ACT.Copy)
            elif step == 1:
                c = mlp_out[1] = A("activation", mm, *some(free["act1"]), out=act1, in_=b[:, :], func=ACT.Silu,
                                   scale=8 ** -0.5)
            elif step == 2:
                c = mlp_out[2] = A("activation", mm, *some(free["act2"]), out=act2, in_=b[:, :], func=ACT.Silu,
                                   scale=SILU_2MOM / 8)
            else:
                hl = act3[r % 2][step - 3]
                high = A("activation", mm, *some(act3_free[r % 2]), out=hl, in_=b[:, :], func=ACT.Silu,
                         scale=SILU_2MOM / 8)
                full = silu3[step - 3]
                c = A("activation", *some(free[step]), out=full[64:], in_=b[64:, :], func=ACT.Silu,
                      scale=SILU_2MOM / 8)
                free[step] = mlp_out[3, r, step - 3] = V(
                    "tensor_tensor", high, c, out=hl[64:], in0=full[64:], in1=hl[64:].bitcast(F32),
                    op=ALU.subtract)
            free[b.name] = c

        tp_free, tp_in = [None] * NTP, {}
        tp_bank = [banks[3 + i] for i in range(NTP)]

        def weights_of(i):
            batch, k, half = i // BT, (i % BT) // 2, i % 2
            c, hl = slice(k * 128, (k + 1) * 128), act3[batch % 2][half]
            PE.quiet("matmul", mlp_out[3, batch, half], *some(tp_free[i % NTP]), out=tp_bank[i % NTP][:, :],
                     lhsT=hl[:, c], rhs=m4_high, start=True, stop=False)
            tp_in[i] = PE("matmul", out=tp_bank[i % NTP][:, :], lhsT=hl[:64, c], rhs=m4_low[:64],
                          start=False, stop=True)
            if i % BT == BT - 1:
                act3_free[batch % 2] = tp_in[i]

        hot_free, pick_free = [None] * NHOT, [None] * NM
        hot_made, pick_made, msg_made, terms_made = {}, {}, {}, {}

        def hot_of(i):
            q = (i // 2) % NHOT
            hot_made[i // 2] = V("tensor_tensor", *node_done, *some(hot_free[q]), out=hot[q],
                                 in0=K["node"][:, 0:WN].unsqueeze(1).to_broadcast([128, 2, WN]),
                                 in1=recs[:, i:i + 2, 1:2].to_broadcast([128, 2, WN]), op=ALU.is_equal)

        def picks_of(i):
            s, q = i % NM, (i // 2) % NHOT
            for c in range(4):
                pick_made[i] = A("activation", hot_made[i // 2], *some(pick_free[s]), out=picks[s][:, c],
                                 in_=hot[q][:, i % 2], func=ACT.Copy, scale=recs[:, i, 2 + c:3 + c])

        def terms_of(i):
            s, s1 = i % NM, gat[i % NGAT][:, MUL:].rearrange("p (m u) -> p m u", m=3)
            for m in range(3):
                terms_made[i] = A("activation", gat_in[i], *node_done, *some(msg_made.get(i - NM)),
                                  out=dot[s][:, m * MUL:(m + 1) * MUL], in_=s1[:, m], func=ACT.Copy,
                                  scale=recs[:, i, 3 + m:4 + m])

        def messages_of(i):
            s, gs = i % NM, i % NGAT
            tp = tp_bank[i % NTP][:, :].rearrange("p (w u) -> p w u", w=4)
            s1 = gat[gs][:, MUL:].rearrange("p (m u) -> p m u", m=3)
            term = [dot[s][:, m * MUL:(m + 1) * MUL] for m in range(3)]
            two = V("tensor_tensor", terms_made[i], out=term[0], in0=term[0], in1=term[1], op=ALU.add)
            V("tensor_tensor", tp_in[i], *some(pick_free[s]), out=msg_a[s].rearrange("p (w u) -> p w u", w=2), in0=tp[:, 0:2],
              in1=gat[gs][:, 0:MUL].unsqueeze(1).to_broadcast([128, 2, MUL]), op=ALU.mult)
            three = V("tensor_tensor", two, out=term[0], in0=term[0], in1=term[2], op=ALU.add)
            gat_free[gs] = V("tensor_tensor", out=msg_b[s][:, 0:3 * MUL].rearrange("p (m u) -> p m u", m=3),
                             in0=tp[:, 2:3].to_broadcast([128, 3, MUL]), in1=s1, op=ALU.mult)
            msg_made[i] = tp_free[i % NTP] = V("tensor_tensor", three, out=msg_b[s][:, 3 * MUL:], in0=tp[:, 3],
                                               in1=term[0], op=ALU.mult)

        stored_group = {}
        bank_free, sum_free, sum_made = [None] * NBANK, [None] * NSUM, {-1: sum_zero}
        summed = {}

        def sum_up(i):
            s, g, k = i % NM, i // GT, i % GT
            bank, wait = banks[g % NBANK], [msg_made[i], pick_made[i]] + some(bank_free[g % NBANK])

            def add(cols, msg, pick, first=False, last=True):
                n = pick.shape[-1]
                return PE("matmul", *wait, out=bank[:, cols * WN:cols * WN + n], lhsT=msg, rhs=pick,
                          start=first and k == 0, stop=last and k == GT - 1, skip_group_check=True)

            y0 = picks[s][:, 0]
            add(0, msg_a[s][:, 0:MUL], y0, first=True)
            for m in range(3):
                add(1 + m, msg_b[s][:, m * MUL:(m + 1) * MUL], y0)
            add(4, msg_b[s][:, 3 * MUL:], hot[(i // 2) % NHOT][:, i % 2])
            pick_free[s] = summed[g] = add(5, msg_a[s][:, MUL:], picks[s][:, 1:4].rearrange("p c n -> p (c n)"))
            hot_free[(i // 2) % NHOT] = pick_free[s]

        def close_group(g):
            b, q = g % NBANK, g % NSUM
            sum_made[g] = bank_free[b] = V(
                "scalar_tensor_tensor", summed[g], sum_made[g - 1], *some(sum_free[q]), out=run_sum[q],
                in0=run_sum[(g - 1) % NSUM], scalar=g_same[:, g:g + 1], in1=banks[b][:, :], op0=ALU.mult,
                op1=ALU.add)
            sum_free[q] = G.dma(d_sum[q], sum_made[g], out=sums,
                                out_offset=bass.IndirectOffsetOnAxis(ap=g_row[:, g:g + 1].bitcast(I32), axis=0),
                                in_=run_sum[q], in_offset=None, bounds_check=NW * 128 - 1, oob_is_err=False)
            stored_group[g] = sum_free[q]

        m4_made = V("tensor_copy", ready_late, *node_done, out=m4_high, in_=m4_sb)
        m4_made = V("tensor_tensor", m4_made, out=m4_low, in0=m4_sb, in1=m4_high.bitcast(F32), op=ALU.subtract)
        for step in range(5):
            mlp_function(*mlp_products(0, step))
        mlp_function(*mlp_products(1, 0))
        MLP_AFTER = {6: [0], 0: [1], 2: [2], 4: [3, 4]}
        under_way = [mlp_products(1, 1)]
        PE.wait([m4_made, *node_done])
        for i in range(NGAT):
            gather(i)
        hot_of(0)
        weights_of(0)
        weights_of(1)
        for i in range(2):
            picks_of(i)
            terms_of(i)
        closed = 0
        for i in range(0, NTILE + 2, 2):
            if i + 2 < NTILE:
                hot_of(i + 2)
                weights_of(i + 2)
            for j in (i, i + 1):
                if j < NTILE:
                    messages_of(j)
                    if j + NGAT < NTILE:
                        gather(j + NGAT)
                if j - 2 >= 0:
                    sum_up(j - 2)
                if closed < (j - 2) // GT:
                    close_group(closed)
                    closed += 1
            for j in (i + 2, i + 3):
                if j < NTILE:
                    terms_of(j)
            for j in (i + 2, i + 3):
                if j < NTILE:
                    picks_of(j)
            for step in under_way:
                mlp_function(*step)
            if i + 3 < NTILE:
                weights_of(i + 3)
            batch = (i + 4) // BT + 1
            under_way = [mlp_products(batch, step) for step in MLP_AFTER[(i + 2) % BT] if batch < NB]
        close_group(NG - 1)
        edges_made = V.last

        stage("out")
        p4 = A("activation", ready_late, out=wo_sb[:, MUL:2 * MUL], in_=wo_sb[:, MUL:2 * MUL], func=ACT.Copy,
               scale=3 ** -0.5)
        sums_in = [ring(8 * WN) for i in range(6)]
        d_sin = [done(f"sums_in{i}") for i in range(6)]
        sin_free, o_free = [None] * 6, [None] * 2

        def load_sums(w):
            g = NG - NW + w
            return S.dma(d_sin[w % 6], *node_done, *(stored_group[g - k] for k in range(NSUM)),
                         *some(sin_free[w % 6]), out=sums_in[w % 6], in_=sums[w * 128:(w + 1) * 128])

        inn = {w: load_sums(w) for w in range(6)}
        next_phase()
        x_hl = phase_tensor("nodes_hl", 2 * 4 * T1, F32R).rearrange("p (s k n) -> p s k n", s=2, k=4)
        a1_hl = phase_tensor("w_in_hl", 2048, F32R).rearrange("p (s k h) -> p s k h", s=2, k=4)
        a2_hl = phase_tensor("w_out_hl", 2048, F32R).rearrange("p (s k d) -> p s k d", s=2, k=2)
        h_hl = [phase_tensor(f"second_hidden_hl{i}", 1024, F32R).rearrange("p (s n) -> p s n", s=2)
                for i in range(2)]
        a1_free, a2_free, a1_made, a2_made = None, None, {}, {}

        def in_two(src, out, *after):
            high = A("activation", *after, out=out[0], in_=src, func=ACT.Copy)
            return V("tensor_tensor", high, out=out[1], in0=src, in1=out[0].bitcast(F32), op=ALU.subtract)

        def split_in(e):
            w = e_w[e % 2]
            a1_made[e] = in_two(w[:, 0:1024], [a1_hl[:, q].rearrange("p k h -> p (k h)") for q in range(2)],
                                second_in[e], *some(a1_free))

        def split_out(e):
            w = e_w[e % 2]
            a2_made[e] = in_two(w[:, 1024:2048], [a2_hl[:, q].rearrange("p k d -> p (k d)") for q in range(2)],
                                second_in[e], *some(a2_free))
            if e + 2 < E1:
                second_in.append(load_second(e + 2, a2_made[e]))

        A.wait([summed[NG - 1], edges_made])
        V.wait([summed[NG - 1]])
        split_in(0)
        split_out(0)
        out_scale = (SILU_2MOM / 8) / 16 / 10
        for t in range(NT):
            s = t % 2
            bank = banks[4 + s]
            for h in range(2):
                w = 2 * t + h
                q = w % 6
                for k in range(4):
                    for n, blk in enumerate((0, 4) if k == 0 else (4 + k, k)):
                        o = (256 if k else 0) + n * MUL
                        mm = PE("matmul", inn[w], p4, *some(o_free[s]),
                                out=bank[64 * h:64 * h + WN, k * 128:(k + 1) * 128],
                                lhsT=sums_in[q][:, blk * WN:(blk + 1) * WN], rhs=wo_sb[:, o:o + MUL],
                                start=n == 0, stop=n == 1)
                sin_free[q] = mm
                if w + 6 < NW:
                    inn[w + 6] = load_sums(w + 6)
            r = rows(t)
            V("scalar_tensor_tensor", mm, out=xs[:r, t, 0:MUL], in0=bank[:r, 0:MUL], scalar=out_scale,
              in1=xs[:r, t, 0:MUL], op0=ALU.mult, op1=ALU.add)
            xv = xs[:r, t, MUL:].rearrange("p (u m) -> p m u", m=3)
            o_free[s] = V("scalar_tensor_tensor", out=xv, in0=bank[:r, MUL:].rearrange("p (m u) -> p m u", m=3),
                          scalar=out_scale, in1=xv, op0=ALU.mult, op1=ALU.add)
            if t < T5:
                block_stats(t, o_free[s])

        stage("second")
        d_store = done("store")
        S.dma(d_store, o_free[1], out=out[T5 * NP:NP * (NT - 1)].rearrange("(t p) d -> p t d", p=NP),
              in_=xs[:, T5:NT - 1])
        S.dma(d_store, o_free[1], out=out[NP * (NT - 1):], in_=xs[:last, NT - 1])
        normed = layer_norm(range(T5))
        sz = zone_of(zone, ZONE)
        hidT = [sz(512) for i in range(2)]

        turned = [None, None]
        for t in range(T5):
            tr, block = turn_ln(t, normed[t])
            turned[t % 2] = lnT_done = in_two(block, [x_hl[:, q, :, t * NP:(t + 1) * NP] for q in range(2)], tr)
        V("tensor_copy", ready_ew, out=ei_sb, in_=ei_sb.bitcast(I32))
        co = sz(E1 * T5).rearrange("p (e t) -> p e t", e=E1)
        cw = sz(2 * T5).rearrange("p (t k) -> p t k", k=2)
        for e in range(E1):
            V("scalar_tensor_tensor", out=cw, in0=ei_sb.rearrange("p (t k) -> p t k", k=2), scalar=float(e),
              in1=ew_sb.rearrange("p (t k) -> p t k", k=2), op0=ALU.is_equal, op1=ALU.mult)
            coef = V("tensor_reduce", out=co[:, e], in_=cw, op=ALU.add, axis=AX.X)
        h_free, yb_free, hb_free, h_made = [None] * 2, [None] * 4, [None] * 2, [None] * 2
        PASSES = ((0, 0), (0, 1), (1, 0))
        n_y = 0
        for e in range(E1):
            for h in range(2):
                bank = banks[2 + h]
                for k in range(4):
                    for a, b in PASSES:
                        mm = PE("matmul", lnT_done, a1_made[e], *some(hb_free[h]), out=bank[:, :],
                                lhsT=a1_hl[:, a, k, h * 128:(h + 1) * 128], rhs=x_hl[:, b, k],
                                start=k + a + b == 0, stop=k == 3 and a == 1)
                gelu = hb_free[h] = A("activation", mm, *some(h_made[h]), out=hidT[h], in_=bank[:, :], func=ACT.Gelu)
                h_made[h] = in_two(hidT[h], [h_hl[h][:, q] for q in range(2)], gelu, *some(h_free[h]))
            a1_free = mm
            if e + 1 < E1:
                split_in(e + 1)
            for t in range(T5):
                q = n_y % 4
                bank = banks[4 + q]
                for k in range(2):
                    for a, b in PASSES:
                        mm = PE("matmul", h_made[k], a2_made[e], *some(yb_free[q]), out=bank[:, :],
                                lhsT=h_hl[k][:, a, t * NP:(t + 1) * NP], rhs=a2_hl[:, b, k],
                                start=k + a + b == 0, stop=k == 1 and a == 1)
                yb_free[q] = V("scalar_tensor_tensor", mm, coef, out=xs[:, t], in0=bank[:, :],
                               scalar=co[:, e, t:t + 1], in1=xs[:, t], op0=ALU.mult, op1=ALU.add)
                n_y += 1
            h_free, a2_free = [mm, mm], mm
            if e + 1 < E1:
                split_out(e + 1)
        stored = S.dma(d_store, V.last, out=out[0:T5 * NP].rearrange("(t p) d -> p t d", p=NP), in_=xs[:, 0:T5])
        S.wait([stored, (d_pair.sem, d_pair.count), *sum_free, *sent, *yo_free, filled, zeroed, scattered])

        block = ctx.enter_context(nc.Block())
        for lane, where in ((PE, block.tensor), (V, block.vector), (A, block.scalar), (G, block.gpsimd),
                            (S, block.sync)):
            where(lane.run)


def kernel(**inputs):
    import concourse.bacc as bacc
    from concourse.bass_utils import run_bass_kernel_spmd

    a = {k: np.asarray(v) for k, v in inputs.items()}
    above, below, leaf = search_tree()
    src, dst = a["src"], a["dst"]
    leaf32 = leaf.astype(np.int32)
    table = np.stack([leaf32, np.where(leaf32 < 0, np.int32(NE - 1), leaf32), src[leaf], dst[leaf]], 1)

    def feature_rows(w, k):
        return w.reshape(w.shape[0], k, 128, w.shape[-1]).transpose(0, 2, 1, 3)

    w1, w3, w2 = (a[f"L0_ffn_{n}"].transpose(0, 2, 1) for n in ("w1", "w3", "w2"))
    w13 = np.stack([feature_rows(w, 4).reshape(E0, 128, 4, HB, 512) for w in (w1, w3)], 4)
    w13 = w13.transpose(3, 0, 1, 2, 4, 5).reshape(HB * E0 * 128, 4096)
    w2 = w2.reshape(E0, HB, 4, 128, D).transpose(1, 0, 3, 2, 4).reshape(HB * E0 * 128, 2048)

    def twice(w):
        z = np.zeros_like(w)
        return np.block([[w, z], [z, w]])

    g = {k[7:]: v for k, v in a.items() if k.startswith("L1_gnn_")}
    arrays = dict(
        consts=constants(), x=a["x"], anc=src[above], sub=src[below], leaf_table=table, src=src, dst=dst,
        ea4=a["edge_attr_4"], ea8=a["edge_attr_8"],
        gate=a["L0_ffn_gate_w"].T.reshape(4, 128, E0).transpose(1, 0, 2), w13=w13, w2=w2,
        w_up=np.concatenate([g["W_up0"], g["W_up1"]], 1), w_mlp1=twice(g["W_mlp1"]),
        w_mlp23=np.concatenate([twice(g["W_mlp2"]), np.tile(g["W_mlp3"], (2, 2))], 1),
        w_mlp4=np.concatenate([g["W_mlp4"], g["W_mlp4"]], 0),
        w_out=np.concatenate([g["W_out0"][:128], g["W_out0"][128:], g["W_out1"][:128], g["W_out1"][128:]], 1),
        ew=a["L1_ffn_expert_weights"], ei=a["L1_ffn_expert_indices"],
        v1=feature_rows(a["L1_ffn_w1"], 4).reshape(E1, 128, 1024),
        v2=feature_rows(a["L1_ffn_w2"], 2).reshape(E1, 128, 1024))
    nc = bacc.Bacc("TRN2", target_bir_lowering=False, num_devices=1)
    given, args = {}, []
    for name, v in arrays.items():
        v = np.ascontiguousarray(v)
        given[f"in_{name}"] = v
        args.append(nc.dram_tensor(f"in_{name}", v.shape, mybir.dt.from_np(v.dtype), kind="ExternalInput").ap())
    out = nc.dram_tensor("out", (N, D), F32, kind="ExternalOutput").ap()
    program(nc, *args, out)
    return run_bass_kernel_spmd(nc, [given], core_ids=[0]).results[0]["out"]
```
